# Optimizing a Trainium2 kernel written in Bass

```python
import numpy as np
import jax
import jax.numpy as jnp

def _softmax(x, axis=-1):
    return jax.nn.softmax(x, axis=axis)

def _gelu(x):
    return jax.nn.gelu(x, approximate=True)

def _silu(x):
    return jax.nn.silu(x)

def _sigmoid(x):
    return jax.nn.sigmoid(x)

def _layernorm(x, axis=-1, eps=1e-05):
    m = jnp.mean(x, axis=axis, keepdims=True)
    v = jnp.var(x, axis=axis, keepdims=True)
    return (x - m) / jnp.sqrt(v + eps)

def _scatter_add(tgt, idx, src, axis=0):
    return tgt.at[idx].add(src)

def _segment_sum(src, seg, n):
    return jax.ops.segment_sum(src, seg, n)
kernel_name = 'mk_prb_d2_jaxref_r8_964d70'

def setup_inputs(seed: int=0):
    np.random.seed(seed)
    _w = jnp.asarray

    def _L0_attn_setup():
        import jax, jax.numpy as jnp
        import numpy as np
        DIM = 128
        key = jax.random.key(seed)
        kx, kw = jax.random.split(key)
        x = jax.random.normal(kx, (4, 256, DIM), dtype=jnp.float32)
        W_qkv = jax.random.normal(kw, (3 * DIM, DIM), dtype=jnp.float32) * DIM ** (-0.5)
        return {'x': x, 'W_qkv': W_qkv}
    _L0_attn_in = _L0_attn_setup()

    def _L0_ffn_setup():
        import jax, jax.numpy as jnp
        import numpy as np
        from jax import lax
        B, S, D = (4, 256, 128)
        E = 8
        K = 2
        F = 408
        NORM_TOPK = True
        key = jax.random.key(seed)
        ks = jax.random.split(key, 8)
        sd = 0.02
        return {'x': jax.random.normal(ks[0], (B, S, D), jnp.float32), 'gate_w': jax.random.normal(ks[1], (E, D), jnp.float32) * sd, 'gate_b': jnp.zeros((E,), jnp.float32), 'up_w': jax.random.normal(ks[2], (E, F, D), jnp.float32) * sd, 'up_b': jnp.zeros((E, F), jnp.float32), 'gp_w': jax.random.normal(ks[3], (E, F, D), jnp.float32) * sd, 'gp_b': jnp.zeros((E, F), jnp.float32), 'down_w': jax.random.normal(ks[4], (E, D, F), jnp.float32) * sd, 'down_b': jnp.zeros((E, D), jnp.float32)}
    _L0_ffn_in = _L0_ffn_setup()

    def _L1_attn_setup():
        import jax, jax.numpy as jnp
        import numpy as np
        import math
        N_HEAD = 16
        LATENT_RANK = 64
        key = jax.random.key(seed)
        ks = jax.random.split(key, 8)
        B, T, C, H, R = (4, 256, 128, N_HEAD, LATENT_RANK)
        std = 0.02
        return {'hidden_states': jax.random.normal(ks[0], (B, T, C), jnp.float32), 'basis_w': jax.random.normal(ks[1], (R, C), jnp.float32) * std, 'core': jax.random.normal(ks[2], (R, R), jnp.float32) * std, 'head_residual': jax.random.normal(ks[3], (H, R, R), jnp.float32) * (std / 10.0), 'v_w': jax.random.normal(ks[4], (C, C), jnp.float32) * std, 'v_b': jnp.zeros((C,), jnp.float32), 'o_w': jax.random.normal(ks[5], (C, C), jnp.float32) * std, 'o_b': jnp.zeros((C,), jnp.float32)}
    _L1_attn_in = _L1_attn_setup()

    def _L1_ffn_setup():
        import jax, jax.numpy as jnp
        import numpy as np
        E = 8
        TOPK = 2

        def _moe_forward(x, Wg, W1, W2, W3):
            B, S, D = x.shape
            xt = x.reshape(-1, D)
            T = xt.shape[0]
            logits = xt @ Wg.T
            scores = jax.nn.softmax(logits, axis=-1)
            w, idx = jax.lax.top_k(scores, TOPK)
            w = w / (w.sum(axis=-1, keepdims=True) + 1e-20)
            cw = jnp.zeros((T, E), xt.dtype).at[jnp.arange(T)[:, None], idx].add(w)
            h = jax.nn.silu(jnp.einsum('td,ehd->teh', xt, W1)) * jnp.einsum('td,ehd->teh', xt, W3)
            out = jnp.einsum('teh,edh->ted', h, W2)
            y = jnp.einsum('te,ted->td', cw, out)
            return y.reshape(B, S, D)
        key = jax.random.key(seed)
        k0, k1, k2, k3, k4 = jax.random.split(key, 5)
        B, S, D, H = (1, 256, 128, 352)
        scale = 0.02
        x = jax.random.normal(k0, (B, S, D), jnp.float32)
        Wg = jax.random.normal(k1, (E, D), jnp.float32) * scale
        W1 = jax.random.normal(k2, (E, H, D), jnp.float32) * scale
        W2 = jax.random.normal(k3, (E, D, H), jnp.float32) * scale
        W3 = jax.random.normal(k4, (E, H, D), jnp.float32) * scale
        return {'x': x, 'Wg': Wg, 'W1': W1, 'W2': W2, 'W3': W3}
    _L1_ffn_in = _L1_ffn_setup()
    _d = {'L0_attn_x': _L0_attn_in['x'], 'L0_attn_W_qkv': _L0_attn_in['W_qkv'], 'L0_ffn_gate_w': _L0_ffn_in['gate_w'], 'L0_ffn_gate_b': _L0_ffn_in['gate_b'], 'L0_ffn_up_w': _L0_ffn_in['up_w'], 'L0_ffn_up_b': _L0_ffn_in['up_b'], 'L0_ffn_gp_w': _L0_ffn_in['gp_w'], 'L0_ffn_gp_b': _L0_ffn_in['gp_b'], 'L0_ffn_down_w': _L0_ffn_in['down_w'], 'L0_ffn_down_b': _L0_ffn_in['down_b'], 'L1_attn_basis_w': _L1_attn_in['basis_w'], 'L1_attn_core': _L1_attn_in['core'], 'L1_attn_head_residual': _L1_attn_in['head_residual'], 'L1_attn_v_w': _L1_attn_in['v_w'], 'L1_attn_v_b': _L1_attn_in['v_b'], 'L1_attn_o_w': _L1_attn_in['o_w'], 'L1_attn_o_b': _L1_attn_in['o_b'], 'L1_ffn_Wg': _L1_ffn_in['Wg'], 'L1_ffn_W1': _L1_ffn_in['W1'], 'L1_ffn_W2': _L1_ffn_in['W2'], 'L1_ffn_W3': _L1_ffn_in['W3']}
    _x0 = _d['L0_attn_x']
    _d['L0_attn_x'] = jax.random.normal(jax.random.fold_in(jax.random.key(seed), 1), (4, 1024, 128), dtype=_x0.dtype)
    del _x0
    return _d

def reference(L0_attn_x, L0_attn_W_qkv, L0_ffn_gate_w, L0_ffn_gate_b, L0_ffn_up_w, L0_ffn_up_b, L0_ffn_gp_w, L0_ffn_gp_b, L0_ffn_down_w, L0_ffn_down_b, L1_attn_basis_w, L1_attn_core, L1_attn_head_residual, L1_attn_v_w, L1_attn_v_b, L1_attn_o_w, L1_attn_o_b, L1_ffn_Wg, L1_ffn_W1, L1_ffn_W2, L1_ffn_W3):

    def _L0_attn_ref(x, W_qkv):
        import jax, jax.numpy as jnp
        import numpy as np
        DIM = 128
        qkv = jnp.einsum('bnd,ed->bne', x, W_qkv)
        B, N, _ = qkv.shape
        qkv = qkv.reshape(B, N, 3, DIM).transpose(2, 0, 1, 3)
        q, k, v = (qkv[0], qkv[1], qkv[2])
        scale = DIM ** (-0.5)
        attn = jnp.einsum('bnd,bmd->bnm', q * scale, k)
        attn = jax.nn.softmax(attn, axis=-1)
        out = jnp.einsum('bnm,bmd->bnd', attn, v)
        return out

    def _L0_ffn_ref(x, gate_w, gate_b, up_w, up_b, gp_w, gp_b, down_w, down_b):
        import jax, jax.numpy as jnp
        import numpy as np
        from jax import lax
        B, S, D = (4, 256, 128)
        E = 8
        K = 2
        F = 408
        NORM_TOPK = True
        bs, slen, dim = x.shape
        xf = x.reshape(-1, dim)
        N = xf.shape[0]
        scores = jax.nn.softmax(xf @ gate_w.T + gate_b, axis=-1)
        top_w, top_idx = lax.top_k(scores, K)
        if NORM_TOPK:
            top_w = top_w / (top_w.sum(-1, keepdims=True) + 1e-20)
        comb = jnp.zeros((N, E), xf.dtype).at[jnp.arange(N)[:, None], top_idx].add(top_w)

        def step(acc, p):
            uw, ub, gw, gb, dw, db, w = p
            h = jax.nn.silu((xf @ gw.T + gb) * (xf @ uw.T + ub))
            return (acc + w[:, None] * (h @ dw.T + db), None)
        y0 = jnp.zeros_like(xf)
        y, _ = lax.scan(step, y0, (up_w, up_b, gp_w, gp_b, down_w, down_b, comb.T))
        return y.reshape(bs, slen, dim)

    def _L1_attn_ref(hidden_states, basis_w, core, head_residual, v_w, v_b, o_w, o_b):
        import jax, jax.numpy as jnp
        import numpy as np
        import math
        N_HEAD = 16
        LATENT_RANK = 64
        B, T, C = hidden_states.shape
        H = N_HEAD
        R = LATENT_RANK
        head_dim = C // H
        latent = jnp.einsum('btc,rc->btr', hidden_states, basis_w)
        core_sym = 0.5 * (core + core.T)
        centered = head_residual - head_residual.mean(axis=0, keepdims=True)
        head_mats = core_sym[None] / float(H) + centered
        lt = jnp.einsum('btr,hrs->bhts', latent, head_mats)
        att = jnp.einsum('bhts,bus->bhtu', lt, latent) * (1.0 / math.sqrt(R))
        causal = jnp.tril(jnp.ones((T, T), jnp.bool_))
        att = jnp.where(causal[None, None], att, jnp.float32(-jnp.inf))
        att = jax.nn.softmax(att, axis=-1)
        v = (hidden_states @ v_w.T + v_b).reshape(B, T, H, head_dim).transpose(0, 2, 1, 3)
        y = att @ v
        y = y.transpose(0, 2, 1, 3).reshape(B, T, C)
        y = y @ o_w.T + o_b
        return y

    def _L1_ffn_ref(x, Wg, W1, W2, W3):
        import jax, jax.numpy as jnp
        import numpy as np
        E = 8
        TOPK = 2

        def _moe_forward(x, Wg, W1, W2, W3):
            B, S, D = x.shape
            xt = x.reshape(-1, D)
            T = xt.shape[0]
            logits = xt @ Wg.T
            scores = jax.nn.softmax(logits, axis=-1)
            w, idx = jax.lax.top_k(scores, TOPK)
            w = w / (w.sum(axis=-1, keepdims=True) + 1e-20)
            cw = jnp.zeros((T, E), xt.dtype).at[jnp.arange(T)[:, None], idx].add(w)
            h = jax.nn.silu(jnp.einsum('td,ehd->teh', xt, W1)) * jnp.einsum('td,ehd->teh', xt, W3)
            out = jnp.einsum('teh,edh->ted', h, W2)
            y = jnp.einsum('te,ted->td', cw, out)
            return y.reshape(B, S, D)
        return _moe_forward(x, Wg, W1, W2, W3)
    x = L0_attn_x
    xn = _layernorm(x, axis=-1)
    x = x + _L0_attn_ref(xn, L0_attn_W_qkv) + _L0_ffn_ref(xn, L0_ffn_gate_w, L0_ffn_gate_b, L0_ffn_up_w, L0_ffn_up_b, L0_ffn_gp_w, L0_ffn_gp_b, L0_ffn_down_w, L0_ffn_down_b)
    xn = _layernorm(x, axis=-1)
    x = x + _L1_attn_ref(xn, L1_attn_basis_w, L1_attn_core, L1_attn_head_residual, L1_attn_v_w, L1_attn_v_b, L1_attn_o_w, L1_attn_o_b) + _L1_ffn_ref(xn, L1_ffn_Wg, L1_ffn_W1, L1_ffn_W2, L1_ffn_W3)
    return x

_drawn_inputs = setup_inputs


def setup_inputs(seed=0):
    import zlib

    import numpy as np

    out = dict(_drawn_inputs(seed))
    spreads = {'L0_ffn_gate_b': (0.0, 0.1),
     'L0_ffn_up_b': (0.0, 0.8),
     'L0_ffn_gp_b': (0.0, 0.8),
     'L0_ffn_down_b': (0.0, 0.1),
     'L1_attn_v_b': (0.0, 2.0),
     'L1_attn_o_b': (0.0, 0.534)}
    factors = {'L0_ffn_up_w': 7.19,
     'L0_ffn_gp_w': 7.234,
     'L0_ffn_down_w': 6.58,
     'L1_attn_basis_w': 64.0,
     'L1_attn_core': 64.0,
     'L1_attn_head_residual': 64.0,
     'L1_attn_v_w': 28.994,
     'L1_ffn_Wg': 8.0,
     'L1_ffn_W1': 8.0,
     'L1_ffn_W2': 8.0,
     'L1_ffn_W3': 8.0}
    for name, (base, spread) in spreads.items():
        noise = np.random.default_rng([zlib.crc32(name.encode()), seed]).standard_normal(out[name].shape)
        drawn = base * np.exp(spread * noise) if base else spread * noise
        out[name] = jnp.asarray(drawn.astype(out[name].dtype))
    for name, factor in factors.items():
        out[name] = (out[name] * factor).astype(out[name].dtype)
    return out
```

```python
from contextlib import ExitStack

import numpy as np

import concourse.bass as bass
from concourse import mybir

F32 = mybir.dt.float32
F16 = mybir.dt.float16
BF16 = mybir.dt.bfloat16
I32 = mybir.dt.int32
U32 = mybir.dt.uint32
ALU = mybir.AluOpType
ACT = mybir.ActivationFunctionType
AX = mybir.AxisListType

P = 128
D = 128
BATCH, SEQ = 4, 1024
NT = BATCH * SEQ // P
TB = SEQ // P
NE = 8
F0, F1 = 408, 352
CH0 = [102] * 4
CH1 = [128, 128, 96]
NTILE = 72
NSLOT = NTILE * P
HEADS, RANK, HD = 16, 64, 8
OUT_USES = 2
HG = 4
NG = BATCH * HEADS // HG
DMA_RING = 4096
EPS = 1e-5
BIG = 1e30
SHIFT = 16.0


def known_below(i, bound):
    return isinstance(i, int) and i < bound


def known(i, value):
    return isinstance(i, int) and i == value


def turn_of(j):
    return j // 2 if isinstance(j, int) else j >> 1


def sequence_of(n):
    return n // TB if isinstance(n, int) else (n >> (TB.bit_length() - 1)).with_bounds(min_val=0, max_val=BATCH - 1)


def tile_loop(eng, start, end, body, peel=2, tail=2):
    for i in range(start, start + peel):
        body(i, i % 2)
    with eng.Fori((start + peel) // 2, (end - tail) // 2) as pair:
        body(2 * pair, 0)
        body(2 * pair + 1, 1)
    for i in range(end - tail, end):
        body(i, i % 2)


def two_layers(nc, a, out):
    with ExitStack() as ctx:
        def sb(name, shape, dt=F32):
            return ctx.enter_context(nc.sbuf_tensor(name, shape, dt))

        def dram(name, shape, dt=F32):
            return nc.dram_tensor(name, shape, dt).ap()

        def sem(name):
            return ctx.enter_context(nc.semaphore(name))

        PS = ctx.enter_context(nc.psum_tensor("PS", [P, 8, 512], F32))

        slots_in = [dram("slots_in0", [NSLOT, D]), dram("slots_in1", [NSLOT, D])]
        slots_out = [dram("slots_out0", [NSLOT, D]), dram("slots_out1", [NSLOT, D])]

        X = sb("X", [P, NT, D])
        XN = sb("XN", [P, NT, D])
        ident = sb("ident", [P, P])
        before = sb("before", [P, P])
        ones = sb("ones", [P, P])
        mean_var = sb("mean_var", [P, NT, 2])
        std = sb("std", [P, NT])
        rstd = sb("rstd", [P, NT])
        xn_fixed = sb("xn_fixed", [P, 2, D])
        xnT = sb("xnT", [P, 2, P])
        iota_e = sb("iota_e", [P, NE])
        steps128 = sb("steps128", [P, NT])
        tile_no = sb("tile_no", [P, NTILE])
        r_tile = sb("r_tile", [P, NTILE])
        r_small = [sb("r_small%d" % i, [P, NT]) for i in range(6)]
        r_e = [sb("r_e%d" % i, [P, NE]) for i in range(4)]
        w_top = [[sb("w_top%d_%d" % (l, c), [P, NT]) for c in range(2)] for l in range(2)]
        slot = [[sb("slot%d_%d" % (l, c), [P, NT], I32) for c in range(2)] for l in range(2)]
        expert_of = [sb("expert_of%d" % l, [P, NTILE], I32) for l in range(2)]
        w_in = sb("w_in", [P, NE, 2 * F0])
        w_dn = sb("w_dn", [P, NE, 4, D])
        xe = sb("xe", [P, 2, D])
        xeT = sb("xeT", [P, 2, P])
        ye = sb("ye", [P, 2, D])
        gat = sb("gat", [P, 4, D])
        ARENA = 30400
        arena = sb("arena", [P, ARENA])
        at = [0]

        def carve(cols, dt=F32):
            view = arena[:, at[0]:at[0] + cols]
            at[0] += cols
            assert at[0] <= ARENA, at[0]
            return view if dt == F32 else view.bitcast(dt)

        kT = carve(NT * P).rearrange("p (n t) -> p n t", t=P)
        qT = carve(NT * P).rearrange("p (n t) -> p n t", t=P)
        v_lg = carve(NT * (D + NE)).rearrange("p (n c) -> p n c", c=D + NE)
        work = at[0]
        prob = carve(2 * SEQ).rearrange("p (k c) -> p k c", k=2)
        probT = carve(2 * SEQ).rearrange("p (k c) -> p k c", k=2)
        at[0] = 12800
        RT = [carve(NT * NE).rearrange("p (n e) -> p n e", e=NE) for _ in range(6)]
        stats = RT[0].rearrange("p n e -> p (n e)")[:, 0:NT * 6].rearrange("p (n c) -> p n c", c=6)
        r_map = carve(NTILE * NE).rearrange("p (j e) -> p j e", e=NE)
        at[0] = work
        both = carve(2 * F0).rearrange("p (c f) -> p c f", c=2)
        pre = carve(2 * F0).rearrange("p (k f) -> p k f", k=2)
        hid = carve(2 * F0).rearrange("p (k f) -> p k f", k=2)
        hidT = carve(2 * 4 * P).rearrange("p (k c t) -> p k c t", k=2, c=4)
        at[0] = work + 4 * SEQ
        b_in = carve(NE * 2 * F0).rearrange("p (e f) -> p e f", e=NE)
        b_dn = carve(NE * D).rearrange("p (e d) -> p e d", e=NE)
        at[0] = 0
        lat = carve(BATCH * SEQ)
        lat_hi = carve(BATCH * SEQ // 2, F16)
        lat_lo = carve(BATCH * SEQ // 2, F16)
        v9 = carve(NT * HEADS * (HD + 1)).rearrange("p (n h c) -> p n h c", h=HEADS, c=HD + 1)
        lt_hl = carve(2 * HG * SEQ // 2, F16).rearrange("p (k h t) -> p k h t", k=2, h=HG)
        lt_hm = carve(2 * HG * SEQ // 2, F16).rearrange("p (k h t) -> p k h t", k=2, h=HG)
        prob1 = [carve(HG * w).rearrange("p (h t) -> p h t", h=HG) for w in (SEQ, SEQ - P)]
        V_COLS = TB * HG * (HD + 1)
        v_rows = carve(2 * (V_COLS + 32)).rearrange("p (k c) -> p k c", k=2)
        v_fixed = [v_rows[:, k, 0:V_COLS].rearrange("p (j h c) -> p j h c", j=TB, h=HG) for k in range(2)]
        oT = carve(SEQ)
        y1 = XN

        wq = sb("wq", [P, 3 * D + NE])
        gb = sb("gb", [P, NE])
        heads_fixed = sb("heads_fixed", [P, 2, HG * RANK])
        q_fixed = heads_fixed[:, 0, :].rearrange("p (k t) -> p k t", k=2)
        core = heads_fixed[0:RANK, 1, 0:2 * RANK].rearrange("p (c s) -> p c s", c=2)
        head_mean = heads_fixed[0:RANK, 1, 2 * RANK:3 * RANK]
        nmax = sb("nmax", [P, 2])
        den = sb("den", [P, 2])
        rden = sb("rden", [P, 2])

        wv1 = sb("wv1", [P, D + NE])
        basis = sb("basis", [P, P])
        vb = sb("vb", [P, D])
        ob = sb("ob", [P, D])
        ow = sb("ow", [P, D])
        lg1 = sb("lg1", [P, NT, NE])
        heads = sb("heads", [P, HEADS, RANK])
        late = sb("late", [P, 512], BF16)
        late16 = sb("late16", [P, P], BF16)
        ident16 = sb("ident16", [P, P], BF16)
        identh = sb("identh", [P, P], F16)
        junk = gat[:].rearrange("p a b -> p (a b)").bitcast(BF16).rearrange("p (k c) -> p k c", k=2)
        maxima1 = sb("maxima1", [P, 2, HG, 12])
        shift = sb("shift", [P, 2, 2, HG, TB], F16)
        shiftT = sb("shiftT", [2 * HG * TB, 2, P], F16)
        rden1 = sb("rden1", [P, OUT_USES, 4, HG])
        y_fixed = xn_fixed
        yT = xnT
        o_tmp = ye

        block_sems = {}

        def S(name):
            if name not in block_sems:
                block_sems[name] = sem(name)
            return block_sems[name]

        loaded_x = S("loaded_x")
        loaded_w0 = S("loaded_w0")
        loaded_w1 = S("loaded_w1")
        W1_LOADS = 11
        loaded_moe = [S("loaded_moe0"), S("loaded_moe1")]
        zeroed = S("zeroed")
        names = ("stats mv var sd rstd xs_ready xn_ready xn_t xt_ready proj ev_act ev_dve route route_act "
                 "route_pe routed scattered xe_t xeT_ready up_done pre_ready hid_ready hid_t "
                 "hidT_ready dn_done ye_ready gat_used half_sum both_ready").split()
        L = [{n: S(n + str(l)) for n in names} for l in range(2)]
        for l in range(2):
            for n in ("xe_loaded", "ye_stored", "gathered"):
                L[l][n] = [S(n + "%d_%d" % (l, k)) for k in range(2)]
        q_ready, s_done, max_done, exp_done, p_t, pT_dve, pT_act, pv_done, rden_done, x_att0 = (
            S(n) for n in "q_ready s_done max_done exp_done p_t pT_dve pT_act pv_done rden_done x_att0".split())



        def moe_sp(sp, l):
            s = L[l]
            sp.wait_ge(s["scattered"], 16 * 2 * NT)

            def load(j, k):
                if not known_below(j, 2):
                    sp.wait_ge(s["xe_t"], j - 1)
                sp.dma_start(xe[:, k, :], slots_in[l][bass.ds(j * P, P), :]).then_inc(s["xe_loaded"][k], 16)

            def store(j, k):
                sp.wait_ge(s["ye_ready"], j + 1)
                sp.dma_start(slots_out[l][bass.ds(j * P, P), :], ye[:, k, :]).then_inc(s["ye_stored"][k], 16)

            def step(j, k):
                if not (isinstance(j, int) and j >= NTILE - 2):
                    load(j + 2, k)
                if not known_below(j, 2):
                    store(j - 2, k)
            load(0, 0)
            load(1, 1)
            tile_loop(sp, 0, NTILE, step)
            store(NTILE - 2, 0)
            store(NTILE - 1, 1)

        def route_pool(pool, l):
            s = L[l]
            pool.wait_ge(s["routed"], 1)
            pool.wait_ge(s["xn_ready"], NT)
            for n in range(NT):
                for c in range(2):
                    pool.indirect_dma_start(
                        out=slots_in[l], out_offset=bass.IndirectOffsetOnAxis(ap=slot[l][c][:, n:n + 1], axis=0),
                        in_=XN[:, n, :], in_offset=None).then_inc(s["scattered"], 16)
            for k in range(2):
                pool.wait_ge(s["ye_stored"][k], 16 * (NTILE // 2))
            for n in range(NT):
                if n >= 2:
                    pool.wait_ge(s["gat_used"], n - 1)
                for c in range(2):
                    pool.indirect_dma_start(
                        out=gat[:, 2 * (n % 2) + c, :], out_offset=None, in_=slots_out[l],
                        in_offset=bass.IndirectOffsetOnAxis(ap=slot[l][c][:, n:n + 1], axis=0),
                    ).then_inc(s["gathered"][n % 2], 16)

        def proj_pe(pe, l):
            s = L[l]

            def transpose(n, k):
                pe.wait_ge(s["xs_ready"], n + 1)
                if not known_below(n, 2):
                    pe.wait_ge(s["xt_ready"], n - 1)
                pe.transpose(PS[:, k, 0:P], xn_fixed[:, k, :], ident[:]).then_inc(s["xn_t"], 1)

            def project(n, k):
                pe.wait_ge(s["xt_ready"], n + 1)
                if not known_below(n, 2):
                    pe.wait_ge(s["ev_act"], n - 1)
                    pe.wait_ge(s["ev_dve"], n - 1)
                bank = PS[:, 2 + k, :]
                if l == 0:
                    pe.matmul(bank[:, 0:P], wq[:, D:2 * D], xnT[:, k, :], start=True, stop=True)
                    pe.matmul(bank[:, P:2 * P], wq[:, 0:D], xnT[:, k, :], start=True, stop=True)
                else:
                    pe.matmul(bank[:, 0:P], basis[:], xnT[:, k, :], start=True, stop=True)
                rows = wq[:, 2 * D:3 * D + NE] if l == 0 else wv1[:]
                pe.matmul(PS[:, 4 + k, 0:D + NE], xnT[:, k, :], rows,
                          start=True, stop=True).then_inc(s["proj"], 1)

            def step(n, k):
                if not (isinstance(n, int) and n == NT - 1):
                    transpose(n + 1, 1 - k)
                project(n, k)
            transpose(0, 0)
            tile_loop(pe, 0, NT, step)

        def route_pe(pe, l):
            s = L[l]
            pe.wait_ge(s["route_pe"], 1)
            chosen = RT[4][:].rearrange("p n e -> p (n e)")
            pe.matmul(PS[:, 4, 0:NT * NE], before[:], chosen, start=True, stop=True)
            pe.matmul(PS[:, 5, 0:NT * NE], ones[:], chosen, start=True, stop=True).then_inc(s["route_pe"], 1)

        def attention0_pe(pe, first, end):
            if first == 0:
                pe.wait_ge(L[0]["ev_act"], NT)
                pe.wait_ge(L[0]["ev_dve"], NT)
                pe.wait_ge(L[0]["routed"], 1)
            else:
                pe.wait_ge(L[0]["ye_ready"], NTILE)

            def scores(n, k):
                pe.wait_ge(q_ready, n + 1)
                if not known_below(n, 2):
                    pe.wait_ge(exp_done, n - 1)
                b = sequence_of(n)
                for c in range(2):
                    mm = pe.matmul(PS[:, 2 * k + c, :], q_fixed[:, k, :], kT[:, bass.ds(b * TB + 4 * c, 4), :],
                                   start=True, stop=True)
                mm.then_inc(s_done, 1)

            def turn(n, k):
                pe.wait_ge(exp_done, n + 1)
                if not known_below(n, 1):
                    pe.wait_ge(pT_dve, n)
                    pe.wait_ge(pT_act, n)
                for c in range(TB):
                    mm = pe.transpose(PS[:, 4 + c // 4, (c % 4) * P:(c % 4 + 1) * P],
                                      prob[:, k, c * P:(c + 1) * P], ident[:])
                    if c % 4 == 3:
                        mm.then_inc(p_t, 1)

            def values(n, k):
                pe.wait_ge(pT_dve, n + 1)
                pe.wait_ge(pT_act, n + 1)
                if not known_below(n, 2):
                    pe.wait_ge(x_att0, n - 1)
                b = sequence_of(n)
                for c in range(TB):
                    mm = pe.matmul(PS[:, 6 + k, 0:D], probT[:, k, c * P:(c + 1) * P],
                                   v_lg[:, bass.ds(b * TB + c, 1), 0:D], start=(c == 0), stop=(c == TB - 1))
                mm.then_inc(pv_done, 1)

            def step(n, k):
                if not known(n, end - 1):
                    scores(n + 1, 1 - k)
                turn(n, k)
                if not known(n, first):
                    values(n - 1, 1 - k)
            scores(first, 0)
            tile_loop(pe, first, end, step)
            values(end - 1, 1)

        def moe_pe(pe, l):
            s = L[l]
            FW, chunks = (F0, CH0) if l == 0 else (F1, CH1)
            pe.wait_ge(loaded_moe[l], 16 * 4)
            pe.wait_ge(s["routed"], 1)
            pe.wait_ge(x_att0, NT // 2) if l == 0 else pe.wait_ge(x_att1, NT)

            def turn_in(j, k):
                pe.wait_ge(s["xe_loaded"][k], 16 * (turn_of(j) + 1))
                if not known_below(j, 1):
                    pe.wait_ge(s["xeT_ready"], j)
                pe.transpose(PS[:, 4, 0:P], xe[:, k, :], ident[:]).then_inc(s["xe_t"], 1)

            def up(j, k):
                pe.wait_ge(s["xeT_ready"], j + 1)
                if not known_below(j, 2):
                    pe.wait_ge(s["pre_ready"], j - 1)
                    if l == 1:
                        pe.wait_ge(s["hid_ready"], j - 1)
                e = pe.value_load(expert_of[l][0:1, bass.ds(j, 1)], min_val=0, max_val=NE - 1)
                for c in range(2):
                    mm = pe.matmul(PS[:, 2 * k + c, 0:FW], xeT[:, k, :], w_in[:, bass.ds(e, 1), c * FW:(c + 1) * FW],
                                   start=True, stop=True)
                mm.then_inc(s["up_done"], 1)

            def turn_hidden(j, k):
                pe.wait_ge(s["hid_ready"], j + 1)
                if not known_below(j, 1):
                    pe.wait_ge(s["hidT_ready"], j)
                f = 0
                for c, m in enumerate(chunks):
                    mm = pe.transpose(PS[0:m, 5, c * P:(c + 1) * P], hid[:, k, f:f + m], ident[:])
                    f += m
                mm.then_inc(s["hid_t"], 1)

            def down(j, k):
                pe.wait_ge(s["hidT_ready"], j + 1)
                if not known_below(j, 2):
                    pe.wait_ge(s["ye_ready"], j - 1)
                e = pe.value_load(expert_of[l][0:1, bass.ds(j, 1)], min_val=0, max_val=NE - 1)
                for c, m in enumerate(chunks):
                    mm = pe.matmul(PS[:, 6 + k, 0:D], hidT[0:m, k, c, :], w_dn[0:m, bass.ds(e, 1), c, :],
                                   start=(c == 0), stop=(c == len(chunks) - 1))
                mm.then_inc(s["dn_done"], 1)

            def step(j, k):
                last = isinstance(j, int) and j >= NTILE - 2
                if not (last and j == NTILE - 1):
                    up(j + 1, 1 - k)
                if not last:
                    turn_in(j + 2, k)
                turn_hidden(j, k)
                if not known_below(j, 1):
                    down(j - 1, 1 - k)
            turn_in(0, 0)
            up(0, 0)
            turn_in(1, 1)
            tile_loop(pe, 0, NTILE, step)
            down(NTILE - 1, 1)

        def norm_act(act, l):
            s = L[l]
            act.wait_ge(s["var"], 1)
            act.activation(std[:], std[:], ACT.Sqrt).then_inc(s["sd"], 1)

        def proj_act(act, l):
            s = L[l]

            def copy_xnT(n, k):
                act.wait_ge(s["xn_t"], n + 1)
                if not known_below(n, 2):
                    act.wait_ge(s["proj"], n - 1)
                act.activation(xnT[:, k, :], PS[:, k, 0:P], ACT.Copy).then_inc(s["xt_ready"], 1)

            def copy_kq(n, k):
                act.wait_ge(s["proj"], n + 1)
                if l == 1:
                    act.activation(lat[:, bass.ds(n * P, P)], PS[:, 2 + k, 0:P], ACT.Copy)
                    act.activation(lat_hi[:, bass.ds(n * P, P)], PS[:, 2 + k, 0:P], ACT.Copy).then_inc(s["ev_act"], 1)
                    return
                act.activation(kT[:, bass.ds(n, 1), :], PS[:, 2 + k, 0:P], ACT.Copy)
                act.activation(qT[:, bass.ds(n, 1), :], PS[:, 2 + k, P:2 * P], ACT.Copy,
                               scale=float(D) ** -0.5).then_inc(s["ev_act"], 1)

            def step(n, k):
                if not (isinstance(n, int) and n == NT - 1):
                    copy_xnT(n + 1, 1 - k)
                copy_kq(n, k)
            copy_xnT(0, 0)
            tile_loop(act, 0, NT, step)

        def route_act(act, l):
            s = L[l]
            act.wait_ge(s["route_act"], 1)
            act.activation(RT[1][:], RT[0][:], ACT.Exp).then_inc(s["route_act"], 1)
            act.wait_ge(s["route_act"], 3)
            act.activation(r_small[3][:], r_small[2][:], ACT.Exp).then_inc(s["route_act"], 1)

        def attention0_act(act, first, end):
            if first == 0:
                act.wait_ge(L[0]["ev_act"], NT)

            def copy_q(n, k):
                if not known_below(n, 2):
                    act.wait_ge(s_done, n - 1)
                act.activation(q_fixed[:, k, :], qT[:, bass.ds(n, 1), :], ACT.Copy).then_inc(q_ready, 1)

            def exps(n, k):
                act.wait_ge(max_done, n + 1)
                if not known_below(n, 2):
                    act.wait_ge(p_t, 2 * (n - 1))
                    act.wait_ge(rden_done, n - 1)
                act.activation(prob[:, k, :], PS[:, 2 * k:2 * k + 2, :].rearrange("p a b -> p (a b)"), ACT.Exp,
                               bias=nmax[:, k:k + 1], accum_out=den[:, k:k + 1]).then_inc(exp_done, 1)

            def copy_pT(n, k):
                act.wait_ge(p_t, 2 * n + 2)
                if not known_below(n, 2):
                    act.wait_ge(pv_done, n - 1)
                act.activation(probT[:, k, 512:1024], PS[:, 5, :], ACT.Copy).then_inc(pT_act, 1)

            def step(n, k):
                if not (known(n, end - 2) or known(n, end - 1)):
                    copy_q(n + 2, k)
                if not known(n, end - 1):
                    exps(n + 1, 1 - k)
                copy_pT(n, k)
            copy_q(first, 0)
            copy_q(first + 1, 1)
            exps(first, 0)
            tile_loop(act, first, end, step)

        def moe_act(act, l):
            s = L[l]
            FW, chunks = (F0, CH0) if l == 0 else (F1, CH1)

            def copy_xeT(j, k):
                act.wait_ge(s["xe_t"], j + 1)
                if not known_below(j, 2):
                    act.wait_ge(s["up_done"], j - 1)
                act.activation(xeT[:, k, :], PS[:, 4, 0:P], ACT.Copy).then_inc(s["xeT_ready"], 1)

            def silu(j, k):
                if l == 1:
                    act.wait_ge(s["up_done"], j + 1)
                    if not known_below(j, 2):
                        act.wait_ge(s["hid_ready"], j - 1)
                    act.activation(pre[:, k, 0:FW], PS[:, 2 * k, 0:FW], ACT.Silu).then_inc(s["pre_ready"], 1)
                    return
                act.wait_ge(s["pre_ready"], j + 1)
                if not known_below(j, 2):
                    act.wait_ge(s["hid_t"], j - 1)
                act.activation(hid[:, k, 0:FW], pre[:, k, 0:FW], ACT.Silu).then_inc(s["hid_ready"], 1)

            def copy_hidT(j, k):
                act.wait_ge(s["hid_t"], j + 1)
                if not known_below(j, 2):
                    act.wait_ge(s["dn_done"], j - 1)
                if l == 0:
                    act.activation(hidT[0:102, k, :, :].rearrange("p a b -> p (a b)"), PS[0:102, 5, :],
                                   ACT.Copy).then_inc(s["hidT_ready"], 1)
                else:
                    act.activation(hidT[0:96, k, 2, :], PS[0:96, 5, 2 * P:3 * P], ACT.Copy)
                    act.activation(hidT[:, k, 0:2, :].rearrange("p a b -> p (a b)"), PS[:, 5, 0:2 * P],
                                   ACT.Copy).then_inc(s["hidT_ready"], 1)

            def step(j, k):
                last = isinstance(j, int) and j >= NTILE - 2
                if not last:
                    copy_xeT(j + 2, k)
                copy_hidT(j, k)
                if not (last and j == NTILE - 1):
                    silu(j + 1, 1 - k)
            copy_xeT(0, 0)
            copy_xeT(1, 1)
            silu(0, 0)
            tile_loop(act, 0, NTILE, step)

        def norm_dve(dve, l):
            s = L[l]
            for n in range(NT):
                ins = dve.bn_stats(stats[:, n, :], X[:, n, :])
            ins.then_inc(s["stats"], 1)
            dve.wait_ge(s["stats"], 1)
            for n in range(NT):
                ins = dve.bn_aggr(mean_var[:, n, :], stats[:, n, :])
            ins.then_inc(s["mv"], 1)
            dve.wait_ge(s["mv"], 1)
            dve.tensor_scalar(std[:], mean_var[:, :, 1], EPS, None, ALU.add).then_inc(s["var"], 1)
            dve.wait_ge(s["sd"], 1)
            dve.reciprocal(rstd[:], std[:]).then_inc(s["rstd"], 1)
            dve.wait_ge(s["rstd"], 1)

        def proj_dve(dve, l):
            s = L[l]

            def normalise(n, k):
                if not known_below(n, 2):
                    dve.wait_ge(s["xn_t"], n - 1)
                for dst, done in ((xn_fixed[:, k, :], "xs_ready"), (XN[:, bass.ds(n, 1), :], "xn_ready")):
                    dve.tensor_scalar(dst, X[:, bass.ds(n, 1), :], mean_var[:, bass.ds(n, 1), 0],
                                      rstd[:, bass.ds(n, 1)], ALU.subtract, ALU.mult).then_inc(s[done], 1)

            def copy_v(n, k):
                dve.wait_ge(s["proj"], n + 1)
                if l == 1:
                    dve.tensor_tensor(v9[:, bass.ds(n, 1), :, 0:HD],
                                      PS[:, 4 + k, 0:D].rearrange("p (o h c) -> p o h c", o=1, h=HEADS),
                                      vb[:].rearrange("p (o h c) -> p o h c", o=1, h=HEADS), ALU.add)
                    dve.tensor_copy(lg1[:, bass.ds(n, 1), :], PS[:, 4 + k, D:D + NE].unsqueeze(1))
                    dve.wait_ge(s["ev_act"], n + 1)
                    dve.tensor_tensor(lat_lo[0:RANK, bass.ds(n * P, P)], PS[0:RANK, 2 + k, 0:P],
                                      lat_hi[0:RANK, bass.ds(n * P, P)], ALU.subtract).then_inc(s["ev_dve"], 1)
                    return
                dve.tensor_copy(v_lg[:, bass.ds(n, 1), :], PS[:, 4 + k, 0:D + NE]).then_inc(s["ev_dve"], 1)

            def step(n, k):
                if not (isinstance(n, int) and n >= NT - 2):
                    normalise(n + 2, k)
                copy_v(n, k)
            normalise(0, 0)
            normalise(1, 1)
            tile_loop(dve, 0, NT, step)

        def route_dve(dve, l):
            s = L[l]
            count = [0]

            def link(ins):
                count[0] += 1
                ins.then_inc(s["route"], 1)
                dve.wait_ge(s["route"], count[0])

            def wide(t):
                return t[:].unsqueeze(2).to_broadcast([P, NT, NE])

            def over_tiles(t):
                return t[:].unsqueeze(1).to_broadcast([P, NT, NE])
            rel, ex, tmp, hot1, chosen, hot2 = RT
            top, first, second, e2, z, tot = r_small
            dve.wait_ge(s["ev_dve"], NT)
            dve.wait_ge(loaded_w0, 16 * 7)
            logits = v_lg[:, :, D:D + NE] if l == 0 else lg1[:]
            if l == 0:
                link(dve.tensor_tensor(tmp[:], logits, over_tiles(gb), ALU.add))
                logits = tmp[:]
            link(dve.tensor_reduce(top[:], logits, AX.X, ALU.max))
            dve.tensor_tensor(rel[:], logits, wide(top), ALU.subtract).then_inc(s["route_act"], 1)
            dve.wait_ge(s["route_act"], 2)
            link(dve.tensor_reduce(z[:], ex[:], AX.X, ALU.add))
            link(dve.tensor_scalar(tmp[:], rel[:], 0.0, None, ALU.is_ge))
            link(dve.tensor_tensor(tmp[:], tmp[:], over_tiles(iota_e), ALU.mult))
            link(dve.tensor_reduce(first[:], tmp[:], AX.X, ALU.min))
            link(dve.tensor_tensor(hot1[:], over_tiles(iota_e), wide(first), ALU.is_equal))
            link(dve.scalar_tensor_tensor(out=ex[:].rearrange("p n e -> p (n e)"),
                                          in0=hot1[:].rearrange("p n e -> p (n e)"), scalar=-BIG,
                                          in1=rel[:].rearrange("p n e -> p (n e)"), op0=ALU.mult, op1=ALU.add))
            dve.tensor_reduce(second[:], ex[:], AX.X, ALU.max).then_inc(s["route_act"], 1)
            dve.wait_ge(s["route_act"], 4)
            link(dve.tensor_tensor(tmp[:], ex[:], wide(second), ALU.is_equal))
            link(dve.tensor_tensor(tmp[:], tmp[:], over_tiles(iota_e), ALU.mult))
            link(dve.tensor_reduce(first[:], tmp[:], AX.X, ALU.min))
            link(dve.tensor_tensor(hot2[:], over_tiles(iota_e), wide(first), ALU.is_equal))
            dve.tensor_tensor(chosen[:], hot1[:], hot2[:], ALU.add).then_inc(s["route_pe"], 1)
            link(dve.reciprocal(z[:], z[:]))
            link(dve.tensor_tensor(e2[:], e2[:], z[:], ALU.mult))
            link(dve.scalar_tensor_tensor(out=tot[:], in0=z[:], scalar=1e-20, in1=e2[:], op0=ALU.add, op1=ALU.add))
            link(dve.reciprocal(tot[:], tot[:]))
            link(dve.tensor_tensor(w_top[l][0][:], z[:], tot[:], ALU.mult))
            link(dve.tensor_tensor(w_top[l][1][:], e2[:], tot[:], ALU.mult))
            dve.wait_ge(s["route_pe"], 2)
            link(dve.tensor_copy(rel[:].rearrange("p n e -> p (n e)"), PS[:, 5, 0:NT * NE]))
            src, dst, shift = rel, tmp, 1
            while shift < NT:
                link(dve.tensor_copy(dst[:, 0:shift, :], src[:, 0:shift, :]))
                link(dve.tensor_tensor(dst[:, shift:, :], src[:, shift:, :], src[:, 0:NT - shift, :], ALU.add))
                src, dst, shift = dst, (ex if dst is tmp else tmp), 2 * shift
            total, n_tiles, upto, other = r_e
            link(dve.tensor_copy(total[:], src[:, NT - 1, :]))
            link(dve.tensor_tensor(src[:], src[:], rel[:], ALU.subtract))
            link(dve.tensor_tensor(src[:].rearrange("p n e -> p (n e)"), src[:].rearrange("p n e -> p (n e)"),
                                   PS[:, 4, 0:NT * NE], ALU.add))
            link(dve.tensor_tensor(rel[:].rearrange("p n e -> p (n e)").rearrange("p (e n) -> p e n", e=NE),
                                   total[:].unsqueeze(2).to_broadcast([P, NE, NT]),
                                   steps128[:].unsqueeze(1).to_broadcast([P, NE, NT]), ALU.is_gt))
            link(dve.tensor_reduce(n_tiles[:], rel[:].rearrange("p n e -> p (n e)").rearrange("p (e n) -> p e n", e=NE),
                                   AX.X, ALU.add))
            cur, nxt = n_tiles, upto
            for shift in (1, 2, 4):
                link(dve.tensor_copy(nxt[:, 0:shift], cur[:, 0:shift]))
                link(dve.tensor_tensor(nxt[:, shift:], cur[:, shift:], cur[:, 0:NE - shift], ALU.add))
                cur, nxt = nxt, (other if nxt is upto else upto)
            ends = cur
            link(dve.tensor_tensor(nxt[:], ends[:], n_tiles[:], ALU.subtract))
            link(dve.tensor_scalar(nxt[:], nxt[:], float(P), None, ALU.mult))
            link(dve.tensor_tensor(src[:], src[:], over_tiles(nxt), ALU.add))
            link(dve.tensor_tensor(r_map[:], tile_no[:].unsqueeze(2).to_broadcast([P, NTILE, NE]),
                                   ends[:].unsqueeze(1).to_broadcast([P, NTILE, NE]), ALU.is_ge))
            link(dve.tensor_reduce(r_tile[:], r_map[:], AX.X, ALU.add))
            link(dve.tensor_scalar(expert_of[l][:], r_tile[:], float(NE - 1), None, ALU.min))
            for c, hot in enumerate((hot1, hot2)):
                link(dve.tensor_tensor(rel[:], hot[:], src[:], ALU.mult))
                link(dve.tensor_reduce(tot[:], rel[:], AX.X, ALU.add))
                ins = dve.tensor_copy(slot[l][c][:], tot[:])
                if c == 0:
                    link(ins)
            ins.then_inc(s["routed"], 1)

        def attention0_dve(dve, first, end):
            def maxima(n, k):
                dve.wait_ge(s_done, n + 1)
                if not known_below(n, 2):
                    dve.wait_ge(exp_done, n - 1)
                dve.tensor_reduce(nmax[:, k:k + 1], PS[:, 2 * k:2 * k + 2, :], AX.XY, ALU.max,
                                  negate=True).then_inc(max_done, 1)

            def copy_pT(n, k):
                dve.wait_ge(p_t, 2 * n + 1)
                if not known_below(n, 2):
                    dve.wait_ge(pv_done, n - 1)
                dve.tensor_copy(probT[:, k, 0:512], PS[:, 4, :]).then_inc(pT_dve, 1)

            def add(n, k):
                dve.wait_ge(exp_done, n + 1)
                dve.reciprocal(rden[:, k:k + 1], den[:, k:k + 1]).then_inc(rden_done, 1)
                dve.wait_ge(rden_done, n + 1)
                dve.wait_ge(pv_done, n + 1)
                dve.scalar_tensor_tensor(out=X[:, bass.ds(n, 1), :], in0=PS[:, 6 + k, 0:D].unsqueeze(1), scalar=rden[:, k:k + 1],
                                         in1=X[:, bass.ds(n, 1), :], op0=ALU.mult, op1=ALU.add).then_inc(x_att0, 1)

            def step(n, k):
                if not known(n, end - 1):
                    maxima(n + 1, 1 - k)
                copy_pT(n, k)
                if not known(n, first):
                    add(n - 1, 1 - k)
                if first > 0:
                    for c in range(NT // (end - first)):
                        combine(dve, 0, (n - first) * (NT // (end - first)) + c, c % 2, x_att0, n)
            maxima(first, 0)
            tile_loop(dve, first, end, step)
            add(end - 1, 1)

        def moe_dve(dve, l):
            s = L[l]
            FW = F0 if l == 0 else F1
            dve.wait_ge(loaded_moe[l], 16 * 4)

            def biased_product(j, k):
                if l == 1:
                    dve.wait_ge(s["pre_ready"], j + 1)
                    if not known_below(j, 2):
                        dve.wait_ge(s["hid_t"], j - 1)
                    dve.tensor_tensor(hid[:, k, 0:FW], pre[:, k, 0:FW], PS[:, 2 * k + 1, 0:FW],
                                      ALU.mult).then_inc(s["hid_ready"], 1)
                    return
                e = dve.value_load(expert_of[l][0:1, bass.ds(j, 1)], min_val=0, max_val=NE - 1)
                dve.wait_ge(s["up_done"], j + 1)
                if not known_below(j, 1):
                    dve.wait_ge(s["pre_ready"], j)
                dve.tensor_tensor(both[:], PS[:, 2 * k:2 * k + 2, 0:FW],
                                  b_in[:, bass.ds(e, 1), :].rearrange("p o (c f) -> p (o c) f", c=2),
                                  ALU.add).then_inc(s["both_ready"], 1)
                dve.wait_ge(s["both_ready"], j + 1)
                if not known_below(j, 2):
                    dve.wait_ge(s["hid_ready"], j - 1)
                dve.tensor_tensor(pre[:, k, :], both[:, 0, :], both[:, 1, :], ALU.mult).then_inc(s["pre_ready"], 1)

            def add_bias(j, k):
                if l == 1:
                    dve.wait_ge(s["dn_done"], j + 1)
                    if not known_below(j, 2):
                        dve.wait_ge(s["ye_stored"][k], 16 * turn_of(j))
                    dve.tensor_copy(ye[:, k, :], PS[:, 6 + k, 0:D]).then_inc(s["ye_ready"], 1)
                    return
                e = dve.value_load(expert_of[l][0:1, bass.ds(j, 1)], min_val=0, max_val=NE - 1)
                dve.wait_ge(s["dn_done"], j + 1)
                if not known_below(j, 2):
                    dve.wait_ge(s["ye_stored"][k], 16 * turn_of(j))
                dve.tensor_tensor(ye[:, k, :].unsqueeze(1), PS[:, 6 + k, 0:D].unsqueeze(1), b_dn[:, bass.ds(e, 1), :],
                                  ALU.add).then_inc(s["ye_ready"], 1)

            def step(j, k):
                if not (isinstance(j, int) and j == NTILE - 1):
                    biased_product(j + 1, 1 - k)
                if not known_below(j, 1):
                    add_bias(j - 1, 1 - k)
            biased_product(0, 0)
            tile_loop(dve, 0, NTILE, step)
            add_bias(NTILE - 1, 1)

        def combine(dve, l, m, k, attended, count):
            s = L[l]
            one = bass.ds(m, 1)
            dve.wait_ge(attended, count)
            dve.wait_ge(s["gathered"][k], 32 * (turn_of(m) + 1))
            dve.scalar_tensor_tensor(out=X[:, one, :], in0=gat[:, 2 * k:2 * k + 1, :], scalar=w_top[l][0][:, one],
                                     in1=X[:, one, :], op0=ALU.mult, op1=ALU.add).then_inc(s["half_sum"], 1)
            dve.wait_ge(s["half_sum"], m + 1)
            dve.scalar_tensor_tensor(out=X[:, one, :], in0=gat[:, 2 * k + 1:2 * k + 2, :], scalar=w_top[l][1][:, one],
                                     in1=X[:, one, :], op0=ALU.mult, op1=ALU.add).then_inc(s["gat_used"], 1)

        (x_att1, aux_full, aux_free, lt_hi_done, lt_ready, head_fixed, v_ready, score_done, exp1_done, pv1_done,
         oT_ready, max_ready, shiftT_ready, shift_loaded0, shift_loaded1, y_done, y_ready, y_t, yT_ready, o_done,
         chain1, hm_ready, const1, passed_pe, passed_dve, passed_sp) = (
            S(n) for n in ("x_att1 aux_full aux_free lt_hi_done lt_ready head_fixed v_ready score_done exp1_done "
                           "pv1_done oT_ready max_ready shiftT_ready shift_loaded0 shift_loaded1 y_done y_ready y_t "
                           "yT_ready o_done chain1 hm_ready const1 passed_pe passed_dve passed_sp").split())
        shift_loaded = [shift_loaded0, shift_loaded1]
        BLOCKS = [(i, 0, i) for i in range(4)] + [x for i in range(4, TB) for x in ((i, 0, 4 + i), (i, 1, i))]
        MAX_USES = HG * len(BLOCKS)
        LT_USES = 4
        BEFORE = 2 * LT_USES + MAX_USES + 1
        STEP_USES = MAX_USES + 1 + LT_USES + OUT_USES
        SPREAD = [3] * 3 + [2] * 12 + [2, 1, 1, 1, 1, 1, 1, 1, 2, 1, 1, 1, 1]

        def uses_before(q):
            return BEFORE + STEP_USES * q - (LT_USES if isinstance(q, int) and q == NG - 1 else 0)

        def group_of(q):
            if isinstance(q, int):
                return q // (HEADS // HG), q % (HEADS // HG)
            b = (q >> 2).with_bounds(min_val=0, max_val=BATCH - 1)
            return b, (q & 3).with_bounds(min_val=0, max_val=HEADS // HG - 1)

        def has(q, lead):
            return not (isinstance(q, int) and q + lead > NG - 1)

        def aux_bank(parity, offset):
            return 6 + (BEFORE + STEP_USES * parity + offset) % 2

        def head_matrices_dve(dve):
            c = [0]

            def link(ins):
                c[0] += 1
                ins.then_inc(hm_ready, 1)
                dve.wait_ge(hm_ready, c[0])
            dve.memset(heads[RANK:P, :, :], 0.0)
            link(dve.tensor_reduce(head_mean[:], heads[0:RANK, :, :].rearrange("p h s -> p s h"), AX.X, ALU.add))
            link(dve.tensor_tensor(core[:, 0, :], core[:, 0, :], core[:, 1, :], ALU.add))
            link(dve.tensor_scalar(core[:, 0, :], core[:, 0, :], 0.5 / HEADS, None, ALU.mult))
            link(dve.scalar_tensor_tensor(out=core[:, 0, :], in0=head_mean[:], scalar=-1.0 / HEADS,
                                          in1=core[:, 0, :], op0=ALU.mult, op1=ALU.add))
            link(dve.tensor_tensor(heads[0:RANK, :, :], heads[0:RANK, :, :],
                                   core[:, 0, :].unsqueeze(1).to_broadcast([RANK, HEADS, RANK]), ALU.add))

        def prepare1_dve(dve):
            dve.memset(lat_lo[RANK:RANK + 2, :], 1.0).then_inc(const1, 1)
            dve.wait_ge(const1, 1)
            dve.memset(lat_lo[RANK:RANK + 1, :], SHIFT)
            dve.memset(v9[:, :, :, HD:HD + 1], 1.0)
            dve.memset(v_rows, 0.0).then_inc(const1, 1)

        def stand_alone(eng, counter):
            eng.sem_inc(counter, 1)

        def attention1_pe(pe):
            pe.wait_ge(hm_ready, 5)
            pe.wait_ge(L[1]["ev_act"], NT)
            pe.wait_ge(L[1]["ev_dve"], NT)
            pe.wait_ge(L[1]["routed"], 1)

            def fill(u, products):
                if not known_below(u, 2):
                    pe.wait_ge(aux_free, u - 1)
                products().then_inc(aux_full, 1)

            def latent_heads(q, k, u, bank):
                b, _ = group_of(q)
                pe.wait_ge(head_fixed, q + 1)
                for pair in range(2):
                    for c in range(2):
                        o = 2 * pair + c
                        fill(u + o, lambda: pe.matmul(
                            PS[:, bank(o), :], heads_fixed[:, k, pair * P:(pair + 1) * P],
                            lat[:, bass.ds(b * SEQ + c * 512, 512)], start=True, stop=True))

            def block(q, k, u, bank, n):
                b, _ = group_of(q)
                h, (i, c, _) = n // len(BLOCKS), BLOCKS[n % len(BLOCKS)]
                width = min(512, (i + 1) * P - 512 * c)
                if n == 0:
                    pe.wait_ge(lt_ready, q + 1)
                fill(u, lambda: pe.matmul(PS[:, bank, 0:width], lt_hl[:, k, h, i * P:(i + 1) * P],
                                          lat_hi[:, bass.ds(b * SEQ + c * 512, width)], start=True, stop=True))

            def turn_shift(q, k, u, bank):
                pe.wait_ge(max_ready, 3 * (q + 1))
                fill(u, lambda: stand_alone(pe, passed_pe) or pe.transpose(PS[0:2 * HG * TB, bank, 0:P // 2].bitcast(F16),
                                             shift[:, k, :, :, :].rearrange("p r h i -> p (r h i)"), identh[:]))

            def scores(q, k, j, h):
                b, _ = group_of(q)
                n = q * (TB * HG) + j * HG + h
                if j == 0 and h == 0:
                    pe.wait_ge(shift_loaded[k], 16 * (turn_of(q) + 1))
                if not known_below(n, 2):
                    pe.wait_ge(exp1_done, n - 1)
                keys = bass.ds(b * SEQ + j * P, P)
                for c, width in enumerate([min(512, (TB - j) * P), (TB - j) * P - 512]):
                    if width <= 0:
                        continue
                    where = PS[:, 2 * (h % 2) + c, 0:width]
                    queries = slice(j * P + 512 * c, j * P + 512 * c + width)
                    pe.matmul(where, lat_hi[:, keys], lt_hl[:, k, h, queries], start=True, stop=False)
                    mm = pe.matmul(where, lat_lo[0:RANK + 2, keys], lt_hm[0:RANK + 2, k, h, queries],
                                   start=False, stop=(c == 1))
                    if c == 0:
                        mm = pe.matmul(where[:, 0:P], ident16[:], late16[:], start=False, stop=True)
                mm.then_inc(score_done, 1)

            def values(q, k, j):
                pe.wait_ge(exp1_done, q * (TB * HG) + (j + 1) * HG)
                if j == 0:
                    pe.wait_ge(v_ready, q + 1)
                    if not known_below(q, 1):
                        pe.wait_ge(oT_ready, q)
                for c in range(2):
                    lo, hi = max(j * P, 512 * c), 512 * (c + 1)
                    if lo >= hi:
                        continue
                    for h in range(HG):
                        v0 = (j * HG + h) * (HD + 1)
                        mm = pe.matmul(PS[32 * h:32 * h + 32, 4 + c, lo - 512 * c:hi - 512 * c],
                                       v_rows[:, k, v0:v0 + 32], prob1[j % 2][:, h, lo - j * P:hi - j * P],
                                       start=(j == 0), stop=(j == TB - 1 or (c == 0 and j == 3)),
                                       tile_position=(0, 32 * h))
                mm.then_inc(pv1_done, 1)

            def turn_out(q, u, bank):
                pe.wait_ge(oT_ready, q + 1)
                for o in range(OUT_USES):
                    def four():
                        for i in range(4):
                            mm = pe.transpose(PS[:, bank(o), i * P:(i + 1) * P],
                                              oT[:, (4 * o + i) * P:(4 * o + i + 1) * P], ident[:])
                        return mm
                    fill(u + o, four)

            def step(q, k):
                u = uses_before(q)
                n = 0
                for j in range(TB):
                    for h in range(HG):
                        scores(q, k, j, h)
                        if has(q, 1) and j * HG + h < len(SPREAD):
                            for _ in range(SPREAD[j * HG + h]):
                                block(q + 1, 1 - k, u + n, aux_bank(k, n), n)
                                n += 1
                    if j > 0:
                        values(q, k, j - 1)
                values(q, k, TB - 1)
                assert n in (0, MAX_USES)
                if has(q, 1):
                    turn_shift(q + 1, 1 - k, u + n, aux_bank(k, n))
                    n += 1
                if has(q, 2):
                    latent_heads(q + 2, k, u + n, lambda o: aux_bank(k, n + o))
                    n += LT_USES
                turn_out(q, u + n, lambda o: aux_bank(k, n + o))

            for q in range(2):
                latent_heads(q, q, q * LT_USES, lambda o: 6 + o % 2)
            for n in range(MAX_USES):
                block(0, 0, 2 * LT_USES + n, 6 + n % 2, n)
            turn_shift(0, 0, BEFORE - 1, 6 + (BEFORE - 1) % 2)
            tile_loop(pe, 0, NG, step)
            project_out_pe(pe)

        def project_out_pe(pe):
            pe.wait_ge(exp1_done, NG * TB * HG)

            def turn(n, k):
                pe.wait_ge(y_ready, n + 1)
                if not known_below(n, 2):
                    pe.wait_ge(yT_ready, n - 1)
                pe.transpose(PS[:, k, 0:P], y_fixed[:, k, :], ident[:]).then_inc(y_t, 1)

            def product(n, k):
                pe.wait_ge(yT_ready, n + 1)
                if not known_below(n, 2):
                    pe.wait_ge(x_att1, n - 1)
                pe.matmul(PS[:, 2 + k, 0:D], yT[:, k, :], ow[:], start=True, stop=True).then_inc(o_done, 1)

            def step(n, k):
                if not (isinstance(n, int) and n == NT - 1):
                    turn(n + 1, 1 - k)
                product(n, k)
            turn(0, 0)
            tile_loop(pe, 0, NT, step)

        def attention1_act(act):
            act.wait_ge(hm_ready, 5)
            act.wait_ge(const1, 2)
            act.wait_ge(L[1]["ev_dve"], NT)

            def fix_heads(q, k):
                _, g = group_of(q)
                if not known_below(q, 2):
                    act.wait_ge(lt_ready, q - 1)
                act.activation(heads_fixed[:, k, :].rearrange("p (h s) -> p h s", h=HG),
                               heads[:, bass.ds(g * HG, HG), :], ACT.Copy).then_inc(head_fixed, 1)

            def fix_values(q, k):
                b, g = group_of(q)
                if not known_below(q, 2):
                    act.wait_ge(pv1_done, TB * (q - 1))
                act.activation(v_fixed[k], v9[:, bass.ds(b * TB, TB), bass.ds(g * HG, HG), :],
                               ACT.Copy).then_inc(v_ready, 1)

            def latent_hi(q, k, u, bank):
                for pair in range(2):
                    for c in range(2):
                        o = 2 * pair + c
                        act.wait_ge(aux_full, u + o + 1)
                        for half in range(2):
                            rows = slice(64 * half, 64 * half + 64)
                            ins = act.activation(lt_hl[rows, k, 2 * pair + half, c * 512:(c + 1) * 512],
                                                 PS[rows, bank(o), :], ACT.Copy)
                        ins.then_inc(lt_hi_done, 1)

            def exps(q, k, j, h):
                n = q * (TB * HG) + j * HG + h
                act.wait_ge(score_done, n + 1)
                if h == 0 and not (isinstance(q, int) and q * TB + j < 2):
                    act.wait_ge(pv1_done, q * TB + j - 1)
                width = (TB - j) * P
                act.activation(prob1[j % 2][:, h, 0:width],
                               PS[:, 2 * (h % 2):2 * (h % 2) + 2, :].rearrange("p a b -> p (a b)")[:, 0:width],
                               ACT.Exp, scale=RANK ** -0.5).then_inc(exp1_done, 1)

            def step(q, k):
                for j in range(TB):
                    for h in range(HG):
                        exps(q, k, j, h)
                    if j == 0 and has(q, 2):
                        fix_heads(q + 2, k)
                act.wait_ge(pv1_done, TB * (q + 1))
                act.activation(oT, PS[:, 4:6, :].rearrange("p a b -> p (a b)"), ACT.Copy).then_inc(oT_ready, 1)
                if has(q, 2):
                    n = MAX_USES + 1
                    latent_hi(q + 2, k, uses_before(q) + n, lambda o: aux_bank(k, n + o))
                    fix_values(q + 2, k)

            for q in range(2):
                fix_heads(q, q)
                fix_values(q, q)
                latent_hi(q, q, q * LT_USES, lambda o: 6 + o % 2)
            tile_loop(act, 0, NG, step)
            project_out_act(act)

        def project_out_act(act):
            act.wait_ge(aux_free, uses_before(NG - 1) + OUT_USES)

            def fix(n, k):
                if not known_below(n, 2):
                    act.wait_ge(y_t, n - 1)
                act.activation(y_fixed[:, k, :], y1[:, bass.ds(n, 1), :], ACT.Copy).then_inc(y_ready, 1)

            def copy_yT(n, k):
                act.wait_ge(y_t, n + 1)
                if not known_below(n, 2):
                    act.wait_ge(o_done, n - 1)
                act.activation(yT[:, k, :], PS[:, k, 0:P], ACT.Copy).then_inc(yT_ready, 1)

            def step(n, k):
                if not (isinstance(n, int) and n >= NT - 2):
                    fix(n + 2, k)
                copy_yT(n, k)
            fix(0, 0)
            fix(1, 1)
            tile_loop(act, 0, NT, step)

        def attention1_dve(dve):
            def latent_lo(q, k, u, bank):
                for pair in range(2):
                    for c in range(2):
                        o = 2 * pair + c
                        cols = slice(c * 512, (c + 1) * 512)
                        dve.wait_ge(lt_hi_done, LT_USES * q + o + 1)
                        for half in range(2):
                            h = 2 * pair + half
                            rows, others = slice(64 * half, 64 * half + 64), slice(64 - 64 * half, 128 - 64 * half)
                            ins = dve.tensor_tensor(lt_hl[others, k, h, cols], PS[rows, bank(o), :],
                                                    lt_hl[rows, k, h, cols], ALU.subtract)
                        ins.then_inc(aux_free, 1)
                for h in range(HG):
                    rows = slice(64 * (h % 2), 64 * (h % 2) + 64)
                    ins = dve.tensor_copy(lt_hm[0:RANK, k, h, :], lt_hl[rows, k, h, :])
                ins.then_inc(lt_ready, 1)

            def block(q, k, u, bank, n):
                h, (i, c, column) = n // len(BLOCKS), BLOCKS[n % len(BLOCKS)]
                width = min(512, (i + 1) * P - 512 * c)
                dve.wait_ge(aux_full, u + 1)
                accum = maxima1[:, k, h, column:column + 1]
                if column < TB:
                    if not known_below(u, 2):
                        dve.wait_ge(aux_free, u - 1)
                    stand_alone(dve, passed_dve)
                    ins = dve.tensor_tensor_reduce(junk[:, bank - 6, 0:width], PS[:, bank, 0:width], late[:, 512 - width:512],
                                                   1.0, -3e38, ALU.add, ALU.max, accum)
                else:
                    ins = dve.tensor_reduce(accum, PS[:, bank, 0:width], AX.X, ALU.max)
                ins.then_inc(aux_free, 1)

            def prepare_shift(q, k):
                dve.wait_ge(aux_free, uses_before(q - 1) + MAX_USES if not isinstance(q, int) or q > 0
                            else 2 * LT_USES + MAX_USES)
                m = maxima1[:, k, :, :]
                dve.tensor_tensor(m[:, :, 4:8], m[:, :, 4:8], m[:, :, 8:12], ALU.max).then_inc(max_ready, 1)
                dve.wait_ge(max_ready, 3 * q + 1)
                dve.tensor_scalar(shift[:, k, 0, :, :], m[:, :, 0:TB], -1.0 / SHIFT, None,
                                  ALU.mult).then_inc(max_ready, 1)
                dve.wait_ge(max_ready, 3 * q + 2)
                dve.scalar_tensor_tensor(out=shift[:, k, 1, :, :], in0=shift[:, k, 0, :, :], scalar=-SHIFT,
                                         in1=m[:, :, 0:TB], op0=ALU.mult, op1=ALU.subtract).then_inc(max_ready, 1)

            def copy_shiftT(q, k, u, bank):
                dve.wait_ge(aux_full, u + 1)
                if not known_below(q, 2):
                    dve.wait_ge(shift_loaded[k], 16 * turn_of(q))
                dve.tensor_copy(shiftT[:, k, :], PS[0:2 * HG * TB, bank, 0:P // 2].bitcast(F16))\
                   .then_inc(aux_free, 1)

            def outputs(q, u, bank):
                b, g = group_of(q)
                if known(q, 0):
                    dve.wait_ge(L[1]["scattered"], 16 * 2 * NT)
                for o in range(OUT_USES):
                    dve.wait_ge(aux_full, u + o + 1)
                    o4 = PS[:, bank(o), :].rearrange("p (i h c) -> p i h c", i=4, h=HG)
                    dve.reciprocal(rden1[:, o, :, :], o4[:, :, :, HD]).then_inc(chain1, 1)
                    dve.wait_ge(chain1, OUT_USES * q + o + 1)
                    ins = dve.tensor_tensor(
                        y1[:, bass.ds(b * TB + 4 * o, 4), bass.ds(g * HG * HD, HG * HD)]
                        .rearrange("p i (h c) -> p i h c", h=HG), o4[:, :, :, 0:HD],
                        rden1[:, o, :, :].unsqueeze(3).to_broadcast([P, 4, HG, HD]), ALU.mult)
                    ins.then_inc(aux_free, 1)

            def step(q, k):
                u = uses_before(q)
                n = 0
                if has(q, 1):
                    for n in range(MAX_USES):
                        block(q + 1, 1 - k, u + n, aux_bank(k, n), n)
                    n = MAX_USES
                    prepare_shift(q + 1, 1 - k)
                    copy_shiftT(q + 1, 1 - k, u + n, aux_bank(k, n))
                    n += 1
                if has(q, 2):
                    latent_lo(q + 2, k, u + n, lambda o: aux_bank(k, n + o))
                    n += LT_USES
                outputs(q, u + n, lambda o: aux_bank(k, n + o))

            for q in range(2):
                latent_lo(q, q, q * LT_USES, lambda o: 6 + o % 2)
            for n in range(MAX_USES):
                block(0, 0, 2 * LT_USES + n, 6 + n % 2, n)
            prepare_shift(0, 0)
            copy_shiftT(0, 0, BEFORE - 1, 6 + (BEFORE - 1) % 2)
            tile_loop(dve, 0, NG, step)
            project_out_dve(dve)

        def project_out_dve(dve):
            def step(n, k):
                dve.wait_ge(o_done, n + 1)
                dve.tensor_tensor(o_tmp[:, k, :], PS[:, 2 + k, 0:D], ob[:], ALU.add).then_inc(y_done, 1)
                dve.wait_ge(y_done, n + 1)
                dve.tensor_tensor(X[:, bass.ds(n, 1), :], X[:, bass.ds(n, 1), :], o_tmp[:, k, :].unsqueeze(1),
                                  ALU.add).then_inc(x_att1, 1)
            tile_loop(dve, 0, NT, step)

        def attention1_sp(sp):
            def step(q, k):
                sp.wait_ge(aux_free, BEFORE if isinstance(q, int) and q == 0 else uses_before(q - 1) + MAX_USES + 1)
                stand_alone(sp, passed_sp)
                sp.wait_ge(lt_ready, q + 1)
                sp.dma_start(lt_hm[RANK:RANK + 2, k, :, :].rearrange("r h t -> r (h t)")
                             .rearrange("r (m t) -> r m t", t=P), shiftT[:, k, :]).then_inc(shift_loaded[k], 16)
            tile_loop(sp, 0, NG, step)

        block = ctx.enter_context(nc.Block())

        @block.sync
        def _(sp):
            sp.dma_start(X[:], a["x"].rearrange("(n p) d -> p n d", p=P)).then_inc(loaded_x, 16)
            sp.dma_start(ident[:], a["ident"]).then_inc(loaded_w0, 16)
            sp.dma_start(wq[:], a["wqkvg"]).then_inc(loaded_w0, 16)
            sp.dma_start(gb[:], a["gate_b"].partition_broadcast(P)).then_inc(loaded_w0, 16)
            sp.dma_start(before[:], a["before"]).then_inc(loaded_w0, 16)
            sp.dma_start(iota_e[:], a["iota_e"].partition_broadcast(P)).then_inc(loaded_w0, 16)
            sp.dma_start(steps128[:], a["steps128"].partition_broadcast(P)).then_inc(loaded_w0, 16)
            sp.dma_start(tile_no[:], a["tile_no"].partition_broadcast(P)).then_inc(loaded_w0, 16)
            for dst, name in ((wv1, "wv1"), (basis, "basis"), (ow, "ow"), (core, "core"), (late, "late"),
                              (late16, "late16"), (ident16, "ident16"), (identh, "identh")):
                sp.dma_start(dst[:], a[name]).then_inc(loaded_w1, 16)
            sp.dma_start(heads[0:RANK, :, :], a["heads"]).then_inc(loaded_w1, 16)
            for dst, name in ((vb, "v_b"), (ob, "o_b")):
                sp.dma_start(dst[:], a[name].partition_broadcast(P)).then_inc(loaded_w1, 16)
            sp.dma_start(w_in[:], a["w_in0"]).then_inc(loaded_moe[0], 16)
            sp.dma_start(b_in[:], a["b_in0"].partition_broadcast(P)).then_inc(loaded_moe[0], 16)
            sp.dma_start(b_dn[:], a["b_dn0"].partition_broadcast(P)).then_inc(loaded_moe[0], 16)
            sp.dma_start(w_dn[0:102, :, :, :], a["w_dn0"]).then_inc(loaded_moe[0], 16)
            moe_sp(sp, 0)
            sp.wait_ge(L[0]["ye_ready"], NTILE)
            sp.dma_start(w_in[:, :, 0:2 * F1], a["w_in1"]).then_inc(loaded_moe[1], 16)
            first = 0
            for c, m in enumerate(CH1):
                sp.dma_start(w_dn[0:m, :, c, :], a["w_dn1"][:, first:first + m, :].rearrange("e f d -> f e d"))\
                    .then_inc(loaded_moe[1], 16)
                first += m
            attention1_sp(sp)
            moe_sp(sp, 1)
            sp.wait_ge(L[1]["gat_used"], NT)
            sp.dma_start(out.rearrange("(n p) d -> p n d", p=P), X[:]).then_inc(S("stored"), 16)
            sp.wait_ge(S("stored"), 16)

        @block.gpsimd
        def _(pool):
            nc.gpsimd.memset(gat[:], 0.0).then_inc(S("zero_tile"), 1)
            pool.wait_ge(S("zero_tile"), 1)
            for l in range(2):
                pool.dma_start(slots_in[l].rearrange("(p n c) d -> p n (c d)", p=P, c=4),
                               gat[:].rearrange("p a b -> p (a b)").unsqueeze(1)
                               .to_broadcast([P, NTILE // 4, 4 * D])).then_inc(zeroed, 16)
            pool.wait_ge(zeroed, 32)
            route_pool(pool, 0)
            route_pool(pool, 1)

        @block.tensor
        def _(pe):
            pe.wait_ge(loaded_w0, 16 * 7)
            proj_pe(pe, 0)
            route_pe(pe, 0)
            attention0_pe(pe, 0, NT // 2)
            moe_pe(pe, 0)
            attention0_pe(pe, NT // 2, NT)
            pe.wait_ge(loaded_w1, 16 * W1_LOADS)
            pe.wait_ge(x_att0, NT)
            proj_pe(pe, 1)
            route_pe(pe, 1)
            attention1_pe(pe)
            moe_pe(pe, 1)

        @block.scalar
        def _(act):
            norm_act(act, 0)
            proj_act(act, 0)
            route_act(act, 0)
            attention0_act(act, 0, NT // 2)
            moe_act(act, 0)
            attention0_act(act, NT // 2, NT)
            norm_act(act, 1)
            proj_act(act, 1)
            route_act(act, 1)
            attention1_act(act)
            moe_act(act, 1)

        @block.vector
        def _(dve):
            dve.memset(ones[:], 1.0)
            dve.wait_ge(loaded_x, 16)
            norm_dve(dve, 0)
            proj_dve(dve, 0)
            route_dve(dve, 0)
            attention0_dve(dve, 0, NT // 2)
            moe_dve(dve, 0)
            attention0_dve(dve, NT // 2, NT)
            dve.wait_ge(L[0]["gat_used"], NT)
            dve.wait_ge(x_att0, NT)
            norm_dve(dve, 1)
            prepare1_dve(dve)
            dve.wait_ge(loaded_w1, 16 * W1_LOADS)
            head_matrices_dve(dve)
            proj_dve(dve, 1)
            route_dve(dve, 1)
            attention1_dve(dve)
            moe_dve(dve, 1)
            for n in range(NT):
                combine(dve, 1, n, n % 2, x_att1, NT)


INPUTS = ("L0_attn_x L0_attn_W_qkv L0_ffn_gate_w L0_ffn_gate_b L0_ffn_up_w L0_ffn_up_b L0_ffn_gp_w L0_ffn_gp_b "
          "L0_ffn_down_w L0_ffn_down_b L1_attn_basis_w L1_attn_core L1_attn_head_residual L1_attn_v_w L1_attn_v_b "
          "L1_attn_o_w L1_attn_o_b L1_ffn_Wg L1_ffn_W1 L1_ffn_W2 L1_ffn_W3").split()


def laid_out(i):
    f32 = np.float32
    a = {"x": i["L0_attn_x"].reshape(BATCH * SEQ, D)}
    a["wqkvg"] = np.concatenate([i["L0_attn_W_qkv"], i["L0_ffn_gate_w"]], 0).T
    a["gate_b"] = i["L0_ffn_gate_b"]
    a["w_in0"] = np.concatenate([i["L0_ffn_gp_w"], i["L0_ffn_up_w"]], 1).transpose(2, 0, 1)
    a["b_in0"] = np.concatenate([i["L0_ffn_gp_b"], i["L0_ffn_up_b"]], 1)
    a["w_dn0"] = i["L0_ffn_down_w"].transpose(0, 2, 1).reshape(NE, 4, 102, D).transpose(2, 0, 1, 3)
    a["b_dn0"] = i["L0_ffn_down_b"]
    a["w_in1"] = np.concatenate([i["L1_ffn_W1"], i["L1_ffn_W3"]], 1).transpose(2, 0, 1)
    a["w_dn1"] = i["L1_ffn_W2"].transpose(0, 2, 1)
    a["wv1"] = np.concatenate([i["L1_attn_v_w"], i["L1_ffn_Wg"]], 0).T
    a["basis"] = np.concatenate([i["L1_attn_basis_w"]] * 2, 0).T
    a["ow"] = i["L1_attn_o_w"].T
    a["v_b"], a["o_b"] = i["L1_attn_v_b"], i["L1_attn_o_b"]
    a["core"] = np.stack([i["L1_attn_core"], i["L1_attn_core"].T], 1)
    a["heads"] = i["L1_attn_head_residual"].transpose(1, 0, 2)
    row, col = np.arange(P)[:, None], np.arange(P)[None]
    a["late"] = np.concatenate([np.zeros((P, 3 * P), f32), np.where(col > row, f32(-BIG), f32(0))], 1).astype(mybir.dt.np(BF16))
    a["late16"] = np.where(row > col, f32(-BIG), f32(0)).astype(mybir.dt.np(BF16))
    a["ident16"] = np.eye(P).astype(mybir.dt.np(BF16))
    a["identh"] = np.eye(P, dtype=np.float16)
    a["ident"] = np.eye(P, dtype=f32)
    a["before"] = np.triu(np.ones((P, P), f32), 1)
    a["iota_e"] = np.arange(NE, dtype=f32) - NE
    a["steps128"] = np.arange(NT, dtype=f32) * P
    a["tile_no"] = np.arange(NTILE, dtype=f32)
    return {"in_" + n: np.ascontiguousarray(v) for n, v in a.items()}


def kernel(**inputs):
    import concourse.bacc as _bacc
    from concourse.bass_utils import run_bass_kernel_spmd as _run

    arrays = laid_out({n: np.asarray(inputs[n]) for n in INPUTS})
    nc = _bacc.Bacc("TRN2", target_bir_lowering=False, num_devices=1, dynamic_dma_scratch_size=DMA_RING)
    ins = {n[3:]: nc.dram_tensor(n, v.shape, mybir.dt.from_np(v.dtype), kind="ExternalInput").ap()
           for n, v in arrays.items()}
    out = nc.dram_tensor("out", (BATCH * SEQ, D), F32, kind="ExternalOutput").ap()
    two_layers(nc, ins, out)
    r = _run(nc, [arrays], core_ids=[0])
    return r.results[0]["out"].reshape(BATCH, SEQ, D)
```

```python
from contextlib import ExitStack

import numpy as np

import concourse.bass as bass
from concourse import mybir

F32 = mybir.dt.float32
F16 = mybir.dt.float16
BF16 = mybir.dt.bfloat16
I32 = mybir.dt.int32
U32 = mybir.dt.uint32
ALU = mybir.AluOpType
ACT = mybir.ActivationFunctionType
AX = mybir.AxisListType

P = 128
D = 128
BATCH, SEQ = 4, 1024
NT = BATCH * SEQ // P
TB = SEQ // P
NE = 8
F0, F1 = 408, 352
CH0 = [102] * 4
CH1 = [128, 128, 96]
NTILE = 72
NSLOT = NTILE * P
HEADS, RANK, HD = 16, 64, 8
HG = 4
NG = BATCH * HEADS // HG
DMA_RING = 4096
EPS = 1e-5
BIG = 1e30
SHIFT = 16.0


def known_below(i, bound):
    return isinstance(i, int) and i < bound


def known(i, value):
    return isinstance(i, int) and i == value


def turn_of(j):
    return j // 2 if isinstance(j, int) else j >> 1


def sequence_of(n):
    return n // TB if isinstance(n, int) else (n >> (TB.bit_length() - 1)).with_bounds(min_val=0, max_val=BATCH - 1)


def tile_loop(eng, start, end, body, unroll=4, peel=2, tail=2, before=None):
    assert (end - start - peel - tail) % unroll == 0 and (start + peel) % 2 == unroll % 2 == 0
    for i in range(start, start + peel):
        body(i, i % 2)
    with eng.Fori(0, (end - start - peel - tail) // unroll) as turn:
        for x in range(unroll):
            if before is not None:
                before(unroll * turn + start + peel, x)
            body(unroll * turn + start + peel + x, x % 2)
    for i in range(end - tail, end):
        body(i, i % 2)


def two_layers(nc, a, out):
    with ExitStack() as ctx:
        def sb(name, shape, dt=F32):
            return ctx.enter_context(nc.sbuf_tensor(name, shape, dt))

        def dram(name, shape, dt=F32):
            return nc.dram_tensor(name, shape, dt).ap()

        def sem(name):
            return ctx.enter_context(nc.semaphore(name))

        PS = ctx.enter_context(nc.psum_tensor("PS", [P, 8, 512], F32))

        slots_in = [dram("slots_in0", [NSLOT, D]), dram("slots_in1", [NSLOT, D])]
        slots_out = [dram("slots_out0", [NSLOT, D]), dram("slots_out1", [NSLOT, D])]

        X = sb("X", [P, NT, D])
        XN = sb("XN", [P, NT, D])
        ident = sb("ident", [P, P])
        before = sb("before", [P, P])
        ones = sb("ones", [P, P])
        mean = sb("mean", [P, NT])
        std = sb("std", [P, NT])
        rstd = sb("rstd", [P, NT])
        xn_fixed = sb("xn_fixed", [P, 2, D])
        xnT = sb("xnT", [P, 2, P])
        iota_e = sb("iota_e", [P, NE])
        steps128 = sb("steps128", [P, NT])
        tile_no = sb("tile_no", [P, NTILE])
        r_tile = sb("r_tile", [P, NTILE])
        r_small = [sb("r_small%d" % i, [P, NT]) for i in range(6)]
        r_e = [sb("r_e%d" % i, [P, NE]) for i in range(4)]
        w_top = [[sb("w_top%d_%d" % (l, c), [P, NT]) for c in range(2)] for l in range(2)]
        slot = [[sb("slot%d_%d" % (l, c), [P, NT], I32) for c in range(2)] for l in range(2)]
        expert_of = [sb("expert_of%d" % l, [P, NTILE], I32) for l in range(2)]
        w_in = sb("w_in", [P, NE, 2 * F0])
        w_dn = sb("w_dn", [P, NE, 4, D])
        xe = sb("xe", [P, 2, D])
        xeT = sb("xeT", [P, 2, P])
        ye = sb("ye", [P, 2, D])
        gat = sb("gat", [P, 4, D])
        zeros = gat[:].rearrange("p a b -> p (a b)")
        ARENA = 30400
        arena = sb("arena", [P, ARENA])
        at = [0]

        def carve(cols, dt=F32):
            view = arena[:, at[0]:at[0] + cols]
            at[0] += cols
            assert at[0] <= ARENA, at[0]
            return view if dt == F32 else view.bitcast(dt)

        kT = carve(NT * P).rearrange("p (n t) -> p n t", t=P)
        qT = carve(NT * P).rearrange("p (n t) -> p n t", t=P)
        v_lg = carve(NT * (D + NE)).rearrange("p (n c) -> p n c", c=D + NE)
        work = at[0]
        prob = carve(2 * SEQ).rearrange("p (k c) -> p k c", k=2)
        probT = carve(2 * SEQ).rearrange("p (k c) -> p k c", k=2)
        at[0] = work

        def routing_buffers():
            return ([carve(NT * NE).rearrange("p (n e) -> p n e", e=NE) for _ in range(6)],
                    carve(NTILE * NE).rearrange("p (j e) -> p j e", e=NE))
        routing = [routing_buffers()]
        at[0] = work
        both = carve(2 * F0).rearrange("p (c f) -> p c f", c=2)

        def experts_buffers(width, chunks):
            pre = carve(2 * width).rearrange("p (k f) -> p k f", k=2)
            hid = carve(2 * width).rearrange("p (k f) -> p k f", k=2)
            return pre, hid, carve(2 * chunks * P).rearrange("p (k c t) -> p k c t", k=2, c=chunks)
        experts = [experts_buffers(F0, len(CH0))]
        at[0] = work + 4 * SEQ
        b_in = carve(NE * 2 * F0).rearrange("p (e f) -> p e f", e=NE)
        b_dn = carve(NE * D).rearrange("p (e d) -> p e d", e=NE)
        at[0] = 0
        lat = carve(BATCH * SEQ)
        lat_hi = carve(BATCH * SEQ // 2, F16)
        lat_lo = carve(BATCH * SEQ // 2, F16)
        v9 = carve(NT * HEADS * (HD + 1)).rearrange("p (n h c) -> p n h c", h=HEADS, c=HD + 1)
        lt_hl = carve(2 * HG * SEQ // 2, F16).rearrange("p (k h t) -> p k h t", k=2, h=HG)
        lt_hm = carve(2 * HG * SEQ // 2, F16).rearrange("p (k h t) -> p k h t", k=2, h=HG)
        start = at[0]
        routing.append(routing_buffers())
        at[0] = start
        stats = [rt[0].rearrange("p n e -> p (n e)")[:, 0:NT * 6].rearrange("p (n c) -> p n c", c=6)
                 for rt, _ in routing]
        prob1 = [carve(HG * w).rearrange("p (h t) -> p h t", h=HG) for w in (SEQ, SEQ - P)]
        after = at[0]
        at[0] -= HG * (SEQ - P)
        experts.append(experts_buffers(F1, len(CH1)))
        assert at[0] <= after
        at[0] = after
        after = at[0]
        at[0] = 0
        y_fixed, yT, o_tmp = [carve(2 * 4 * P).rearrange("p (k i c) -> p k i c", k=2, i=4) for _ in range(3)]
        at[0] = after
        V_COLS = TB * HG * (HD + 1)
        v_rows = carve(2 * (V_COLS + 32)).rearrange("p (k c) -> p k c", k=2)
        v_fixed = [v_rows[:, k, 0:V_COLS].rearrange("p (j h c) -> p j h c", j=TB, h=HG) for k in range(2)]
        oT = carve(SEQ)
        y1 = XN

        wq = sb("wq", [P, 3 * D + NE])
        gb = sb("gb", [P, NE])
        heads_fixed = sb("heads_fixed", [P, 2, HG * RANK])
        q_fixed = heads_fixed[:, 0, :].rearrange("p (k t) -> p k t", k=2)
        core = heads_fixed[0:RANK, 1, 0:2 * RANK].rearrange("p (c s) -> p c s", c=2)
        head_mean = heads_fixed[0:RANK, 1, 2 * RANK:3 * RANK]
        nmax = sb("nmax", [P, 2])
        den = sb("den", [P, 2])
        rden = sb("rden", [P, 2])

        wv1 = sb("wv1", [P, D + NE])
        basis = sb("basis", [P, P])
        vb = sb("vb", [P, D])
        ob = sb("ob", [P, D])
        ow = sb("ow", [P, D])
        lg1 = sb("lg1", [P, NT, NE])
        heads = sb("heads", [P, HEADS, RANK])
        late = sb("late", [P, 512], BF16)
        late16 = sb("late16", [P, P], BF16)
        ident16 = sb("ident16", [P, P], BF16)
        identh = sb("identh", [P, P], F16)
        gat_junk = gat[:].rearrange("p (k a) b -> p k (a b)", k=2)
        junk = [[gat_junk[:, k, :].bitcast(BF16) for k in range(2)],
                [t[:].rearrange("p a b -> p (a b)").bitcast(BF16) for t in (xe, xeT)]]
        maxima1 = sb("maxima1", [P, 2, HG, 12])
        shift = sb("shift", [P, 2, 2, HG, TB], F16)
        shiftT = sb("shiftT", [2 * HG * TB, 2, P], F16)
        rden1 = sb("rden1", [P, 2, 4, HG])

        block_sems = {}

        def S(name):
            if name not in block_sems:
                block_sems[name] = sem(name)
            return block_sems[name]

        loaded_x = [S("loaded_x%d" % b) for b in range(BATCH)]
        loaded_wq = S("loaded_wq")
        loaded_w0 = S("loaded_w0")
        loaded_w1 = S("loaded_w1")
        W1_LOADS = 11
        loaded_moe = [S("loaded_moe0"), S("loaded_moe1")]
        zeroed = [S("zeroed0"), S("zeroed1")]
        names = ("stats mv var sd rstd xs_ready xn_ready xn_t xt_ready proj ev_act ev_dve route route_act "
                 "route_pe routed scattered xe_t xeT_ready up_done pre_ready hid_ready hid_t "
                 "hidT_ready dn_done ye_ready gat_used half_sum both_ready").split()
        L = [{n: S(n + str(l)) for n in names} for l in range(2)]
        for l in range(2):
            for n in ("xe_loaded", "ye_stored", "gathered"):
                L[l][n] = [S(n + "%d_%d" % (l, k)) for k in range(2)]
        q_ready, s_done, max_done, exp_done, p_t, pT_ready, pv_done, rden_done, x_att0 = (
            S(n) for n in "q_ready s_done max_done exp_done p_t pT_ready pv_done rden_done x_att0".split())



        def moe_sp(sp, l):
            s = L[l]
            sp.wait_ge(s["scattered"], 16 * 2 * NT)

            def load(j, k):
                if not known_below(j, 2):
                    sp.wait_ge(s["xe_t"], j - 1)
                sp.dma_start(xe[:, k, :], slots_in[l][bass.ds(j * P, P), :]).then_inc(s["xe_loaded"][k], 16)

            def store(j, k):
                sp.wait_ge(s["ye_ready"], j + 1)
                sp.dma_start(slots_out[l][bass.ds(j * P, P), :], ye[:, k, :]).then_inc(s["ye_stored"][k], 16)

            def step(j, k):
                if not (isinstance(j, int) and j >= NTILE - 2):
                    load(j + 2, k)
                if not known_below(j, 2):
                    store(j - 2, k)
            load(0, 0)
            load(1, 1)
            tile_loop(sp, 0, NTILE, step)
            store(NTILE - 2, 0)
            store(NTILE - 1, 1)

        def zero_slots(pool, l):
            pool.dma_start(slots_in[l].rearrange("(p n c) d -> p n (c d)", p=P, c=4),
                           zeros.unsqueeze(1).to_broadcast([P, NTILE // 4, 4 * D])).then_inc(zeroed[l], 16)

        def route_pool(pool, l):
            s = L[l]
            pool.wait_ge(s["routed"], 1)
            pool.wait_ge(s["xn_ready"], NT)
            pool.wait_ge(zeroed[l], 16)
            for n in range(NT):
                for c in range(2):
                    pool.indirect_dma_start(
                        out=slots_in[l], out_offset=bass.IndirectOffsetOnAxis(ap=slot[l][c][:, n:n + 1], axis=0),
                        in_=XN[:, n, :], in_offset=None).then_inc(s["scattered"], 16)
            pool.wait_ge(zeroed[1], 16)
            for k in range(2):
                pool.wait_ge(s["ye_stored"][k], 16 * (NTILE // 2))
            for n in range(NT):
                if n >= 2:
                    pool.wait_ge(s["gat_used"], n - 1)
                for c in range(2):
                    pool.indirect_dma_start(
                        out=gat[:, 2 * (n % 2) + c, :], out_offset=None, in_=slots_out[l],
                        in_offset=bass.IndirectOffsetOnAxis(ap=slot[l][c][:, n:n + 1], axis=0),
                    ).then_inc(s["gathered"][n % 2], 16)

        def proj_pe(pe, l):
            s = L[l]

            def transpose(n, k):
                pe.wait_ge(s["xs_ready"], n + 1)
                if not known_below(n, 2):
                    pe.wait_ge(s["xt_ready"], n - 1)
                pe.transpose(PS[:, k, 0:P], xn_fixed[:, k, :], ident[:]).then_inc(s["xn_t"], 1)

            def project(n, k):
                pe.wait_ge(s["xt_ready"], n + 1)
                if not known_below(n, 2):
                    pe.wait_ge(s["ev_act"], n - 1)
                    pe.wait_ge(s["ev_dve"], n - 1)
                bank = PS[:, 2 + k, :]
                if l == 0:
                    pe.matmul(bank[:, 0:P], wq[:, D:2 * D], xnT[:, k, :], start=True, stop=True)
                    pe.matmul(bank[:, P:2 * P], wq[:, 0:D], xnT[:, k, :], start=True, stop=True)
                else:
                    pe.matmul(bank[:, 0:P], basis[:], xnT[:, k, :], start=True, stop=True)
                rows = wq[:, 2 * D:3 * D + NE] if l == 0 else wv1[:]
                pe.matmul(PS[:, 4 + k, 0:D + NE], xnT[:, k, :], rows,
                          start=True, stop=True).then_inc(s["proj"], 1)

            def step(n, k):
                if not (isinstance(n, int) and n == NT - 1):
                    transpose(n + 1, 1 - k)
                project(n, k)
            transpose(0, 0)
            tile_loop(pe, 0, NT, step)

        def route_pe(pe, l):
            s = L[l]
            pe.wait_ge(loaded_w0, 16 * 5)
            pe.wait_ge(s["route_pe"], 1)
            chosen = routing[l][0][4][:].rearrange("p n e -> p (n e)")
            pe.matmul(PS[:, 6, 0:NT * NE], before[:], chosen, start=True, stop=True)
            pe.matmul(PS[:, 7, 0:NT * NE], ones[:], chosen, start=True, stop=True).then_inc(s["route_pe"], 1)

        def attention0_pe(pe, first, end):
            if first == 0:
                pe.wait_ge(L[0]["ev_act"], NT)
                pe.wait_ge(L[0]["ev_dve"], NT)
            else:
                pe.wait_ge(L[0]["ye_ready"], NTILE)

            def scores(n, k):
                pe.wait_ge(q_ready, n + 1)
                if not known_below(n, 2):
                    pe.wait_ge(exp_done, n - 1)
                b = sequence_of(n)
                for c in range(2):
                    mm = pe.matmul(PS[:, 2 * k + c, :], q_fixed[:, k, :], kT[:, bass.ds(b * TB + 4 * c, 4), :],
                                   start=True, stop=True)
                mm.then_inc(s_done, 1)

            def turn(n, k):
                pe.wait_ge(exp_done, n + 1)
                if not known_below(n, 1):
                    pe.wait_ge(pT_ready, n)
                for c in range(TB):
                    mm = pe.transpose(PS[:, 4 + c // 4, (c % 4) * P:(c % 4 + 1) * P],
                                      prob[:, k, c * P:(c + 1) * P], ident[:])
                mm.then_inc(p_t, 1)

            def values(n, k):
                pe.wait_ge(pT_ready, n + 1)
                if known(n, 0):
                    pe.wait_ge(L[0]["routed"], 1)
                if not known_below(n, 2):
                    pe.wait_ge(x_att0, n - 1)
                b = sequence_of(n)
                for c in range(TB):
                    mm = pe.matmul(PS[:, 6 + k, 0:D], probT[:, k, c * P:(c + 1) * P],
                                   v_lg[:, bass.ds(b * TB + c, 1), 0:D], start=(c == 0), stop=(c == TB - 1))
                mm.then_inc(pv_done, 1)

            def step(n, k):
                if not known(n, end - 1):
                    scores(n + 1, 1 - k)
                turn(n, k)
                if not known(n, first):
                    values(n - 1, 1 - k)
            scores(first, 0)
            tile_loop(pe, first, end, step)
            values(end - 1, 1)

        class Experts:
            def __init__(self, eng, l):
                self.eng, self.of, self.place = eng, expert_of[l], None
                self.registers = [eng.alloc_register("expert%d_%d" % (l, i)) for i in range(8)]

            def before(self, first, x):
                self.place = x
                if x == 0:
                    self.eng.load(self.registers, self.of[0:1, bass.ds(first - 2, 8)])
                    self.values = [self.eng.snap(r).with_bounds(min_val=0, max_val=NE - 1) for r in self.registers]

            def __call__(self, j, lead):
                if isinstance(j, int):
                    return self.eng.value_load(self.of[0:1, j:j + 1], min_val=0, max_val=NE - 1)
                return self.values[self.place + 2 + lead]

        def moe_pe(pe, l):
            expert = Experts(pe, l)
            s = L[l]
            pre, hid, hidT = experts[l]
            FW, chunks = (F0, CH0) if l == 0 else (F1, CH1)
            pe.wait_ge(loaded_moe[l], 16 * 4)
            pe.wait_ge(s["routed"], 1)
            if l == 0:
                pe.wait_ge(x_att0, NT // 2)

            def turn_in(j, k):
                pe.wait_ge(s["xe_loaded"][k], 16 * (turn_of(j) + 1))
                if not known_below(j, 1):
                    pe.wait_ge(s["xeT_ready"], j)
                pe.transpose(PS[:, 4, 0:P], xe[:, k, :], ident[:]).then_inc(s["xe_t"], 1)

            def up(j, k):
                e = expert(j, 1)
                pe.wait_ge(s["xeT_ready"], j + 1)
                if not known_below(j, 2):
                    pe.wait_ge(s["pre_ready"], j - 1)
                    if l == 1:
                        pe.wait_ge(s["hid_ready"], j - 1)
                for c in range(2):
                    mm = pe.matmul(PS[:, 2 * k + c, 0:FW], xeT[:, k, :], w_in[:, bass.ds(e, 1), c * FW:(c + 1) * FW],
                                   start=True, stop=True)
                mm.then_inc(s["up_done"], 1)

            def turn_hidden(j, k):
                pe.wait_ge(s["hid_ready"], j + 1)
                if not known_below(j, 1):
                    pe.wait_ge(s["hidT_ready"], j)
                f = 0
                for c, m in enumerate(chunks):
                    mm = pe.transpose(PS[0:m, 5, c * P:(c + 1) * P], hid[:, k, f:f + m], ident[:])
                    f += m
                mm.then_inc(s["hid_t"], 1)

            def down(j, k):
                e = expert(j, -1)
                pe.wait_ge(s["hidT_ready"], j + 1)
                if not known_below(j, 2):
                    pe.wait_ge(s["ye_ready"], j - 1)
                for c, m in enumerate(chunks):
                    mm = pe.matmul(PS[:, 6 + k, 0:D], hidT[0:m, k, c, :], w_dn[0:m, bass.ds(e, 1), c, :],
                                   start=(c == 0), stop=(c == len(chunks) - 1))
                mm.then_inc(s["dn_done"], 1)

            def step(j, k):
                last = isinstance(j, int) and j >= NTILE - 2
                if not (last and j == NTILE - 1):
                    up(j + 1, 1 - k)
                if not last:
                    turn_in(j + 2, k)
                turn_hidden(j, k)
                if not known_below(j, 1):
                    down(j - 1, 1 - k)
            turn_in(0, 0)
            up(0, 0)
            turn_in(1, 1)
            tile_loop(pe, 0, NTILE, step, before=expert.before)
            down(NTILE - 1, 1)

        def norm_act(act, l):
            s = L[l]
            act.wait_ge(s["var"], 1)
            act.activation(std[:], std[:], ACT.Sqrt).then_inc(s["sd"], 1)

        def proj_act(act, l):
            s = L[l]

            def copy_xnT(n, k):
                act.wait_ge(s["xn_t"], n + 1)
                if not known_below(n, 2):
                    act.wait_ge(s["proj"], n - 1)
                act.activation(xnT[:, k, :], PS[:, k, 0:P], ACT.Copy).then_inc(s["xt_ready"], 1)

            def copy_row(n, k):
                act.wait_ge(s["xs_ready"], n + 1)
                act.activation(XN[:, bass.ds(n, 1), :], xn_fixed[:, k, :].unsqueeze(1), ACT.Copy).then_inc(s["xn_ready"], 1)

            def copy_kq(n, k):
                act.wait_ge(s["proj"], n + 1)
                if l == 1:
                    act.activation(lat[:, bass.ds(n * P, P)], PS[:, 2 + k, 0:P], ACT.Copy)
                    act.activation(lat_hi[:, bass.ds(n * P, P)], PS[:, 2 + k, 0:P], ACT.Copy).then_inc(s["ev_act"], 1)
                    return
                act.activation(kT[:, bass.ds(n, 1), :], PS[:, 2 + k, 0:P], ACT.Copy)
                act.activation(qT[:, bass.ds(n, 1), :], PS[:, 2 + k, P:2 * P], ACT.Copy,
                               scale=float(D) ** -0.5).then_inc(s["ev_act"], 1)

            def step(n, k):
                if not (isinstance(n, int) and n == NT - 1):
                    copy_xnT(n + 1, 1 - k)
                    copy_row(n + 1, 1 - k)
                copy_kq(n, k)
            copy_xnT(0, 0)
            copy_row(0, 0)
            tile_loop(act, 0, NT, step)

        def route_act(act, l):
            s = L[l]
            act.wait_ge(s["route_act"], 1)
            rel, ex = routing[l][0][0:2]
            act.activation(ex[:], rel[:], ACT.Exp).then_inc(s["route_act"], 1)
            act.wait_ge(s["route_act"], 3)
            act.activation(r_small[3][:], r_small[2][:], ACT.Exp).then_inc(s["route_act"], 1)

        def attention0_act(act, first, end):
            if first == 0:
                act.wait_ge(L[0]["ev_act"], NT)

            def copy_q(n, k):
                if not known_below(n, 2):
                    act.wait_ge(s_done, n - 1)
                act.activation(q_fixed[:, k, :], qT[:, bass.ds(n, 1), :], ACT.Copy).then_inc(q_ready, 1)

            def exps(n, k):
                act.wait_ge(max_done, n + 1)
                if not known_below(n, 2):
                    act.wait_ge(p_t, n - 1)
                    act.wait_ge(rden_done, n - 1)
                act.activation(prob[:, k, :], PS[:, 2 * k:2 * k + 2, :].rearrange("p a b -> p (a b)"), ACT.Exp,
                               bias=nmax[:, k:k + 1], accum_out=den[:, k:k + 1]).then_inc(exp_done, 1)

            def copy_pT(n, k):
                act.wait_ge(p_t, n + 1)
                if not known_below(n, 2):
                    act.wait_ge(pv_done, n - 1)
                act.activation(probT[:, k, :], PS[:, 4:6, :].rearrange("p a b -> p (a b)"), ACT.Copy).then_inc(pT_ready, 1)

            def step(n, k):
                if not (known(n, end - 2) or known(n, end - 1)):
                    copy_q(n + 2, k)
                if not known(n, end - 1):
                    exps(n + 1, 1 - k)
                copy_pT(n, k)
            copy_q(first, 0)
            copy_q(first + 1, 1)
            exps(first, 0)
            tile_loop(act, first, end, step)

        def moe_act(act, l):
            s = L[l]
            pre, hid, hidT = experts[l]
            FW, chunks = (F0, CH0) if l == 0 else (F1, CH1)

            def copy_xeT(j, k):
                act.wait_ge(s["xe_t"], j + 1)
                if not known_below(j, 2):
                    act.wait_ge(s["up_done"], j - 1)
                act.activation(xeT[:, k, :], PS[:, 4, 0:P], ACT.Copy).then_inc(s["xeT_ready"], 1)

            def silu(j, k):
                if l == 1:
                    act.wait_ge(s["up_done"], j + 1)
                    if not known_below(j, 2):
                        act.wait_ge(s["hid_ready"], j - 1)
                    act.activation(pre[:, k, 0:FW], PS[:, 2 * k, 0:FW], ACT.Silu).then_inc(s["pre_ready"], 1)
                    return
                act.wait_ge(s["pre_ready"], j + 1)
                if not known_below(j, 2):
                    act.wait_ge(s["hid_t"], j - 1)
                act.activation(hid[:, k, 0:FW], pre[:, k, 0:FW], ACT.Silu).then_inc(s["hid_ready"], 1)

            def copy_hidT(j, k):
                act.wait_ge(s["hid_t"], j + 1)
                if not known_below(j, 2):
                    act.wait_ge(s["dn_done"], j - 1)
                if l == 0:
                    act.activation(hidT[0:102, k, :, :].rearrange("p a b -> p (a b)"), PS[0:102, 5, :],
                                   ACT.Copy).then_inc(s["hidT_ready"], 1)
                else:
                    act.activation(hidT[0:96, k, 2, :], PS[0:96, 5, 2 * P:3 * P], ACT.Copy)
                    act.activation(hidT[:, k, 0:2, :].rearrange("p a b -> p (a b)"), PS[:, 5, 0:2 * P],
                                   ACT.Copy).then_inc(s["hidT_ready"], 1)

            def step(j, k):
                last = isinstance(j, int) and j >= NTILE - 2
                if not last:
                    copy_xeT(j + 2, k)
                copy_hidT(j, k)
                if not (last and j == NTILE - 1):
                    silu(j + 1, 1 - k)
            copy_xeT(0, 0)
            copy_xeT(1, 1)
            silu(0, 0)
            tile_loop(act, 0, NTILE, step)

        def stats_dve(dve, l, n):
            dve.bn_stats(stats[l][:, n, :], X[:, n, :]).then_inc(L[l]["stats"], 1)

        def norm_dve(dve, l):
            s = L[l]
            total, apart, square = r_small[0:3]
            dve.wait_ge(s["stats"], NT)
            even, odd = stats[l][:, :, 0:3], stats[l][:, :, 3:6]
            dve.tensor_tensor(total[:], even[:, :, 1], odd[:, :, 1], ALU.add)
            dve.tensor_tensor(apart[:], even[:, :, 1], odd[:, :, 1], ALU.subtract)
            dve.tensor_tensor(std[:], even[:, :, 2], odd[:, :, 2], ALU.add).then_inc(s["mv"], 1)
            dve.wait_ge(s["mv"], 1)
            dve.tensor_scalar(mean[:], total[:], 0.5, None, ALU.mult)
            dve.tensor_tensor(square[:], apart[:], apart[:], ALU.mult)
            dve.tensor_scalar(std[:], std[:], 1.0 / D, EPS, ALU.mult, ALU.add).then_inc(s["mv"], 1)
            dve.wait_ge(s["mv"], 2)
            dve.scalar_tensor_tensor(out=std[:], in0=square[:], scalar=0.25, in1=std[:],
                                     op0=ALU.mult, op1=ALU.add).then_inc(s["var"], 1)
            dve.wait_ge(s["sd"], 1)
            dve.reciprocal(rstd[:], std[:]).then_inc(s["rstd"], 1)
            dve.wait_ge(s["rstd"], 1)

        def proj_dve(dve, l):
            s = L[l]

            def normalise(n, k):
                if not known_below(n, 2):
                    dve.wait_ge(s["xn_t"], n - 1)
                    dve.wait_ge(s["xn_ready"], n - 1)
                dve.tensor_scalar(xn_fixed[:, k, :], X[:, bass.ds(n, 1), :], mean[:, bass.ds(n, 1)],
                                  rstd[:, bass.ds(n, 1)], ALU.subtract, ALU.mult).then_inc(s["xs_ready"], 1)

            def copy_v(n, k):
                dve.wait_ge(s["proj"], n + 1)
                if l == 1:
                    dve.tensor_tensor(v9[:, bass.ds(n, 1), :, 0:HD],
                                      PS[:, 4 + k, 0:D].rearrange("p (o h c) -> p o h c", o=1, h=HEADS),
                                      vb[:].rearrange("p (o h c) -> p o h c", o=1, h=HEADS), ALU.add)
                    dve.tensor_copy(lg1[:, bass.ds(n, 1), :], PS[:, 4 + k, D:D + NE].unsqueeze(1))
                    return
                dve.tensor_copy(v_lg[:, bass.ds(n, 1), :], PS[:, 4 + k, 0:D + NE]).then_inc(s["ev_dve"], 1)

            def latent_rest(n, k):
                dve.wait_ge(s["ev_act"], n + 1)
                dve.tensor_tensor(lat_lo[0:RANK, bass.ds(n * P, P)], PS[0:RANK, 2 + k, 0:P],
                                  lat_hi[0:RANK, bass.ds(n * P, P)], ALU.subtract).then_inc(s["ev_dve"], 1)

            def step(n, k):
                if not (isinstance(n, int) and n >= NT - 2):
                    normalise(n + 2, k)
                if l == 1 and not known(n, 0):
                    latent_rest(n - 1, 1 - k)
                copy_v(n, k)
            normalise(0, 0)
            normalise(1, 1)
            tile_loop(dve, 0, NT, step)
            if l == 1:
                latent_rest(NT - 1, 1)

        def route_dve(dve, l):
            s = L[l]
            count = [0]

            def link(ins):
                count[0] += 1
                ins.then_inc(s["route"], 1)
                dve.wait_ge(s["route"], count[0])

            def wide(t):
                return t[:].unsqueeze(2).to_broadcast([P, NT, NE])

            def over_tiles(t):
                return t[:].unsqueeze(1).to_broadcast([P, NT, NE])
            (rel, ex, tmp, hot1, chosen, hot2), r_map = routing[l]
            top, first, second, e2, z, tot = r_small
            dve.wait_ge(s["ev_dve"], NT)
            dve.wait_ge(loaded_w0, 16 * 5)
            logits = v_lg[:, :, D:D + NE] if l == 0 else lg1[:]
            if l == 0:
                link(dve.tensor_tensor(tmp[:], logits, over_tiles(gb), ALU.add))
                logits = tmp[:]
            link(dve.tensor_reduce(top[:], logits, AX.X, ALU.max))
            dve.tensor_tensor(rel[:], logits, wide(top), ALU.subtract).then_inc(s["route_act"], 1)
            dve.wait_ge(s["route_act"], 2)
            link(dve.tensor_reduce(z[:], ex[:], AX.X, ALU.add))
            link(dve.tensor_scalar(tmp[:], rel[:], 0.0, None, ALU.is_ge))
            link(dve.tensor_tensor(tmp[:], tmp[:], over_tiles(iota_e), ALU.mult))
            link(dve.tensor_reduce(first[:], tmp[:], AX.X, ALU.min))
            link(dve.tensor_tensor(hot1[:], over_tiles(iota_e), wide(first), ALU.is_equal))
            link(dve.scalar_tensor_tensor(out=ex[:].rearrange("p n e -> p (n e)"),
                                          in0=hot1[:].rearrange("p n e -> p (n e)"), scalar=-BIG,
                                          in1=rel[:].rearrange("p n e -> p (n e)"), op0=ALU.mult, op1=ALU.add))
            dve.tensor_reduce(second[:], ex[:], AX.X, ALU.max).then_inc(s["route_act"], 1)
            dve.wait_ge(s["route_act"], 4)
            link(dve.tensor_tensor(tmp[:], ex[:], wide(second), ALU.is_equal))
            link(dve.tensor_tensor(tmp[:], tmp[:], over_tiles(iota_e), ALU.mult))
            link(dve.tensor_reduce(first[:], tmp[:], AX.X, ALU.min))
            link(dve.tensor_tensor(hot2[:], over_tiles(iota_e), wide(first), ALU.is_equal))
            dve.tensor_tensor(chosen[:], hot1[:], hot2[:], ALU.add).then_inc(s["route_pe"], 1)
            link(dve.reciprocal(z[:], z[:]))
            link(dve.tensor_tensor(e2[:], e2[:], z[:], ALU.mult))
            link(dve.scalar_tensor_tensor(out=tot[:], in0=z[:], scalar=1e-20, in1=e2[:], op0=ALU.add, op1=ALU.add))
            link(dve.reciprocal(tot[:], tot[:]))
            link(dve.tensor_tensor(w_top[l][0][:], z[:], tot[:], ALU.mult))
            link(dve.tensor_tensor(w_top[l][1][:], e2[:], tot[:], ALU.mult))
            dve.wait_ge(s["route_pe"], 2)
            link(dve.tensor_copy(rel[:].rearrange("p n e -> p (n e)"), PS[:, 7, 0:NT * NE]))
            src, dst, shift = rel, tmp, 1
            while shift < NT:
                link(dve.tensor_copy(dst[:, 0:shift, :], src[:, 0:shift, :]))
                link(dve.tensor_tensor(dst[:, shift:, :], src[:, shift:, :], src[:, 0:NT - shift, :], ALU.add))
                src, dst, shift = dst, (ex if dst is tmp else tmp), 2 * shift
            total, n_tiles, upto, other = r_e
            link(dve.tensor_copy(total[:], src[:, NT - 1, :]))
            link(dve.tensor_tensor(src[:], src[:], rel[:], ALU.subtract))
            link(dve.tensor_tensor(src[:].rearrange("p n e -> p (n e)"), src[:].rearrange("p n e -> p (n e)"),
                                   PS[:, 6, 0:NT * NE], ALU.add))
            link(dve.tensor_tensor(rel[:].rearrange("p n e -> p (n e)").rearrange("p (e n) -> p e n", e=NE),
                                   total[:].unsqueeze(2).to_broadcast([P, NE, NT]),
                                   steps128[:].unsqueeze(1).to_broadcast([P, NE, NT]), ALU.is_gt))
            link(dve.tensor_reduce(n_tiles[:], rel[:].rearrange("p n e -> p (n e)").rearrange("p (e n) -> p e n", e=NE),
                                   AX.X, ALU.add))
            cur, nxt = n_tiles, upto
            for shift in (1, 2, 4):
                link(dve.tensor_copy(nxt[:, 0:shift], cur[:, 0:shift]))
                link(dve.tensor_tensor(nxt[:, shift:], cur[:, shift:], cur[:, 0:NE - shift], ALU.add))
                cur, nxt = nxt, (other if nxt is upto else upto)
            ends = cur
            link(dve.tensor_tensor(nxt[:], ends[:], n_tiles[:], ALU.subtract))
            link(dve.tensor_scalar(nxt[:], nxt[:], float(P), None, ALU.mult))
            link(dve.tensor_tensor(src[:], src[:], over_tiles(nxt), ALU.add))
            link(dve.tensor_tensor(r_map[:], tile_no[:].unsqueeze(2).to_broadcast([P, NTILE, NE]),
                                   ends[:].unsqueeze(1).to_broadcast([P, NTILE, NE]), ALU.is_ge))
            link(dve.tensor_reduce(r_tile[:], r_map[:], AX.X, ALU.add))
            link(dve.tensor_scalar(expert_of[l][:], r_tile[:], float(NE - 1), None, ALU.min))
            for c, hot in enumerate((hot1, hot2)):
                link(dve.tensor_tensor(rel[:], hot[:], src[:], ALU.mult))
                link(dve.tensor_reduce(tot[:], rel[:], AX.X, ALU.add))
                ins = dve.tensor_copy(slot[l][c][:], tot[:])
                if c == 0:
                    link(ins)
            ins.then_inc(s["routed"], 1)

        def attention0_dve(dve, first, end):
            def maxima(n, k):
                dve.wait_ge(s_done, n + 1)
                if not known_below(n, 2):
                    dve.wait_ge(exp_done, n - 1)
                dve.tensor_reduce(nmax[:, k:k + 1], PS[:, 2 * k:2 * k + 2, :], AX.XY, ALU.max,
                                  negate=True).then_inc(max_done, 1)

            def add(n, k):
                dve.wait_ge(exp_done, n + 1)
                dve.reciprocal(rden[:, k:k + 1], den[:, k:k + 1]).then_inc(rden_done, 1)
                dve.wait_ge(rden_done, n + 1)
                dve.wait_ge(pv_done, n + 1)
                dve.scalar_tensor_tensor(out=X[:, bass.ds(n, 1), :], in0=PS[:, 6 + k, 0:D].unsqueeze(1), scalar=rden[:, k:k + 1],
                                         in1=X[:, bass.ds(n, 1), :], op0=ALU.mult, op1=ALU.add).then_inc(x_att0, 1)

            def step(n, k):
                if not known(n, end - 1):
                    maxima(n + 1, 1 - k)
                if not known(n, first):
                    add(n - 1, 1 - k)
                if first == 0 and known(n, end - 2):
                    head_matrices_dve(dve)
                if known(n, NT - 2) or known(n, NT - 1):
                    for m in range(NT - 8, NT - 4) if n == NT - 2 else range(NT - 4, NT - 1):
                        finish(m, m % 2, n)
                elif first > 0 and not known_below(n, first + 2):
                    for c in range(2):
                        finish(2 * (n - first - 2) + c, c, n)

            def finish(m, k, attended):
                dve.wait_ge(x_att0, attended)
                combine(dve, 0, m, k)
                dve.wait_ge(L[0]["gat_used"], m + 1)
                dve.bn_stats(stats[1][:, bass.ds(m, 1), :], X[:, bass.ds(m, 1), :]).then_inc(L[1]["stats"], 1)
            maxima(first, 0)
            tile_loop(dve, first, end, step)
            add(end - 1, 1)
            if first > 0:
                finish(NT - 1, 1, NT)

        def moe_dve(dve, l):
            expert = Experts(dve, l)
            s = L[l]
            pre, hid, hidT = experts[l]
            FW = F0 if l == 0 else F1
            dve.wait_ge(loaded_moe[l], 16 * 4)

            def biased_product(j, k):
                if l == 1:
                    dve.wait_ge(s["pre_ready"], j + 1)
                    if not known_below(j, 2):
                        dve.wait_ge(s["hid_t"], j - 1)
                    dve.tensor_tensor(hid[:, k, 0:FW], pre[:, k, 0:FW], PS[:, 2 * k + 1, 0:FW],
                                      ALU.mult).then_inc(s["hid_ready"], 1)
                    return
                e = expert(j, 1)
                dve.wait_ge(s["up_done"], j + 1)
                if not known_below(j, 1):
                    dve.wait_ge(s["pre_ready"], j)
                dve.tensor_tensor(both[:], PS[:, 2 * k:2 * k + 2, 0:FW],
                                  b_in[:, bass.ds(e, 1), :].rearrange("p o (c f) -> p (o c) f", c=2),
                                  ALU.add).then_inc(s["both_ready"], 1)
                dve.wait_ge(s["both_ready"], j + 1)
                if not known_below(j, 2):
                    dve.wait_ge(s["hid_ready"], j - 1)
                dve.tensor_tensor(pre[:, k, :], both[:, 0, :], both[:, 1, :], ALU.mult).then_inc(s["pre_ready"], 1)

            def add_bias(j, k):
                if l == 1:
                    dve.wait_ge(s["dn_done"], j + 1)
                    if not known_below(j, 2):
                        dve.wait_ge(s["ye_stored"][k], 16 * turn_of(j))
                    dve.tensor_copy(ye[:, k, :], PS[:, 6 + k, 0:D]).then_inc(s["ye_ready"], 1)
                    return
                e = expert(j, -1)
                dve.wait_ge(s["dn_done"], j + 1)
                if not known_below(j, 2):
                    dve.wait_ge(s["ye_stored"][k], 16 * turn_of(j))
                dve.tensor_tensor(ye[:, k, :].unsqueeze(1), PS[:, 6 + k, 0:D].unsqueeze(1), b_dn[:, bass.ds(e, 1), :],
                                  ALU.add).then_inc(s["ye_ready"], 1)

            def step(j, k):
                if not (isinstance(j, int) and j == NTILE - 1):
                    biased_product(j + 1, 1 - k)
                if not known_below(j, 1):
                    add_bias(j - 1, 1 - k)
            biased_product(0, 0)
            tile_loop(dve, 0, NTILE, step, before=expert.before if l == 0 else None)
            add_bias(NTILE - 1, 1)

        def combine(dve, l, m, k):
            s = L[l]
            one = bass.ds(m, 1)
            dve.wait_ge(s["gathered"][k], 32 * (turn_of(m) + 1))
            dve.scalar_tensor_tensor(out=X[:, one, :], in0=gat[:, 2 * k:2 * k + 1, :], scalar=w_top[l][0][:, one],
                                     in1=X[:, one, :], op0=ALU.mult, op1=ALU.add).then_inc(s["half_sum"], 1)
            dve.wait_ge(s["half_sum"], m + 1)
            dve.scalar_tensor_tensor(out=X[:, one, :], in0=gat[:, 2 * k + 1:2 * k + 2, :], scalar=w_top[l][1][:, one],
                                     in1=X[:, one, :], op0=ALU.mult, op1=ALU.add).then_inc(s["gat_used"], 1)

        (x_att1, aux_full, aux_free, lt_hi_done, lt_ready, head_fixed, v_ready, score_done, exp1_done, pv1_done,
         oT_ready, max_ready, shiftT_ready, shift_loaded0, shift_loaded1, y_done, y_ready, y_t, yT_ready, o_done,
         chain1, hm_ready, const1, passed_pe, passed_dve, passed_sp) = (
            S(n) for n in ("x_att1 aux_full aux_free lt_hi_done lt_ready head_fixed v_ready score_done exp1_done "
                           "pv1_done oT_ready max_ready shiftT_ready shift_loaded0 shift_loaded1 y_done y_ready y_t "
                           "yT_ready o_done chain1 hm_ready const1 passed_pe passed_dve passed_sp").split())
        shift_loaded = [shift_loaded0, shift_loaded1]
        BLOCKS = [(i, c, i if 512 * (c + 1) >= (i + 1) * P else TB - 4 + i, h)
                  for i in range(TB) for c in range(1 + i // 4) for h in range(HG)]
        PIECES = [(lo, hi, pair) for lo, hi in ((0, 512), (512, 768), (768, 1024)) for pair in range(2)]
        CHUNKS = []
        for j in range(TB):
            first = SEQ if TB - j <= 4 else (TB - j + 1) // 2 * P
            for h in range(HG):
                CHUNKS += [(j, h, lo, min(first, (TB - j) * P - lo)) for lo in range(0, (TB - j) * P, first)]
        NCHUNK = len(CHUNKS)
        SLOT_END = [max(e for e, chunk in enumerate(CHUNKS) if chunk[0] == j) + 1 for j in range(TB)]

        def order_of_step():
            blocks_per_slot = [7, 12, 11, 10, 8]
            order, e, n = [], 0, 0
            for j in range(TB):
                mine = [x for x in CHUNKS if x[0] == j]
                todo = blocks_per_slot[j] if j < len(blocks_per_slot) else 0
                for m, (_, h, lo, _) in enumerate(mine):
                    order.append(("chunk", e))
                    e += 1
                    last_of_head = m + 1 == len(mine) or mine[m + 1][1] != h
                    if j == 0:
                        if h == 0 and lo == 0:
                            order.append(("latent", 1, 4))
                        if h == 0 and lo > 0:
                            order.append(("latent", 1, 5))
                        if h == 1 and last_of_head:
                            order.append(("values", -1, TB - 1, 1))
                        if h == 3 and lo == 0:
                            order += [("output", 0), ("output", 1)]
                    share = todo * (m + 1) // len(mine) - todo * m // len(mine)
                    order += [("block", n + x) for x in range(share)]
                    n += share
                    if j > 0 and last_of_head:
                        if h == 1 and j - 1 < 4:
                            order.append(("values", 0, j - 1, 0))
                        if h == (3 if j - 1 < 4 else 2):
                            order.append(("values", 0, j - 1, 1))
                    for where, what in (((4, 3), ("latent", 2, 0)), ((5, 1), ("shift", 1)), ((5, 3), ("latent", 2, 1)),
                                        ((6, 1), ("latent", 2, 2)), ((6, 3), ("latent", 2, 3))):
                        if where == (j, h) and last_of_head:
                            order.append(what)
                if j == 0:
                    order.append(("experts", 0))
            assert n == len(BLOCKS)
            return order
        ORDER = order_of_step()

        def has(q, lead):
            return not (isinstance(q, int) and q + lead > NG - 1)

        def uses_of(q):
            return [x for x in ORDER if x[0] == "block" and has(q, 1) or x[0] == "shift" and has(q, 1)
                    or x[0] == "latent" and has(q, x[1]) or x[0] == "output" and not known(q, 0)]
        BEFORE = len(PIECES) + 4 + len(BLOCKS) + 1
        STEP_USES = len(BLOCKS) + 1 + len(PIECES) + 2
        TOTAL_USES = BEFORE + STEP_USES * NG - len(BLOCKS) - 1 - 4 - len(PIECES)
        assert STEP_USES % 3 == 0 and NCHUNK % 3 == 0

        def uses_before(q):
            if known(q, 0):
                return BEFORE
            return BEFORE - 2 + STEP_USES * q - (4 if known(q, NG - 1) else 0)

        def use_mod(q, k, n, m):
            return ((uses_before(q) if isinstance(q, int) else BEFORE - 2 + STEP_USES * k) + n) % m

        def items(q, k):
            uses, n = uses_of(q), 0
            for item in ORDER:
                u = uses_before(q) + n
                if n < len(uses) and item == uses[n]:
                    yield item[0], item[1], item, u, 3 + use_mod(q, k, n, 3), use_mod(q, k, n, 2)
                    n += 1
                elif item[0] in ("chunk", "values", "experts"):
                    yield item[0], item[1], item, u, None, None

        def group_of(q):
            if isinstance(q, int):
                return q // (HEADS // HG), q % (HEADS // HG)
            b = (q >> 2).with_bounds(min_val=0, max_val=BATCH - 1)
            return b, (q & 3).with_bounds(min_val=0, max_val=HEADS // HG - 1)

        def head_matrices_dve(dve):
            c = [0]

            def link(ins):
                c[0] += 1
                ins.then_inc(hm_ready, 1)
                dve.wait_ge(hm_ready, c[0])
            dve.wait_ge(loaded_w1, 16 * W1_LOADS)
            dve.memset(heads[RANK:P, :, :], 0.0)
            link(dve.tensor_reduce(head_mean[:], heads[0:RANK, :, :].rearrange("p h s -> p s h"), AX.X, ALU.add))
            link(dve.tensor_tensor(core[:, 0, :], core[:, 0, :], core[:, 1, :], ALU.add))
            link(dve.tensor_scalar(core[:, 0, :], core[:, 0, :], 0.5 / HEADS, None, ALU.mult))
            link(dve.scalar_tensor_tensor(out=core[:, 0, :], in0=head_mean[:], scalar=-1.0 / HEADS,
                                          in1=core[:, 0, :], op0=ALU.mult, op1=ALU.add))
            link(dve.tensor_tensor(heads[0:RANK, :, :], heads[0:RANK, :, :],
                                   core[:, 0, :].unsqueeze(1).to_broadcast([RANK, HEADS, RANK]), ALU.add))

        def prepare1_pool(pool):
            pool.wait_ge(x_att0, NT)
            pool.wait_ge(s_done, NT)
            pool.memset(lat_lo[RANK:RANK + 2, :], 1.0).then_inc(const1, 1)
            pool.wait_ge(const1, 1)
            pool.memset(lat_lo[RANK:RANK + 1, :], SHIFT).then_inc(const1, 1)
            pool.wait_ge(const1, 2)
            pool.memset(v9[:, :, :, HD:HD + 1], 1.0).then_inc(const1, 1)
            pool.wait_ge(const1, 3)
            pool.memset(v_rows, 0.0).then_inc(const1, 1)

        def stand_alone(eng, counter):
            eng.sem_inc(counter, 1)

        def attention1_pe(pe):
            pe.wait_ge(hm_ready, 5)
            pe.wait_ge(const1, 4)
            pe.wait_ge(L[1]["ev_act"], NT)
            pe.wait_ge(L[1]["ev_dve"], NT)

            def fill(u, products):
                if not known_below(u, 3):
                    pe.wait_ge(aux_free, u - 2)
                products().then_inc(aux_full, 1)

            def latent_heads(q, k, u, bank, piece):
                b, _ = group_of(q)
                lo, hi, pair = PIECES[piece]
                if piece in (0, 4):
                    pe.wait_ge(head_fixed, q + 1)
                fill(u, lambda: pe.matmul(PS[:, bank, 0:hi - lo], heads_fixed[:, k, pair * P:(pair + 1) * P],
                                          lat[:, bass.ds(b * SEQ + lo, hi - lo)], start=True, stop=True))

            def block(q, k, u, bank, n):
                b, _ = group_of(q)
                i, c, _, h = BLOCKS[n]
                width = min(512, (i + 1) * P - 512 * c)
                fill(u, lambda: pe.matmul(PS[:, bank, 0:width], lt_hl[:, k, h, i * P:(i + 1) * P],
                                          lat_hi[:, bass.ds(b * SEQ + c * 512, width)], start=True, stop=True))

            def turn_shift(q, k, u, bank):
                pe.wait_ge(max_ready, 3 * (q + 1))
                fill(u, lambda: stand_alone(pe, passed_pe) or pe.transpose(PS[0:2 * HG * TB, bank, 0:P // 2].bitcast(F16),
                                             shift[:, k, :, :, :].rearrange("p r h i -> p (r h i)"), identh[:]))

            def scores(q, k, e):
                b, _ = group_of(q)
                j, h, lo, width = CHUNKS[e]
                n = q * NCHUNK + e
                if e == 0:
                    pe.wait_ge(shift_loaded[k], 16 * (turn_of(q) + 1))
                if not known_below(n, 3):
                    pe.wait_ge(exp1_done, n - 2)
                keys = bass.ds(b * SEQ + j * P, P)
                where = PS[:, n % 3 if isinstance(n, int) else e % 3, 0:width]
                queries = slice(j * P + lo, j * P + lo + width)
                pe.matmul(where, lat_hi[:, keys], lt_hl[:, k, h, queries], start=True, stop=False)
                mm = pe.matmul(where, lat_lo[0:RANK + 2, keys], lt_hm[0:RANK + 2, k, h, queries],
                               start=False, stop=(lo > 0))
                if lo == 0:
                    mm = pe.matmul(where[:, 0:P], ident16[:], late16[:], start=False, stop=True)
                mm.then_inc(score_done, 1)

            def values(q, k, j, c):
                if c == 0 or j >= 4:
                    pe.wait_ge(exp1_done, q * NCHUNK + SLOT_END[j])
                if j == 0 and c == 0:
                    pe.wait_ge(v_ready, q + 1)
                    if known(q, 0):
                        pe.wait_ge(L[1]["routed"], 1)
                    if not known_below(q, 1):
                        pe.wait_ge(oT_ready, q)
                lo, hi = max(j * P, 512 * c), 512 * (c + 1)
                for h in range(HG):
                    v0 = (j * HG + h) * (HD + 1)
                    mm = pe.matmul(PS[32 * h:32 * h + 32, 6 + c, lo - 512 * c:hi - 512 * c],
                                   v_rows[:, k, v0:v0 + 32], prob1[j % 2][:, h, lo - j * P:hi - j * P],
                                   start=(j == 0), stop=(j == (TB - 1 if c else 3)), tile_position=(0, 32 * h))
                if c == 1:
                    mm.then_inc(pv1_done, 1)

            def turn_out(q, u, bank, o):
                pe.wait_ge(oT_ready, q + 1)

                def four():
                    for i in range(4):
                        mm = pe.transpose(PS[:, bank, i * P:(i + 1) * P],
                                          oT[:, (4 * o + i) * P:(4 * o + i + 1) * P], ident[:])
                    return mm
                fill(u, four)

            def step(q, k):
                for what, x, item, u, bank, _ in items(q, k):
                    if what == "chunk":
                        scores(q, k, x)
                    if what == "values" and (x == 0 or not known(q, 0)):
                        values(q + x, (k + x) % 2, item[2], item[3])
                    if what == "experts" and known(q, 1):
                        pe.wait_ge(aux_free, u)
                        pe.wait_ge(exp1_done, NCHUNK + SLOT_END[0])
                        moe_pe(pe, 1)
                        pe.wait_ge(L[1]["ye_ready"], NTILE)
                    if what == "block":
                        block(q + 1, 1 - k, u, bank, x)
                    if what == "shift":
                        turn_shift(q + 1, 1 - k, u, bank)
                    if what == "latent":
                        latent_heads(q + x, (k + x) % 2, u, bank, item[2])
                    if what == "output":
                        turn_out(q - 1, u, bank, x)

            for u in range(10):
                latent_heads(u // 6, u // 6, u, 3 + u % 3, u % 6)
            for n in range(len(BLOCKS)):
                block(0, 0, 10 + n, 3 + (10 + n) % 3, n)
            turn_shift(0, 0, BEFORE - 1, 3 + (BEFORE - 1) % 3)
            tile_loop(pe, 0, NG, step, unroll=2)
            values(NG - 1, 1, TB - 1, 1)
            for o in range(2):
                u = uses_before(NG - 1) + len(uses_of(NG - 1)) + o
                turn_out(NG - 1, u, 3 + u % 3, o)
            project_out_pe(pe)

        def project_out_pe(pe):
            pe.wait_ge(exp1_done, NG * NCHUNK)
            pe.wait_ge(aux_free, TOTAL_USES)

            def turn(n, k):
                pe.wait_ge(y_ready, n + 1)
                if not known_below(n, 2):
                    pe.wait_ge(yT_ready, n - 1)
                for i in range(4):
                    mm = pe.transpose(PS[:, k, i * P:(i + 1) * P], y_fixed[:, k, i, :], ident[:])
                mm.then_inc(y_t, 1)

            def product(n, k):
                pe.wait_ge(yT_ready, n + 1)
                if not known_below(n, 2):
                    pe.wait_ge(y_done, n - 1)
                for i in range(4):
                    mm = pe.matmul(PS[:, 2 + k, i * P:(i + 1) * P], yT[:, k, i, :], ow[:], start=True, stop=True)
                mm.then_inc(o_done, 1)

            def step(n, k):
                if not known(n, NT // 4 - 1):
                    turn(n + 1, 1 - k)
                product(n, k)
            turn(0, 0)
            tile_loop(pe, 0, NT // 4, step, unroll=2)

        def attention1_act(act):
            act.wait_ge(hm_ready, 5)
            act.wait_ge(const1, 4)
            act.wait_ge(L[1]["ev_dve"], NT)

            def fix_heads(q, k):
                _, g = group_of(q)
                if not known_below(q, 2):
                    act.wait_ge(lt_ready, q - 1)
                act.activation(heads_fixed[:, k, :].rearrange("p (h s) -> p h s", h=HG),
                               heads[:, bass.ds(g * HG, HG), :], ACT.Copy).then_inc(head_fixed, 1)

            def fix_values(q, k):
                b, g = group_of(q)
                if not known_below(q, 2):
                    act.wait_ge(pv1_done, TB * (q - 1))
                act.activation(v_fixed[k], v9[:, bass.ds(b * TB, TB), bass.ds(g * HG, HG), :],
                               ACT.Copy).then_inc(v_ready, 1)

            def latent_hi(q, k, u, bank, piece):
                lo, hi, pair = PIECES[piece]
                act.wait_ge(aux_full, u + 1)
                for half in range(2):
                    rows = slice(64 * half, 64 * half + 64)
                    ins = act.activation(lt_hl[rows, k, 2 * pair + half, lo:hi], PS[rows, bank, 0:hi - lo], ACT.Copy)
                ins.then_inc(lt_hi_done, 1)

            def exps(q, k, e):
                j, h, lo, width = CHUNKS[e]
                act.wait_ge(score_done, q * NCHUNK + e + 1)
                if h == 0 and lo == 0 and not (isinstance(q, int) and q * TB + j < 2):
                    act.wait_ge(pv1_done, q * TB + j - 1)
                act.activation(prob1[j % 2][:, h, lo:lo + width], PS[:, e % 3, 0:width],
                               ACT.Exp, scale=RANK ** -0.5).then_inc(exp1_done, 1)

            def copy_oT(q):
                act.wait_ge(pv1_done, TB * (q + 1))
                if not known_below(q, 1):
                    act.wait_ge(aux_full, uses_before(q) + uses_of(q).index(("output", 1)) + 1)
                act.activation(oT, PS[:, 6:8, :].rearrange("p a b -> p (a b)"), ACT.Copy).then_inc(oT_ready, 1)

            def step(q, k):
                for what, x, item, u, bank, _ in items(q, k):
                    if what == "chunk":
                        exps(q, k, x)
                        if x == SLOT_END[1] - 1 and has(q, 2):
                            fix_heads(q + 2, k)
                        if x == SLOT_END[0] - 1 and has(q, 1) and not known(q, 0):
                            fix_values(q + 1, 1 - k)
                    if what == "values" and x == -1 and not known(q, 0):
                        copy_oT(q - 1)
                    if what == "experts" and known(q, 1):
                        moe_act(act, 1)
                    if what == "latent":
                        latent_hi(q + x, (k + x) % 2, u, bank, item[2])

            for q in range(2):
                fix_heads(q, q)
                fix_values(q, q)
            for u in range(10):
                latent_hi(u // 6, u // 6, u, 3 + u % 3, u % 6)
            tile_loop(act, 0, NG, step, unroll=2)
            copy_oT(NG - 1)
            project_out_act(act)

        def project_out_act(act):
            act.wait_ge(aux_free, TOTAL_USES)

            def fix(n, k):
                if not known_below(n, 2):
                    act.wait_ge(y_t, n - 1)
                act.activation(y_fixed[:, k, :, :], y1[:, bass.ds(4 * n, 4), :], ACT.Copy).then_inc(y_ready, 1)

            def copy_yT(n, k):
                act.wait_ge(y_t, n + 1)
                if not known_below(n, 2):
                    act.wait_ge(o_done, n - 1)
                act.activation(yT[:, k, :, :].rearrange("p i c -> p (i c)"), PS[:, k, :], ACT.Copy).then_inc(yT_ready, 1)

            def step(n, k):
                if not (isinstance(n, int) and n >= NT // 4 - 2):
                    fix(n + 2, k)
                copy_yT(n, k)
            fix(0, 0)
            fix(1, 1)
            tile_loop(act, 0, NT // 4, step, unroll=2)

        def attention1_dve(dve):
            def latent_lo(q, k, u, bank, piece):
                lo, hi, pair = PIECES[piece]
                dve.wait_ge(lt_hi_done, len(PIECES) * q + piece + 1)
                for half in range(2):
                    h = 2 * pair + half
                    rows, others = slice(64 * half, 64 * half + 64), slice(64 - 64 * half, 128 - 64 * half)
                    ins = dve.tensor_tensor(lt_hl[others, k, h, lo:hi], PS[rows, bank, 0:hi - lo],
                                            lt_hl[rows, k, h, lo:hi], ALU.subtract)
                ins.then_inc(aux_free, 1)
                if piece == len(PIECES) - 1:
                    for h in range(HG):
                        rows = slice(64 * (h % 2), 64 * (h % 2) + 64)
                        ins = dve.tensor_copy(lt_hm[0:RANK, k, h, :], lt_hl[rows, k, h, :])
                    ins.then_inc(lt_ready, 1)

            def block(q, k, u, bank, spare, n):
                i, c, column, h = BLOCKS[n]
                width = min(512, (i + 1) * P - 512 * c)
                dve.wait_ge(aux_full, u + 1)
                accum = maxima1[:, k, h, column:column + 1]
                if column < TB:
                    dve.wait_ge(aux_free, u - 1)
                    stand_alone(dve, passed_dve)
                    ins = dve.tensor_tensor_reduce(spare[:, 0:width], PS[:, bank, 0:width], late[:, 512 - width:512],
                                                   1.0, -3e38, ALU.add, ALU.max, accum)
                else:
                    ins = dve.tensor_reduce(accum, PS[:, bank, 0:width], AX.X, ALU.max)
                ins.then_inc(aux_free, 1)

            def prepare_shift(q, k, uses):
                dve.wait_ge(aux_free, uses)
                m = maxima1[:, k, :, :]
                dve.tensor_tensor(m[:, :, 4:8], m[:, :, 4:8], m[:, :, 8:12], ALU.max).then_inc(max_ready, 1)
                dve.wait_ge(max_ready, 3 * q + 1)
                dve.tensor_scalar(shift[:, k, 0, :, :], m[:, :, 0:TB], -1.0 / SHIFT, None,
                                  ALU.mult).then_inc(max_ready, 1)
                dve.wait_ge(max_ready, 3 * q + 2)
                dve.scalar_tensor_tensor(out=shift[:, k, 1, :, :], in0=shift[:, k, 0, :, :], scalar=-SHIFT,
                                         in1=m[:, :, 0:TB], op0=ALU.mult, op1=ALU.subtract).then_inc(max_ready, 1)

            def copy_shiftT(q, k, u, bank):
                dve.wait_ge(aux_full, u + 1)
                if not known_below(q, 2):
                    dve.wait_ge(shift_loaded[k], 16 * turn_of(q))
                dve.tensor_copy(shiftT[:, k, :], PS[0:2 * HG * TB, bank, 0:P // 2].bitcast(F16))\
                   .then_inc(aux_free, 1)

            def outputs(q, u, bank, o):
                b, g = group_of(q)
                if known(q, 0):
                    dve.wait_ge(L[1]["scattered"], 16 * 2 * NT)
                dve.wait_ge(aux_full, u + 1)
                o4 = PS[:, bank, :].rearrange("p (i h c) -> p i h c", i=4, h=HG)
                dve.reciprocal(rden1[:, o, :, :], o4[:, :, :, HD]).then_inc(chain1, 1)
                dve.wait_ge(chain1, 2 * q + o + 1)
                ins = dve.tensor_tensor(
                    y1[:, bass.ds(b * TB + 4 * o, 4), bass.ds(g * HG * HD, HG * HD)]
                    .rearrange("p i (h c) -> p i h c", h=HG), o4[:, :, :, 0:HD],
                    rden1[:, o, :, :].unsqueeze(3).to_broadcast([P, 4, HG, HD]), ALU.mult)
                ins.then_inc(aux_free, 1)

            def step(q, k):
                spare = junk[0 if isinstance(q, int) and q < 2 else 1]
                for what, x, item, u, bank, odd in items(q, k):
                    if what == "block":
                        block(q + 1, 1 - k, u, bank, spare[odd], x)
                        if x == len(BLOCKS) - 1:
                            prepare_shift(q + 1, 1 - k, u + 1)
                    if what == "shift":
                        copy_shiftT(q + 1, 1 - k, u, bank)
                    if what == "latent":
                        latent_lo(q + x, (k + x) % 2, u, bank, item[2])
                    if what == "output":
                        outputs(q - 1, u, bank, x)
                    if what == "experts" and known(q, 1):
                        moe_dve(dve, 1)
                        spare = junk[1]
                if isinstance(q, int) and q >= NG - 2:
                    share = (NT - 2 * (NG - 4)) // 2
                    for m in range(NT - share * (NG - q), NT - share * (NG - 1 - q)):
                        combine(dve, 1, m, m % 2)
                elif not isinstance(q, int):
                    for c in range(2):
                        combine(dve, 1, 2 * (q - 2) + c, c)

            for u in range(10):
                latent_lo(u // 6, u // 6, u, 3 + u % 3, u % 6)
            for n in range(len(BLOCKS)):
                block(0, 0, 10 + n, 3 + (10 + n) % 3, junk[0][n % 2], n)
            prepare_shift(0, 0, 10 + len(BLOCKS))
            copy_shiftT(0, 0, BEFORE - 1, 3 + (BEFORE - 1) % 3)
            tile_loop(dve, 0, NG, step, unroll=2)
            for o in range(2):
                u = uses_before(NG - 1) + len(uses_of(NG - 1)) + o
                outputs(NG - 1, u, 3 + u % 3, o)
            project_out_dve(dve)

        def project_out_dve(dve):
            dve.wait_ge(L[1]["gat_used"], NT)

            def step(n, k):
                dve.wait_ge(o_done, n + 1)
                if not known_below(n, 2):
                    dve.wait_ge(x_att1, n - 1)
                dve.tensor_tensor(o_tmp[:, k, :, :], PS[:, 2 + k, :].rearrange("p (i c) -> p i c", i=4),
                                  ob[:].unsqueeze(1).to_broadcast([P, 4, D]), ALU.add).then_inc(y_done, 1)
                dve.wait_ge(y_done, n + 1)
                dve.tensor_tensor(X[:, bass.ds(4 * n, 4), :], X[:, bass.ds(4 * n, 4), :], o_tmp[:, k, :, :],
                                  ALU.add).then_inc(x_att1, 1)
            tile_loop(dve, 0, NT // 4, step, unroll=2)

        def attention1_sp(sp):
            def step(q, k):
                sp.wait_ge(aux_free, BEFORE if known(q, 0) else uses_before(q - 1) + uses_of(q - 1).index(("shift", 1)) + 1)
                stand_alone(sp, passed_sp)
                sp.wait_ge(lt_ready, q + 1)
                sp.dma_start(lt_hm[RANK:RANK + 2, k, :, :].rearrange("r h t -> r (h t)")
                             .rearrange("r (m t) -> r m t", t=P), shiftT[:, k, :]).then_inc(shift_loaded[k], 16)
                if known(q, 1):
                    moe_sp(sp, 1)
            tile_loop(sp, 0, NG, step, unroll=2)

        block = ctx.enter_context(nc.Block())

        @block.sync
        def _(sp):
            sp.dma_start(ident[:], a["ident"]).then_inc(loaded_wq, 16)
            sp.dma_start(wq[:], a["wqkvg"]).then_inc(loaded_wq, 16)
            for b in range(BATCH):
                sp.dma_start(X[:, b * TB:(b + 1) * TB, :], a["x"][b * SEQ:(b + 1) * SEQ, :]
                             .rearrange("(n p) d -> p n d", p=P)).then_inc(loaded_x[b], 16)
            sp.dma_start(gb[:], a["gate_b"].partition_broadcast(P)).then_inc(loaded_w0, 16)
            sp.dma_start(before[:], a["before"]).then_inc(loaded_w0, 16)
            sp.dma_start(iota_e[:], a["iota_e"].partition_broadcast(P)).then_inc(loaded_w0, 16)
            sp.dma_start(steps128[:], a["steps128"].partition_broadcast(P)).then_inc(loaded_w0, 16)
            sp.dma_start(tile_no[:], a["tile_no"].partition_broadcast(P)).then_inc(loaded_w0, 16)
            for dst, name in ((wv1, "wv1"), (basis, "basis"), (ow, "ow"), (core, "core"), (late, "late"),
                              (late16, "late16"), (ident16, "ident16"), (identh, "identh")):
                sp.dma_start(dst[:], a[name]).then_inc(loaded_w1, 16)
            sp.dma_start(heads[0:RANK, :, :], a["heads"]).then_inc(loaded_w1, 16)
            for dst, name in ((vb, "v_b"), (ob, "o_b")):
                sp.dma_start(dst[:], a[name].partition_broadcast(P)).then_inc(loaded_w1, 16)
            sp.dma_start(w_in[:], a["w_in0"]).then_inc(loaded_moe[0], 16)
            sp.dma_start(b_in[:], a["b_in0"].partition_broadcast(P)).then_inc(loaded_moe[0], 16)
            sp.dma_start(b_dn[:], a["b_dn0"].partition_broadcast(P)).then_inc(loaded_moe[0], 16)
            sp.dma_start(w_dn[0:102, :, :, :], a["w_dn0"]).then_inc(loaded_moe[0], 16)
            moe_sp(sp, 0)
            sp.wait_ge(L[0]["ye_ready"], NTILE)
            sp.dma_start(w_in[:, :, 0:2 * F1], a["w_in1"]).then_inc(loaded_moe[1], 16)
            first = 0
            for c, m in enumerate(CH1):
                sp.dma_start(w_dn[0:m, :, c, :], a["w_dn1"][:, first:first + m, :].rearrange("e f d -> f e d"))\
                    .then_inc(loaded_moe[1], 16)
                first += m
            attention1_sp(sp)
            for b in range(BATCH):
                sp.wait_ge(x_att1, TB // 4 * (b + 1))
                sp.dma_start(out[b * SEQ:(b + 1) * SEQ, :].rearrange("(n p) d -> p n d", p=P),
                             X[:, b * TB:(b + 1) * TB, :]).then_inc(S("stored"), 16)
            sp.wait_ge(S("stored"), 16 * BATCH)

        @block.gpsimd
        def _(pool):
            nc.gpsimd.memset(zeros, 0.0).then_inc(S("zero_tile"), 1)
            pool.wait_ge(S("zero_tile"), 1)
            pool.wait_ge(loaded_wq, 16 * 2)
            for b in range(BATCH):
                pool.wait_ge(loaded_x[b], 16)
            zero_slots(pool, 0)
            zero_slots(pool, 1)
            route_pool(pool, 0)
            prepare1_pool(pool)
            route_pool(pool, 1)

        @block.tensor
        def _(pe):
            pe.wait_ge(loaded_wq, 16 * 2)
            proj_pe(pe, 0)
            route_pe(pe, 0)
            attention0_pe(pe, 0, NT // 2)
            moe_pe(pe, 0)
            attention0_pe(pe, NT // 2, NT)
            pe.wait_ge(loaded_w1, 16 * W1_LOADS)
            pe.wait_ge(x_att0, NT)
            proj_pe(pe, 1)
            route_pe(pe, 1)
            attention1_pe(pe)

        @block.scalar
        def _(act):
            norm_act(act, 0)
            proj_act(act, 0)
            route_act(act, 0)
            attention0_act(act, 0, NT // 2)
            moe_act(act, 0)
            attention0_act(act, NT // 2, NT)
            norm_act(act, 1)
            proj_act(act, 1)
            route_act(act, 1)
            attention1_act(act)

        @block.vector
        def _(dve):
            dve.memset(ones[:], 1.0)
            for n in range(NT):
                if n % TB == 0:
                    dve.wait_ge(loaded_x[n // TB], 16)
                stats_dve(dve, 0, n)
            norm_dve(dve, 0)
            proj_dve(dve, 0)
            route_dve(dve, 0)
            dve.wait_ge(L[0]["xn_ready"], NT)
            attention0_dve(dve, 0, NT // 2)
            moe_dve(dve, 0)
            attention0_dve(dve, NT // 2, NT)
            norm_dve(dve, 1)
            proj_dve(dve, 1)
            route_dve(dve, 1)
            attention1_dve(dve)


INPUTS = ("L0_attn_x L0_attn_W_qkv L0_ffn_gate_w L0_ffn_gate_b L0_ffn_up_w L0_ffn_up_b L0_ffn_gp_w L0_ffn_gp_b "
          "L0_ffn_down_w L0_ffn_down_b L1_attn_basis_w L1_attn_core L1_attn_head_residual L1_attn_v_w L1_attn_v_b "
          "L1_attn_o_w L1_attn_o_b L1_ffn_Wg L1_ffn_W1 L1_ffn_W2 L1_ffn_W3").split()


def laid_out(i):
    f32 = np.float32
    a = {"x": i["L0_attn_x"].reshape(BATCH * SEQ, D)}
    a["wqkvg"] = np.concatenate([i["L0_attn_W_qkv"], i["L0_ffn_gate_w"]], 0).T
    a["gate_b"] = i["L0_ffn_gate_b"]
    a["w_in0"] = np.concatenate([i["L0_ffn_gp_w"], i["L0_ffn_up_w"]], 1).transpose(2, 0, 1)
    a["b_in0"] = np.concatenate([i["L0_ffn_gp_b"], i["L0_ffn_up_b"]], 1)
    a["w_dn0"] = i["L0_ffn_down_w"].transpose(0, 2, 1).reshape(NE, 4, 102, D).transpose(2, 0, 1, 3)
    a["b_dn0"] = i["L0_ffn_down_b"]
    a["w_in1"] = np.concatenate([i["L1_ffn_W1"], i["L1_ffn_W3"]], 1).transpose(2, 0, 1)
    a["w_dn1"] = i["L1_ffn_W2"].transpose(0, 2, 1)
    a["wv1"] = np.concatenate([i["L1_attn_v_w"], i["L1_ffn_Wg"]], 0).T
    a["basis"] = np.concatenate([i["L1_attn_basis_w"]] * 2, 0).T
    a["ow"] = i["L1_attn_o_w"].T
    a["v_b"], a["o_b"] = i["L1_attn_v_b"], i["L1_attn_o_b"]
    a["core"] = np.stack([i["L1_attn_core"], i["L1_attn_core"].T], 1)
    a["heads"] = i["L1_attn_head_residual"].transpose(1, 0, 2)
    row, col = np.arange(P)[:, None], np.arange(P)[None]
    a["late"] = np.concatenate([np.zeros((P, 3 * P), f32), np.where(col > row, f32(-BIG), f32(0))], 1).astype(mybir.dt.np(BF16))
    a["late16"] = np.where(row > col, f32(-BIG), f32(0)).astype(mybir.dt.np(BF16))
    a["ident16"] = np.eye(P).astype(mybir.dt.np(BF16))
    a["identh"] = np.eye(P, dtype=np.float16)
    a["ident"] = np.eye(P, dtype=f32)
    a["before"] = np.triu(np.ones((P, P), f32), 1)
    a["iota_e"] = np.arange(NE, dtype=f32) - NE
    a["steps128"] = np.arange(NT, dtype=f32) * P
    a["tile_no"] = np.arange(NTILE, dtype=f32)
    return {"in_" + n: np.ascontiguousarray(v) for n, v in a.items()}


def kernel(**inputs):
    import concourse.bacc as _bacc
    from concourse.bass_utils import run_bass_kernel_spmd as _run

    arrays = laid_out({n: np.asarray(inputs[n]) for n in INPUTS})
    nc = _bacc.Bacc("TRN2", target_bir_lowering=False, num_devices=1, dynamic_dma_scratch_size=DMA_RING)
    ins = {n[3:]: nc.dram_tensor(n, v.shape, mybir.dt.from_np(v.dtype), kind="ExternalInput").ap()
           for n, v in arrays.items()}
    out = nc.dram_tensor("out", (BATCH * SEQ, D), F32, kind="ExternalOutput").ap()
    two_layers(nc, ins, out)
    r = _run(nc, [arrays], core_ids=[0])
    return r.results[0]["out"].reshape(BATCH, SEQ, D)
```

```python
from contextlib import ExitStack

import numpy as np

import concourse.bass as bass
from concourse import mybir

F32 = mybir.dt.float32
F16 = mybir.dt.float16
BF16 = mybir.dt.bfloat16
I32 = mybir.dt.int32
U32 = mybir.dt.uint32
ALU = mybir.AluOpType
ACT = mybir.ActivationFunctionType
AX = mybir.AxisListType

P = 128
D = 128
BATCH, SEQ = 4, 1024
NT = BATCH * SEQ // P
TB = SEQ // P
NE = 8
F0, F1 = 408, 352
CH0 = [102] * 4
CH1 = [128, 128, 96]
NTILE = (2 * BATCH * SEQ + NE * (P - 1)) // P
NTABLE = NTILE + 1
NSLOT = NTABLE * P
HEADS, RANK, HD = 16, 64, 8
HG = 4
NG = BATCH * HEADS // HG
SPLIT = 16
FIRST_SUM = 18
DMA_RING = 4096
EPS = 1e-5
BIG = 1e30
SHIFT = 16.0


def known_below(i, bound):
    return isinstance(i, int) and i < bound


def known(i, value):
    return isinstance(i, int) and i == value


def turn_of(j, buffers=2):
    return j // buffers if isinstance(j, int) else j >> (buffers.bit_length() - 1)


def sequence_of(n):
    return n // TB if isinstance(n, int) else (n >> (TB.bit_length() - 1)).with_bounds(min_val=0, max_val=BATCH - 1)


def tile_loop(eng, start, end, body, unroll=4, peel=2, tail=2, before=None, buffers=2):
    assert (end - start - peel - tail) % unroll == 0 and (start + peel) % 2 == unroll % buffers == 0
    for i in range(start, start + peel):
        body(i, i % buffers)
    with eng.Fori(0, (end - start - peel - tail) // unroll) as turn:
        for x in range(unroll):
            if before is not None:
                before(unroll * turn + start + peel, x)
            body(unroll * turn + start + peel + x, (start + peel + x) % buffers)
    for i in range(end - tail, end):
        body(i, i % buffers)


def two_layers(nc, a, out):
    with ExitStack() as ctx:
        def sb(name, shape, dt=F32):
            return ctx.enter_context(nc.sbuf_tensor(name, shape, dt))

        def dram(name, shape, dt=F32):
            return nc.dram_tensor(name, shape, dt).ap()

        def sem(name):
            return ctx.enter_context(nc.semaphore(name))

        PS = ctx.enter_context(nc.psum_tensor("PS", [P, 8, 512], F32))

        slots_in = [dram("slots_in0", [NSLOT, D]), dram("slots_in1", [NSLOT, D])]
        slots_out = [dram("slots_out0", [NTILE * P, D]), dram("slots_out1", [NTILE * P, D])]

        X = sb("X", [P, NT, D])
        XN = sb("XN", [P, NT, D])
        ident = sb("ident", [P, P])
        before = sb("before", [P, P])
        ones = sb("ones", [P, P])
        mean = sb("mean", [P, NT])
        std = sb("std", [P, NT])
        rstd = sb("rstd", [P, NT])
        xn_fixed = sb("xn_fixed", [P, 2, D])
        xnT = sb("xnT", [P, 2, P])
        iota_e = sb("iota_e", [P, NE])
        steps128 = sb("steps128", [P, NT])
        tile_no = sb("tile_no", [P, NTABLE])
        r_tile = sb("r_tile", [P, NTABLE])
        r_small = [sb("r_small%d" % i, [P, NT]) for i in range(6)]
        r_e = [sb("r_e%d" % i, [P, NE]) for i in range(4)]
        w_top = [[sb("w_top%d_%d" % (l, c), [P, NT]) for c in range(2)] for l in range(2)]
        slot = [[sb("slot%d_%d" % (l, c), [P, NT], I32) for c in range(2)] for l in range(2)]
        expert_of = [sb("expert_of%d" % l, [P, NTABLE], I32) for l in range(2)]
        weights = sb("weights", [P, NE * (2 * F0 + len(CH0) * D)])
        w_in = weights[:, 0:NE * 2 * F0].rearrange("p (e f) -> p e f", e=NE)
        w_dn = weights[:, NE * 2 * F0:].rearrange("p (e c d) -> p e c d", e=NE, c=len(CH0))
        W1 = NE * (2 * F1 + len(CH1) * D)
        parts = [weights[:].bitcast(F16)[:, i * W1:(i + 1) * W1] for i in range(2)]
        w_in_parts = [t[:, 0:NE * 2 * F1].rearrange("p (e f) -> p e f", e=NE) for t in parts]
        w_dn_parts = [t[:, NE * 2 * F1:].rearrange("p (e c d) -> p e c d", e=NE, c=len(CH1)) for t in parts]
        xe = sb("xe", [P, 4, D])
        xeT = sb("xeT", [P, 2, P])
        xeT_parts = xeT[:].rearrange("p k t -> p (k t)").bitcast(F16).rearrange("p (k i t) -> p k i t", k=2, i=2)
        ye = sb("ye", [P, 2, D])
        gat = sb("gat", [P, 4, D])
        zeros = gat[:].rearrange("p a b -> p (a b)")
        ARENA = 30400
        arena = sb("arena", [P, ARENA])
        at = [0]

        def carve(cols, dt=F32):
            view = arena[:, at[0]:at[0] + cols]
            at[0] += cols
            assert at[0] <= ARENA, at[0]
            return view if dt == F32 else view.bitcast(dt)

        kT = carve(NT * P).rearrange("p (n t) -> p n t", t=P)
        qT = carve(NT * P).rearrange("p (n t) -> p n t", t=P)
        v_lg = carve(NT * (D + NE)).rearrange("p (n c) -> p n c", c=D + NE)
        work = at[0]
        prob = carve(2 * SEQ).rearrange("p (k c) -> p k c", k=2)
        probT = carve(2 * SEQ).rearrange("p (k c) -> p k c", k=2)
        at[0] = work

        def routing_buffers():
            return ([carve(NT * NE).rearrange("p (n e) -> p n e", e=NE) for _ in range(6)],
                    carve(NTABLE * NE).rearrange("p (j e) -> p j e", e=NE))
        routing = [routing_buffers()]
        at[0] = work
        both = carve(2 * F0).rearrange("p (c f) -> p c f", c=2)

        def experts_buffers(width, chunks):
            pre = carve(2 * width).rearrange("p (k f) -> p k f", k=2)
            hid = carve(2 * width).rearrange("p (k f) -> p k f", k=2)
            return pre, hid, carve(2 * chunks * P).rearrange("p (k c t) -> p k c t", k=2, c=chunks)
        experts = [experts_buffers(F0, len(CH0))]
        at[0] = work + 4 * SEQ
        b_in = carve(NE * 2 * F0).rearrange("p (e f) -> p e f", e=NE)
        b_dn = carve(NE * D).rearrange("p (e d) -> p e d", e=NE)
        at[0] = work + 4 * SEQ
        gat0 = carve(8 * D).rearrange("p (i d) -> p i d", d=D)
        at[0] = work + 4 * SEQ + NE * (2 * F0 + D)
        heads = carve(HEADS * RANK)[0:RANK, :].rearrange("p (h s) -> p h s", h=HEADS)
        core = carve(2 * RANK)[0:RANK, :].rearrange("p (c s) -> p c s", c=2)
        head_mean = carve(RANK)[0:RANK, :]
        at[0] = 0
        y_fixed, yT, o_tmp = [carve(2 * 4 * P).rearrange("p (k i c) -> p k i c", k=2, i=4) for _ in range(3)]
        ROUNDS, SHARE = 8, W1 // 8
        at[0] = 0
        staged = [carve(SHARE) for _ in range(2)]
        at[0] = BATCH * SEQ
        lat_hi = carve(BATCH * SEQ // 2, F16)
        lat_lo = carve(BATCH * SEQ // 2, F16)
        v9 = carve(NT * HEADS * (HD + 1)).rearrange("p (n h c) -> p n h c", h=HEADS, c=HD + 1)
        lt_hl = carve(2 * HG * SEQ // 2, F16).rearrange("p (k h t) -> p k h t", k=2, h=HG)
        lt_hm = carve(2 * HG * SEQ // 2, F16).rearrange("p (k h t) -> p k h t", k=2, h=HG)
        start = at[0]
        routing.append(routing_buffers())
        at[0] = start
        stats = [rt[0].rearrange("p n e -> p (n e)")[:, 0:NT * 6].rearrange("p (n c) -> p n c", c=6)
                 for rt, _ in routing]
        prob1 = [carve(HG * w).rearrange("p (h t) -> p h t", h=HG) for w in (SEQ, SEQ - P)]
        after = at[0]
        at[0] -= HG * (SEQ - P)
        experts.append(experts_buffers(F1, len(CH1)))
        assert at[0] <= after
        at[0] = after
        hidT_parts = experts[1][2].rearrange("p k c t -> p (k c t)").bitcast(F16).rearrange(
            "p (k i c t) -> p k i c t", k=2, i=2, c=len(CH1))
        V_COLS = TB * HG * (HD + 1)
        v_rows = carve(2 * (V_COLS + 32)).rearrange("p (k c) -> p k c", k=2)
        v_fixed = [v_rows[:, k, 0:V_COLS].rearrange("p (j h c) -> p j h c", j=TB, h=HG) for k in range(2)]
        oT = carve(SEQ)
        y1 = XN

        wq = sb("wq", [P, 3 * D + NE])
        gb = sb("gb", [P, NE])
        q_fixed = sb("q_fixed", [P, 2, P])
        nmax = sb("nmax", [P, 2])
        den = sb("den", [P, 2])
        rden = sb("rden", [P, 2])

        wv1 = sb("wv1", [P, D + NE])
        basis = sb("basis", [P, P])
        vb = sb("vb", [P, D])
        ob = sb("ob", [P, D])
        ow = sb("ow", [P, D])
        lg1 = sb("lg1", [P, NT, NE])
        heads_hl = sb("heads_hl", [P, HEADS * RANK], F16)
        heads_hi = sb("heads_hi", [RANK + 2, HEADS * RANK], F16)
        late = sb("late", [P, 512], BF16)
        late16 = sb("late16", [P, P], BF16)
        ident16 = sb("ident16", [P, P], BF16)
        identh = sb("identh", [P, P], F16)
        gat_junk = gat[:].rearrange("p (k a) b -> p k (a b)", k=2)
        junk = [[gat_junk[:, k, :].bitcast(BF16) for k in range(2)],
                [t[:].rearrange("p a b -> p (a b)").bitcast(BF16) for t in (xe, xeT)]]
        maxima1 = sb("maxima1", [P, 2, HG, 12])
        shift = sb("shift", [P, 2, 2, HG, TB], F16)
        shiftT = sb("shiftT", [2 * HG * TB, 2, P], F16)
        rden1 = sb("rden1", [P, 2, 4, HG])

        block_sems = {}

        def S(name):
            if name not in block_sems:
                block_sems[name] = sem(name)
            return block_sems[name]

        loaded_x = [S("loaded_x%d" % b) for b in range(BATCH)]
        loaded_wq = S("loaded_wq")
        loaded_w0 = S("loaded_w0")
        loaded_w1 = S("loaded_w1")
        W1_LOADS = 11
        loaded_moe0 = S("loaded_moe0")
        loaded_share = [S("loaded_share0"), S("loaded_share1")]
        zeroed = [S("zeroed0"), S("zeroed1")]
        weights_hi, weights_split, xe_rest, hid_rest = (S(n) for n in "weights_hi weights_split xe_rest hid_rest".split())
        names = ("stats mv var sd rstd xs_ready xn_ready xn_t xt_ready proj ev_act ev_dve route route_act "
                 "route_pe routed scattered xe_t xeT_ready up_done pre_ready hid_ready hid_t "
                 "hidT_ready dn_done ye_ready gat_used half_sum both_ready").split()
        L = [{n: S(n + str(l)) for n in names} for l in range(2)]
        for l in range(2):
            for n in ("xe_loaded", "ye_stored", "gathered"):
                L[l][n] = [S(n + "%d_%d" % (l, k)) for k in range(4 if n == "xe_loaded" or n == "gathered" and l == 0 else 2)]
        gathered_rows = [gat0, gat]
        q_ready, s_done, max_done, exp_done, p_t, pT_ready, pv_done, rden_done, x_att0 = (
            S(n) for n in "q_ready s_done max_done exp_done p_t pT_ready pv_done rden_done x_att0".split())



        def moe_sp(sp, l):
            s = L[l]
            sp.wait_ge(s["scattered"], 16 * 2 * NT)

            def load(j, k):
                if not known_below(j, 4):
                    sp.wait_ge(s["xe_t"], j - 3)
                sp.dma_start(xe[:, k, :], slots_in[l][bass.ds(j * P, P), :]).then_inc(s["xe_loaded"][k], 16)

            def store(j, k):
                sp.wait_ge(s["ye_ready"], j + 1)
                sp.dma_start(slots_out[l][bass.ds(j * P, P), :], ye[:, k, :]).then_inc(s["ye_stored"][k], 16)

            def step(j, k):
                if not (isinstance(j, int) and j >= NTILE - 4):
                    load(j + 4, k)
                if not known_below(j, 2):
                    store(j - 2, k % 2)
            for j in range(4):
                load(j, j)
            tile_loop(sp, 0, NTILE, step, unroll=8, tail=5, buffers=4)
            for j in (NTILE - 2, NTILE - 1):
                store(j, j % 2)

        def zero_slots(pool, l):
            pool.dma_start(slots_in[l].rearrange("(p n c) d -> p n (c d)", p=P, c=4),
                           zeros.unsqueeze(1).to_broadcast([P, NTABLE // 4, 4 * D])).then_inc(zeroed[l], 16)

        def route_pool(pool, l):
            s = L[l]
            pool.wait_ge(s["routed"], 1)
            pool.wait_ge(s["xn_ready"], NT)
            pool.wait_ge(zeroed[l], 16)
            for n in range(NT):
                for c in range(2):
                    pool.indirect_dma_start(
                        out=slots_in[l], out_offset=bass.IndirectOffsetOnAxis(ap=slot[l][c][:, n:n + 1], axis=0),
                        in_=XN[:, n, :], in_offset=None).then_inc(s["scattered"], 16)
            pool.wait_ge(zeroed[1], 16)
            for k in range(2):
                pool.wait_ge(s["ye_stored"][k], 16 * ((NTILE + 1 - k) // 2))
            for n in range(NT):
                buffers = len(s["gathered"])
                if n >= buffers:
                    pool.wait_ge(s["gat_used"], n - buffers + 1)
                for c in range(2):
                    pool.indirect_dma_start(
                        out=gathered_rows[l][:, 2 * (n % buffers) + c, :], out_offset=None, in_=slots_out[l],
                        in_offset=bass.IndirectOffsetOnAxis(ap=slot[l][c][:, n:n + 1], axis=0),
                    ).then_inc(s["gathered"][n % buffers], 16)

        def proj_pe(pe, l):
            s = L[l]

            def transpose(n, k):
                pe.wait_ge(s["xs_ready"], n + 1)
                if not known_below(n, 2):
                    pe.wait_ge(s["xt_ready"], n - 1)
                pe.transpose(PS[:, k, 0:P], xn_fixed[:, k, :], ident[:]).then_inc(s["xn_t"], 1)

            def project(n, k):
                pe.wait_ge(s["xt_ready"], n + 1)
                if not known_below(n, 2):
                    pe.wait_ge(s["ev_act"], n - 1)
                    pe.wait_ge(s["ev_dve"], n - 1)
                bank = PS[:, 2 + k, :]
                if l == 0:
                    pe.matmul(bank[:, 0:P], wq[:, D:2 * D], xnT[:, k, :], start=True, stop=True)
                    pe.matmul(bank[:, P:2 * P], wq[:, 0:D], xnT[:, k, :], start=True, stop=True)
                else:
                    pe.matmul(bank[:, 0:P], basis[:], xnT[:, k, :], start=True, stop=True)
                rows = wq[:, 2 * D:3 * D + NE] if l == 0 else wv1[:]
                pe.matmul(PS[:, 4 + k, 0:D + NE], xnT[:, k, :], rows,
                          start=True, stop=True).then_inc(s["proj"], 1)

            def step(n, k):
                if not (isinstance(n, int) and n == NT - 1):
                    transpose(n + 1, 1 - k)
                project(n, k)
            transpose(0, 0)
            tile_loop(pe, 0, NT, step, unroll=8, tail=6)

        def route_pe(pe, l):
            s = L[l]
            pe.wait_ge(loaded_w0, 16 * 5)
            pe.wait_ge(s["route_pe"], 1)
            chosen = routing[l][0][4][:].rearrange("p n e -> p (n e)")
            pe.matmul(PS[:, 6, 0:NT * NE], before[:], chosen, start=True, stop=True)
            pe.matmul(PS[:, 7, 0:NT * NE], ones[:], chosen, start=True, stop=True).then_inc(s["route_pe"], 1)

        def attention0_pe(pe, first, end):
            if first == 0:
                pe.wait_ge(L[0]["ev_act"], NT)
                pe.wait_ge(L[0]["ev_dve"], NT)
            else:
                pe.wait_ge(L[0]["both_ready"], NTILE)

            def scores(n, k):
                pe.wait_ge(q_ready, n + 1)
                if not known_below(n, 2):
                    pe.wait_ge(exp_done, n - 1)
                b = sequence_of(n)
                for c in range(2):
                    mm = pe.matmul(PS[:, 2 * k + c, :], q_fixed[:, k, :], kT[:, bass.ds(b * TB + 4 * c, 4), :],
                                   start=True, stop=True)
                mm.then_inc(s_done, 1)

            def turn(n, k):
                pe.wait_ge(exp_done, n + 1)
                if known(n, SPLIT):
                    pe.wait_ge(L[0]["hidT_ready"], NTILE)
                if not known_below(n, 1):
                    pe.wait_ge(pT_ready, n)
                for c in range(TB):
                    mm = pe.transpose(PS[:, 4 + c // 4, (c % 4) * P:(c % 4 + 1) * P],
                                      prob[:, k, c * P:(c + 1) * P], ident[:])
                mm.then_inc(p_t, 1)

            def values(n, k):
                pe.wait_ge(pT_ready, n + 1)
                if known(n, 0):
                    pe.wait_ge(L[0]["routed"], 1)
                if known(n, SPLIT):
                    pe.wait_ge(L[0]["ye_ready"], NTILE)
                if not known_below(n, 2):
                    pe.wait_ge(x_att0, n - 1)
                b = sequence_of(n)
                for c in range(TB):
                    mm = pe.matmul(PS[:, 6 + k, 0:D], probT[:, k, c * P:(c + 1) * P],
                                   v_lg[:, bass.ds(b * TB + c, 1), 0:D], start=(c == 0), stop=(c == TB - 1))
                mm.then_inc(pv_done, 1)

            def step(n, k):
                if not known(n, end - 1):
                    scores(n + 1, 1 - k)
                turn(n, k)
                if not known(n, first):
                    values(n - 1, 1 - k)
            scores(first, 0)
            tile_loop(pe, first, end, step)
            values(end - 1, 1)

        class Experts:
            def __init__(self, eng, l):
                self.eng, self.of, self.place = eng, expert_of[l], None
                self.registers = [eng.alloc_register("expert%d_%d" % (l, i)) for i in range(8)]

            def before(self, first, x):
                self.place = x % 4
                if x % 4 == 0:
                    self.eng.load(self.registers, self.of[0:1, bass.ds(first + x - 2, 8)])
                    self.values = [self.eng.snap(r).with_bounds(min_val=0, max_val=NE - 1) for r in self.registers]

            def __call__(self, j, lead):
                if isinstance(j, int):
                    return self.eng.value_load(self.of[0:1, j:j + 1], min_val=0, max_val=NE - 1)
                return self.values[self.place + 2 + lead]

        PARTS = [(0, 0), (0, 1), (1, 0)]

        def moe_pe(pe, l):
            expert = Experts(pe, l)
            s = L[l]
            pre, hid, hidT = experts[l]
            FW, chunks = (F0, CH0) if l == 0 else (F1, CH1)
            if l == 0:
                pe.wait_ge(loaded_moe0, 16 * 4)
            else:
                pe.wait_ge(weights_split, ROUNDS)
            tile_copied, hidden_copied = (s["xeT_ready"], s["hidT_ready"]) if l == 0 else (xe_rest, hid_rest)
            pe.wait_ge(s["routed"], 1)
            if l == 0:
                pe.wait_ge(x_att0, SPLIT)

            def turn_in(j, k):
                pe.wait_ge(s["xe_loaded"][k], 16 * (turn_of(j, 4) + 1))
                if not known_below(j, 1):
                    pe.wait_ge(tile_copied, j)
                pe.transpose(PS[:, 4, 0:P], xe[:, k, :], ident[:]).then_inc(s["xe_t"], 1)

            def up(j, k):
                e = expert(j, 1)
                pe.wait_ge(tile_copied, j + 1)
                if not known_below(j, 2):
                    pe.wait_ge(s["pre_ready"], j - 1)
                    if l == 1:
                        pe.wait_ge(s["hid_ready"], j - 1)
                for x, w in [(None, None)] if l == 0 else PARTS:
                    rows = xeT[:, k, :] if l == 0 else xeT_parts[:, k, x, :]
                    from_ = w_in if l == 0 else w_in_parts[w]
                    for c in range(2):
                        mm = pe.matmul(PS[:, 2 * k + c, 0:FW], rows, from_[:, bass.ds(e, 1), c * FW:(c + 1) * FW],
                                       start=(l == 0 or (x, w) == PARTS[0]), stop=(l == 0 or (x, w) == PARTS[-1]))
                mm.then_inc(s["up_done"], 1)

            def turn_hidden(j, k):
                pe.wait_ge(s["hid_ready"], j + 1)
                if not known_below(j, 1):
                    pe.wait_ge(hidden_copied, j)
                f = 0
                for c, m in enumerate(chunks):
                    mm = pe.transpose(PS[0:m, 5, c * P:(c + 1) * P], hid[:, k, f:f + m], ident[:])
                    f += m
                mm.then_inc(s["hid_t"], 1)

            def down(j, k):
                e = expert(j, -1)
                pe.wait_ge(hidden_copied, j + 1)
                if not known_below(j, 2):
                    pe.wait_ge(s["ye_ready"], j - 1)
                terms = [(c, x, w) for c in range(len(chunks)) for x, w in ([(0, 0)] if l == 0 else PARTS)]
                for c, x, w in terms:
                    m = chunks[c]
                    rows = hidT[0:m, k, c, :] if l == 0 else hidT_parts[0:m, k, x, c, :]
                    from_ = w_dn if l == 0 else w_dn_parts[w]
                    mm = pe.matmul(PS[:, 6 + k, 0:D], rows, from_[0:m, bass.ds(e, 1), c, :],
                                   start=((c, x, w) == terms[0]), stop=((c, x, w) == terms[-1]))
                mm.then_inc(s["dn_done"], 1)

            def step(j, load):
                k = load % 2
                last = isinstance(j, int) and j >= NTILE - 2
                if not (last and j == NTILE - 1):
                    up(j + 1, 1 - k)
                if not last:
                    turn_in(j + 2, (load + 2) % 4)
                turn_hidden(j, k)
                if not known_below(j, 1):
                    down(j - 1, 1 - k)
            turn_in(0, 0)
            up(0, 0)
            turn_in(1, 1)
            tile_loop(pe, 0, NTILE, step, unroll=8, tail=5, buffers=4, before=expert.before)
            down(NTILE - 1, (NTILE - 1) % 2)

        def norm_act(act, l):
            s = L[l]
            act.wait_ge(s["var"], 1)
            act.activation(std[:], std[:], ACT.Sqrt).then_inc(s["sd"], 1)

        def proj_act(act, l):
            s = L[l]

            def copy_xnT(n, k):
                act.wait_ge(s["xn_t"], n + 1)
                if not known_below(n, 2):
                    act.wait_ge(s["proj"], n - 1)
                act.activation(xnT[:, k, :], PS[:, k, 0:P], ACT.Copy).then_inc(s["xt_ready"], 1)

            def copy_row(n, k):
                act.wait_ge(s["xs_ready"], n + 1)
                act.activation(XN[:, bass.ds(n, 1), :], xn_fixed[:, k, :].unsqueeze(1), ACT.Copy).then_inc(s["xn_ready"], 1)

            def copy_kq(n, k):
                act.wait_ge(s["proj"], n + 1)
                if l == 1:
                    act.activation(lat_hi[:, bass.ds(n * P, P)], PS[:, 2 + k, 0:P], ACT.Copy).then_inc(s["ev_act"], 1)
                    return
                act.activation(kT[:, bass.ds(n, 1), :], PS[:, 2 + k, 0:P], ACT.Copy)
                act.activation(qT[:, bass.ds(n, 1), :], PS[:, 2 + k, P:2 * P], ACT.Copy,
                               scale=float(D) ** -0.5).then_inc(s["ev_act"], 1)

            def step(n, k):
                if not (isinstance(n, int) and n == NT - 1):
                    copy_xnT(n + 1, 1 - k)
                    copy_row(n + 1, 1 - k)
                copy_kq(n, k)
            copy_xnT(0, 0)
            copy_row(0, 0)
            tile_loop(act, 0, NT, step, unroll=8, tail=6)

        def route_act(act, l):
            s = L[l]
            act.wait_ge(s["route_act"], 1)
            rel, ex = routing[l][0][0:2]
            act.activation(ex[:], rel[:], ACT.Exp).then_inc(s["route_act"], 1)
            act.wait_ge(s["route_act"], 3)
            act.activation(r_small[3][:], r_small[2][:], ACT.Exp).then_inc(s["route_act"], 1)

        def attention0_act(act, first, end):
            if first == 0:
                act.wait_ge(L[0]["ev_act"], NT)
            else:
                act.wait_ge(L[0]["dn_done"], NTILE)

            def copy_q(n, k):
                if not known_below(n, 2):
                    act.wait_ge(s_done, n - 1)
                act.activation(q_fixed[:, k, :], qT[:, bass.ds(n, 1), :], ACT.Copy).then_inc(q_ready, 1)

            def exps(n, k):
                act.wait_ge(max_done, n + 1)
                if not known_below(n, 2):
                    act.wait_ge(p_t, n - 1)
                    act.wait_ge(rden_done, n - 1)
                act.activation(prob[:, k, :], PS[:, 2 * k:2 * k + 2, :].rearrange("p a b -> p (a b)"), ACT.Exp,
                               bias=nmax[:, k:k + 1], accum_out=den[:, k:k + 1]).then_inc(exp_done, 1)

            def copy_pT(n, k):
                act.wait_ge(p_t, n + 1)
                if not known_below(n, 2):
                    act.wait_ge(pv_done, n - 1)
                act.activation(probT[:, k, :], PS[:, 4:6, :].rearrange("p a b -> p (a b)"), ACT.Copy).then_inc(pT_ready, 1)

            def step(n, k):
                if not (known(n, end - 2) or known(n, end - 1)):
                    copy_q(n + 2, k)
                if not known(n, end - 1):
                    exps(n + 1, 1 - k)
                copy_pT(n, k)
            copy_q(first, 0)
            copy_q(first + 1, 1)
            exps(first, 0)
            tile_loop(act, first, end, step)

        def moe_act(act, l):
            s = L[l]
            pre, hid, hidT = experts[l]
            FW, chunks = (F0, CH0) if l == 0 else (F1, CH1)

            def copy_xeT(j, k):
                act.wait_ge(s["xe_t"], j + 1)
                if not known_below(j, 2):
                    act.wait_ge(s["up_done"], j - 1)
                act.activation(xeT[:, k, :] if l == 0 else xeT_parts[:, k, 0, :], PS[:, 4, 0:P],
                               ACT.Copy).then_inc(s["xeT_ready"], 1)

            def silu(j, k):
                if l == 1:
                    act.wait_ge(s["up_done"], j + 1)
                    if not known_below(j, 2):
                        act.wait_ge(s["hid_ready"], j - 1)
                    act.activation(pre[:, k, 0:FW], PS[:, 2 * k, 0:FW], ACT.Silu).then_inc(s["pre_ready"], 1)
                    return
                act.wait_ge(s["pre_ready"], j + 1)
                if not known_below(j, 2):
                    act.wait_ge(s["hid_t"], j - 1)
                act.activation(hid[:, k, 0:FW], pre[:, k, 0:FW], ACT.Silu).then_inc(s["hid_ready"], 1)

            def copy_hidT(j, k):
                act.wait_ge(s["hid_t"], j + 1)
                if not known_below(j, 2):
                    act.wait_ge(s["dn_done"], j - 1)
                if l == 0:
                    act.activation(hidT[0:102, k, :, :].rearrange("p a b -> p (a b)"), PS[0:102, 5, :],
                                   ACT.Copy).then_inc(s["hidT_ready"], 1)
                else:
                    act.activation(hidT_parts[0:96, k, 0, 2, :], PS[0:96, 5, 2 * P:3 * P], ACT.Copy)
                    act.activation(hidT_parts[:, k, 0, 0:2, :].rearrange("p a b -> p (a b)"), PS[:, 5, 0:2 * P],
                                   ACT.Copy).then_inc(s["hidT_ready"], 1)

            def step(j, k):
                last = isinstance(j, int) and j >= NTILE - 2
                if not last:
                    copy_xeT(j + 2, k)
                if l == 0:
                    copy_hidT(j, k)
                if not (last and j == NTILE - 1):
                    silu(j + 1, 1 - k)
                if l == 1:
                    copy_hidT(j, k)
            copy_xeT(0, 0)
            copy_xeT(1, 1)
            silu(0, 0)
            tile_loop(act, 0, NTILE, step, unroll=8, tail=5)

        def stats_dve(dve, l, n):
            dve.bn_stats(stats[l][:, n, :], X[:, n, :]).then_inc(L[l]["stats"], 1)

        def norm_dve(dve, l):
            s = L[l]
            total, apart, square = r_small[0:3]
            dve.wait_ge(s["stats"], NT)
            even, odd = stats[l][:, :, 0:3], stats[l][:, :, 3:6]
            dve.tensor_tensor(total[:], even[:, :, 1], odd[:, :, 1], ALU.add)
            dve.tensor_tensor(apart[:], even[:, :, 1], odd[:, :, 1], ALU.subtract)
            dve.tensor_tensor(std[:], even[:, :, 2], odd[:, :, 2], ALU.add).then_inc(s["mv"], 1)
            dve.wait_ge(s["mv"], 1)
            dve.tensor_scalar(mean[:], total[:], 0.5, None, ALU.mult)
            dve.tensor_tensor(square[:], apart[:], apart[:], ALU.mult)
            dve.tensor_scalar(std[:], std[:], 1.0 / D, EPS, ALU.mult, ALU.add).then_inc(s["mv"], 1)
            dve.wait_ge(s["mv"], 2)
            dve.scalar_tensor_tensor(out=std[:], in0=square[:], scalar=0.25, in1=std[:],
                                     op0=ALU.mult, op1=ALU.add).then_inc(s["var"], 1)
            dve.wait_ge(s["sd"], 1)
            dve.reciprocal(rstd[:], std[:]).then_inc(s["rstd"], 1)
            dve.wait_ge(s["rstd"], 1)

        def proj_dve(dve, l):
            s = L[l]

            def normalise(n, k):
                if not known_below(n, 2):
                    dve.wait_ge(s["xn_t"], n - 1)
                    dve.wait_ge(s["xn_ready"], n - 1)
                dve.tensor_scalar(xn_fixed[:, k, :], X[:, bass.ds(n, 1), :], mean[:, bass.ds(n, 1)],
                                  rstd[:, bass.ds(n, 1)], ALU.subtract, ALU.mult).then_inc(s["xs_ready"], 1)

            def copy_v(n, k):
                dve.wait_ge(s["proj"], n + 1)
                if l == 1:
                    dve.tensor_tensor(v9[:, bass.ds(n, 1), :, 0:HD],
                                      PS[:, 4 + k, 0:D].rearrange("p (o h c) -> p o h c", o=1, h=HEADS),
                                      vb[:].rearrange("p (o h c) -> p o h c", o=1, h=HEADS), ALU.add)
                    dve.tensor_copy(lg1[:, bass.ds(n, 1), :], PS[:, 4 + k, D:D + NE].unsqueeze(1))
                    return
                dve.tensor_copy(v_lg[:, bass.ds(n, 1), :], PS[:, 4 + k, 0:D + NE]).then_inc(s["ev_dve"], 1)

            def latent_rest(n, k):
                dve.wait_ge(s["ev_act"], n + 1)
                dve.tensor_tensor(lat_lo[0:RANK, bass.ds(n * P, P)], PS[0:RANK, 2 + k, 0:P],
                                  lat_hi[0:RANK, bass.ds(n * P, P)], ALU.subtract).then_inc(s["ev_dve"], 1)

            def step(n, k):
                if not (isinstance(n, int) and n >= NT - 2):
                    normalise(n + 2, k)
                if l == 1 and not known(n, 0):
                    latent_rest(n - 1, 1 - k)
                copy_v(n, k)
            normalise(0, 0)
            normalise(1, 1)
            tile_loop(dve, 0, NT, step, unroll=8, tail=6)
            if l == 1:
                latent_rest(NT - 1, 1)

        def route_dve(dve, l):
            s = L[l]
            count = [0]

            def link(ins):
                count[0] += 1
                ins.then_inc(s["route"], 1)
                dve.wait_ge(s["route"], count[0])

            def wide(t):
                return t[:].unsqueeze(2).to_broadcast([P, NT, NE])

            def over_tiles(t):
                return t[:].unsqueeze(1).to_broadcast([P, NT, NE])
            (rel, ex, tmp, hot1, chosen, hot2), r_map = routing[l]
            top, first, second, e2, z, tot = r_small
            dve.wait_ge(s["ev_dve"], NT)
            dve.wait_ge(loaded_w0, 16 * 5)
            logits = v_lg[:, :, D:D + NE] if l == 0 else lg1[:]
            if l == 0:
                link(dve.tensor_tensor(tmp[:], logits, over_tiles(gb), ALU.add))
                logits = tmp[:]
            link(dve.tensor_reduce(top[:], logits, AX.X, ALU.max))
            dve.tensor_tensor(rel[:], logits, wide(top), ALU.subtract).then_inc(s["route_act"], 1)
            dve.wait_ge(s["route_act"], 2)
            link(dve.tensor_reduce(z[:], ex[:], AX.X, ALU.add))
            link(dve.tensor_scalar(tmp[:], rel[:], 0.0, None, ALU.is_ge))
            link(dve.tensor_tensor(tmp[:], tmp[:], over_tiles(iota_e), ALU.mult))
            link(dve.tensor_reduce(first[:], tmp[:], AX.X, ALU.min))
            link(dve.tensor_tensor(hot1[:], over_tiles(iota_e), wide(first), ALU.is_equal))
            link(dve.scalar_tensor_tensor(out=ex[:].rearrange("p n e -> p (n e)"),
                                          in0=hot1[:].rearrange("p n e -> p (n e)"), scalar=-BIG,
                                          in1=rel[:].rearrange("p n e -> p (n e)"), op0=ALU.mult, op1=ALU.add))
            dve.tensor_reduce(second[:], ex[:], AX.X, ALU.max).then_inc(s["route_act"], 1)
            dve.wait_ge(s["route_act"], 4)
            link(dve.tensor_tensor(tmp[:], ex[:], wide(second), ALU.is_equal))
            link(dve.tensor_tensor(tmp[:], tmp[:], over_tiles(iota_e), ALU.mult))
            link(dve.tensor_reduce(first[:], tmp[:], AX.X, ALU.min))
            link(dve.tensor_tensor(hot2[:], over_tiles(iota_e), wide(first), ALU.is_equal))
            dve.tensor_tensor(chosen[:], hot1[:], hot2[:], ALU.add).then_inc(s["route_pe"], 1)
            link(dve.reciprocal(z[:], z[:]))
            link(dve.tensor_tensor(e2[:], e2[:], z[:], ALU.mult))
            link(dve.scalar_tensor_tensor(out=tot[:], in0=z[:], scalar=1e-20, in1=e2[:], op0=ALU.add, op1=ALU.add))
            link(dve.reciprocal(tot[:], tot[:]))
            link(dve.tensor_tensor(w_top[l][0][:], z[:], tot[:], ALU.mult))
            link(dve.tensor_tensor(w_top[l][1][:], e2[:], tot[:], ALU.mult))
            dve.wait_ge(s["route_pe"], 2)
            link(dve.tensor_copy(rel[:].rearrange("p n e -> p (n e)"), PS[:, 7, 0:NT * NE]))
            src, dst, shift = rel, tmp, 1
            while shift < NT:
                link(dve.tensor_copy(dst[:, 0:shift, :], src[:, 0:shift, :]))
                link(dve.tensor_tensor(dst[:, shift:, :], src[:, shift:, :], src[:, 0:NT - shift, :], ALU.add))
                src, dst, shift = dst, (ex if dst is tmp else tmp), 2 * shift
            total, n_tiles, upto, other = r_e
            link(dve.tensor_copy(total[:], src[:, NT - 1, :]))
            link(dve.tensor_tensor(src[:], src[:], rel[:], ALU.subtract))
            link(dve.tensor_tensor(src[:].rearrange("p n e -> p (n e)"), src[:].rearrange("p n e -> p (n e)"),
                                   PS[:, 6, 0:NT * NE], ALU.add))
            link(dve.tensor_tensor(rel[:].rearrange("p n e -> p (n e)").rearrange("p (e n) -> p e n", e=NE),
                                   total[:].unsqueeze(2).to_broadcast([P, NE, NT]),
                                   steps128[:].unsqueeze(1).to_broadcast([P, NE, NT]), ALU.is_gt))
            link(dve.tensor_reduce(n_tiles[:], rel[:].rearrange("p n e -> p (n e)").rearrange("p (e n) -> p e n", e=NE),
                                   AX.X, ALU.add))
            cur, nxt = n_tiles, upto
            for shift in (1, 2, 4):
                link(dve.tensor_copy(nxt[:, 0:shift], cur[:, 0:shift]))
                link(dve.tensor_tensor(nxt[:, shift:], cur[:, shift:], cur[:, 0:NE - shift], ALU.add))
                cur, nxt = nxt, (other if nxt is upto else upto)
            ends = cur
            link(dve.tensor_tensor(nxt[:], ends[:], n_tiles[:], ALU.subtract))
            link(dve.tensor_scalar(nxt[:], nxt[:], float(P), None, ALU.mult))
            link(dve.tensor_tensor(src[:], src[:], over_tiles(nxt), ALU.add))
            link(dve.tensor_tensor(r_map[:], tile_no[:].unsqueeze(2).to_broadcast([P, NTABLE, NE]),
                                   ends[:].unsqueeze(1).to_broadcast([P, NTABLE, NE]), ALU.is_ge))
            link(dve.tensor_reduce(r_tile[:], r_map[:], AX.X, ALU.add))
            link(dve.tensor_scalar(expert_of[l][:], r_tile[:], float(NE - 1), None, ALU.min))
            for c, hot in enumerate((hot1, hot2)):
                link(dve.tensor_tensor(rel[:], hot[:], src[:], ALU.mult))
                link(dve.tensor_reduce(tot[:], rel[:], AX.X, ALU.add))
                ins = dve.tensor_copy(slot[l][c][:], tot[:])
                if c == 0:
                    link(ins)
            ins.then_inc(s["routed"], 1)

        def attention0_dve(dve, first, end):
            def maxima(n, k):
                dve.wait_ge(s_done, n + 1)
                if not known_below(n, 2):
                    dve.wait_ge(exp_done, n - 1)
                dve.tensor_reduce(nmax[:, k:k + 1], PS[:, 2 * k:2 * k + 2, :], AX.XY, ALU.max,
                                  negate=True).then_inc(max_done, 1)

            def add(n, k):
                dve.wait_ge(exp_done, n + 1)
                dve.reciprocal(rden[:, k:k + 1], den[:, k:k + 1]).then_inc(rden_done, 1)
                dve.wait_ge(rden_done, n + 1)
                dve.wait_ge(pv_done, n + 1)
                dve.scalar_tensor_tensor(out=X[:, bass.ds(n, 1), :], in0=PS[:, 6 + k, 0:D].unsqueeze(1), scalar=rden[:, k:k + 1],
                                         in1=X[:, bass.ds(n, 1), :], op0=ALU.mult, op1=ALU.add).then_inc(x_att0, 1)

            def step(n, k):
                if not known(n, end - 1):
                    maxima(n + 1, 1 - k)
                if not known(n, first):
                    add(n - 1, 1 - k)
                if first == 0 and known(n, end - 2):
                    head_matrices_dve(dve)
                if known(n, NT - 2):
                    finish(NT - 8, 0, 4, n)
                elif known(n, NT - 1):
                    finish(NT - 4, 0, 3, n)
                elif first > 0 and not known_below(n, FIRST_SUM):
                    finish(2 * (n - FIRST_SUM), 2 * k, 2, n)

            def finish(m, k, tiles, attended):
                dve.wait_ge(x_att0, attended)
                combine(dve, 0, m, k, tiles)
                dve.wait_ge(L[0]["gat_used"], m + tiles)
                for t in range(tiles):
                    dve.bn_stats(stats[1][:, bass.ds(m + t, 1), :], X[:, bass.ds(m + t, 1), :]).then_inc(L[1]["stats"], 1)
            maxima(first, 0)
            tile_loop(dve, first, end, step)
            add(end - 1, 1)
            if first > 0:
                finish(NT - 1, 3, 1, NT)

        def moe_dve(dve, l):
            expert = Experts(dve, l)
            s = L[l]
            pre, hid, hidT = experts[l]
            FW = F0 if l == 0 else F1
            if l == 0:
                dve.wait_ge(loaded_moe0, 16 * 4)

            def biased_product(j, k):
                if l == 1:
                    dve.wait_ge(s["pre_ready"], j + 1)
                    if not known_below(j, 2):
                        dve.wait_ge(s["hid_t"], j - 1)
                    dve.tensor_tensor(hid[:, k, 0:FW], pre[:, k, 0:FW], PS[:, 2 * k + 1, 0:FW],
                                      ALU.mult).then_inc(s["hid_ready"], 1)
                    return
                e = expert(j, 1)
                dve.wait_ge(s["up_done"], j + 1)
                if not known_below(j, 1):
                    dve.wait_ge(s["pre_ready"], j)
                dve.tensor_tensor(both[:], PS[:, 2 * k:2 * k + 2, 0:FW],
                                  b_in[:, bass.ds(e, 1), :].rearrange("p o (c f) -> p (o c) f", c=2),
                                  ALU.add).then_inc(s["both_ready"], 1)
                dve.wait_ge(s["both_ready"], j + 1)
                if not known_below(j, 2):
                    dve.wait_ge(s["hid_ready"], j - 1)
                dve.tensor_tensor(pre[:, k, :], both[:, 0, :], both[:, 1, :], ALU.mult).then_inc(s["pre_ready"], 1)

            def add_bias(j, k):
                if l == 1:
                    dve.wait_ge(s["dn_done"], j + 1)
                    if not known_below(j, 2):
                        dve.wait_ge(s["ye_stored"][k], 16 * turn_of(j))
                    dve.tensor_copy(ye[:, k, :], PS[:, 6 + k, 0:D]).then_inc(s["ye_ready"], 1)
                    return
                e = expert(j, -1)
                dve.wait_ge(s["dn_done"], j + 1)
                if not known_below(j, 2):
                    dve.wait_ge(s["ye_stored"][k], 16 * turn_of(j))
                dve.tensor_tensor(ye[:, k, :].unsqueeze(1), PS[:, 6 + k, 0:D].unsqueeze(1), b_dn[:, bass.ds(e, 1), :],
                                  ALU.add).then_inc(s["ye_ready"], 1)

            def rest_of_tile(j, k):
                dve.wait_ge(s["xeT_ready"], j + 1)
                dve.tensor_tensor(xeT_parts[:, k, 1, :], PS[:, 4, 0:P], xeT_parts[:, k, 0, :],
                                  ALU.subtract).then_inc(xe_rest, 1)

            def rest_of_hidden(j, k):
                dve.wait_ge(s["hidT_ready"], j + 1)
                dve.tensor_tensor(hidT_parts[0:96, k, 1, 2, :], PS[0:96, 5, 2 * P:3 * P], hidT_parts[0:96, k, 0, 2, :],
                                  ALU.subtract)
                dve.tensor_tensor(hidT_parts[:, k, 1, 0:2, :].rearrange("p a b -> p (a b)"), PS[:, 5, 0:2 * P],
                                  hidT_parts[:, k, 0, 0:2, :].rearrange("p a b -> p (a b)"),
                                  ALU.subtract).then_inc(hid_rest, 1)

            def step(j, k):
                if l == 1 and not (isinstance(j, int) and j >= NTILE - 2):
                    rest_of_tile(j + 2, k)
                if not (isinstance(j, int) and j == NTILE - 1):
                    biased_product(j + 1, 1 - k)
                if l == 1:
                    rest_of_hidden(j, k)
                if not known_below(j, 1):
                    add_bias(j - 1, 1 - k)
            if l == 1:
                rest_of_tile(0, 0)
                rest_of_tile(1, 1)
            biased_product(0, 0)
            tile_loop(dve, 0, NTILE, step, unroll=8, tail=5, before=expert.before if l == 0 else None)
            add_bias(NTILE - 1, (NTILE - 1) % 2)

        def combine(dve, l, m, k, tiles):
            s, rows = L[l], gathered_rows[l]
            buffers = len(s["gathered"])
            for t in range(tiles):
                one, b = bass.ds(m + t, 1), (k + t) % buffers
                dve.wait_ge(s["gathered"][b], 32 * (turn_of(m + t, buffers) + 1))
                dve.scalar_tensor_tensor(out=X[:, one, :], in0=rows[:, 2 * b:2 * b + 1, :], scalar=w_top[l][0][:, one],
                                         in1=X[:, one, :], op0=ALU.mult, op1=ALU.add).then_inc(s["half_sum"], 1)
            dve.wait_ge(s["half_sum"], m + tiles)
            for t in range(tiles):
                one, b = bass.ds(m + t, 1), (k + t) % buffers
                dve.scalar_tensor_tensor(out=X[:, one, :], in0=rows[:, 2 * b + 1:2 * b + 2, :], scalar=w_top[l][1][:, one],
                                         in1=X[:, one, :], op0=ALU.mult, op1=ALU.add).then_inc(s["gat_used"], 1)

        (x_att1, aux_full, aux_free, lt_hi_done, lt_ready, v_ready, score_done, exp1_done, pv1_done,
         oT_ready, max_ready, shift_loaded0, shift_loaded1, y_done, y_ready, y_t, yT_ready, o_done,
         chain1, hm_ready, const1, passed_pe, passed_dve, passed_sp) = (
            S(n) for n in ("x_att1 aux_full aux_free lt_hi_done lt_ready v_ready score_done exp1_done "
                           "pv1_done oT_ready max_ready shift_loaded0 shift_loaded1 y_done y_ready y_t "
                           "yT_ready o_done chain1 hm_ready const1 passed_pe passed_dve passed_sp").split())
        shift_loaded = [shift_loaded0, shift_loaded1]
        BLOCKS = [(i, c, i if 512 * (c + 1) >= (i + 1) * P else TB - 4 + i, h)
                  for i in range(TB) for c in range(1 + i // 4) for h in range(HG)]
        PIECES = [(lo, hi, pair) for lo, hi in ((0, 512), (512, 768), (768, 1024)) for pair in range(2)]
        CHUNKS = []
        for j in range(TB):
            first = SEQ if TB - j <= 4 else (TB - j + 1) // 2 * P
            for h in range(HG):
                CHUNKS += [(j, h, lo, min(first, (TB - j) * P - lo)) for lo in range(0, (TB - j) * P, first)]
        NCHUNK = len(CHUNKS)
        SLOT_END = [max(e for e, chunk in enumerate(CHUNKS) if chunk[0] == j) + 1 for j in range(TB)]

        def order_of_step():
            blocks_per_slot = [4, 12, 12, 11, 9]
            order, e, n = [], 0, 0
            for j in range(TB):
                mine = [x for x in CHUNKS if x[0] == j]
                todo = blocks_per_slot[j] if j < len(blocks_per_slot) else 0
                for m, (_, h, lo, _) in enumerate(mine):
                    order.append(("chunk", e))
                    e += 1
                    last_of_head = m + 1 == len(mine) or mine[m + 1][1] != h
                    if j == 0:
                        if h == 0 and lo == 0:
                            order.append(("latent", 1, 4))
                        if h == 0 and lo > 0:
                            order.append(("latent", 1, 5))
                        if h == 1 and last_of_head:
                            order.append(("values", -1, TB - 1, 1))
                        if h == 3 and lo == 0:
                            order += [("output", 0), ("output", 1)]
                    if last_of_head and h % 2 == 1 and 2 * j + h // 2 <= ROUNDS:
                        order.append(("weights", 2 * j + h // 2))
                    share = todo * (m + 1) // len(mine) - todo * m // len(mine)
                    order += [("block", n + x) for x in range(share)]
                    n += share
                    if j > 0 and last_of_head:
                        if h == 1 and j - 1 < 4:
                            order.append(("values", 0, j - 1, 0))
                        if h == (3 if j - 1 < 4 else 2):
                            order.append(("values", 0, j - 1, 1))
                    for where, what in (((4, 3), ("latent", 2, 0)), ((5, 1), ("shift", 1)), ((5, 3), ("latent", 2, 1)),
                                        ((6, 1), ("latent", 2, 2)), ((6, 3), ("latent", 2, 3))):
                        if where == (j, h) and last_of_head:
                            order.append(what)
                if j == 0:
                    order.append(("experts", 0))
            assert n == len(BLOCKS)
            return order
        ORDER = order_of_step()

        def has(q, lead):
            return not (isinstance(q, int) and q + lead > NG - 1)

        def uses_of(q):
            return [x for x in ORDER if x[0] == "block" and has(q, 1) or x[0] == "shift" and has(q, 1)
                    or x[0] == "latent" and has(q, x[1]) or x[0] == "output" and not known(q, 0)]
        PROLOGUE = ([("latent", x) for x in range(6)] + [("block", x) for x in range(len(BLOCKS))] + [("shift", 0)]
                    + [("latent", x) for x in range(6, 10)])
        BEFORE = len(PROLOGUE)
        STEP_USES = len(BLOCKS) + 1 + len(PIECES) + 2
        TOTAL_USES = BEFORE + STEP_USES * NG - len(BLOCKS) - 1 - 4 - len(PIECES)
        assert STEP_USES % 3 == 0 and NCHUNK % 3 == 0

        def uses_before(q):
            if known(q, 0):
                return BEFORE
            return BEFORE - 2 + STEP_USES * q - (4 if known(q, NG - 1) else 0)

        def use_mod(q, k, n, m):
            return ((uses_before(q) if isinstance(q, int) else BEFORE - 2 + STEP_USES * k) + n) % m

        def items(q, k):
            uses, n = uses_of(q), 0
            for item in ORDER:
                u = uses_before(q) + n
                if n < len(uses) and item == uses[n]:
                    yield item[0], item[1], item, u, 3 + use_mod(q, k, n, 3), use_mod(q, k, n, 2)
                    n += 1
                elif item[0] in ("chunk", "values", "experts", "weights"):
                    yield item[0], item[1], item, u, None, None

        def group_of(q):
            if isinstance(q, int):
                return q // (HEADS // HG), q % (HEADS // HG)
            b = (q >> 2).with_bounds(min_val=0, max_val=BATCH - 1)
            return b, (q & 3).with_bounds(min_val=0, max_val=HEADS // HG - 1)

        HEAD_LINKS = 7

        def head_matrices_dve(dve):
            c = [0]

            def link(ins):
                c[0] += 1
                ins.then_inc(hm_ready, 1)
                dve.wait_ge(hm_ready, c[0])
            dve.wait_ge(loaded_w1, 16 * W1_LOADS)
            dve.memset(heads_hi[RANK:RANK + 2, :], 0.0)
            link(dve.tensor_reduce(head_mean[:], heads.rearrange("p h s -> p s h"), AX.X, ALU.add))
            link(dve.tensor_tensor(core[:, 0, :], core[:, 0, :], core[:, 1, :], ALU.add))
            link(dve.tensor_scalar(core[:, 0, :], core[:, 0, :], 0.5 / HEADS, None, ALU.mult))
            link(dve.scalar_tensor_tensor(out=core[:, 0, :], in0=head_mean[:], scalar=-1.0 / HEADS,
                                          in1=core[:, 0, :], op0=ALU.mult, op1=ALU.add))
            link(dve.tensor_tensor(heads, heads, core[:, 0, :].unsqueeze(1).to_broadcast([RANK, HEADS, RANK]), ALU.add))
            flat = heads.rearrange("p h s -> p (h s)")
            link(dve.tensor_copy(heads_hl[0:RANK, :], flat))
            dve.tensor_copy(heads_hi[0:RANK, :], heads_hl[0:RANK, :])
            link(dve.tensor_tensor(heads_hl[RANK:P, :], flat, heads_hl[0:RANK, :], ALU.subtract))
            assert c[0] == HEAD_LINKS

        def prepare1_pool(pool):
            pool.wait_ge(x_att0, NT)
            pool.wait_ge(s_done, NT)
            pool.memset(lat_lo[RANK:RANK + 2, :], 1.0).then_inc(const1, 1)
            pool.wait_ge(const1, 1)
            pool.memset(lat_lo[RANK:RANK + 1, :], SHIFT).then_inc(const1, 1)
            pool.wait_ge(const1, 2)
            pool.memset(v9[:, :, :, HD:HD + 1], 1.0).then_inc(const1, 1)
            pool.wait_ge(const1, 3)
            pool.memset(v_rows, 0.0).then_inc(const1, 1)

        def stand_alone(eng, counter):
            eng.sem_inc(counter, 1)

        def attention1_pe(pe):
            pe.wait_ge(hm_ready, HEAD_LINKS)
            pe.wait_ge(const1, 4)
            pe.wait_ge(L[1]["ev_act"], NT)
            pe.wait_ge(L[1]["ev_dve"], NT)

            def fill(u, products):
                if not known_below(u, 3):
                    pe.wait_ge(aux_free, u - 2)
                products().then_inc(aux_full, 1)

            def latent_heads(q, k, u, bank, piece):
                b, g = group_of(q)
                lo, hi, pair = PIECES[piece]
                two_heads = bass.ds(g * HG * RANK + pair * P, P)

                def products():
                    pe.matmul(PS[:, bank, 0:hi - lo], heads_hl[:, two_heads],
                              lat_hi[:, bass.ds(b * SEQ + lo, hi - lo)], start=True, stop=False)
                    return pe.matmul(PS[:, bank, 0:hi - lo], heads_hi[:, two_heads],
                                     lat_lo[0:RANK + 2, bass.ds(b * SEQ + lo, hi - lo)], start=False, stop=True)
                fill(u, products)

            def block(q, k, u, bank, n):
                b, _ = group_of(q)
                i, c, _, h = BLOCKS[n]
                width = min(512, (i + 1) * P - 512 * c)
                fill(u, lambda: pe.matmul(PS[:, bank, 0:width], lt_hl[:, k, h, i * P:(i + 1) * P],
                                          lat_hi[:, bass.ds(b * SEQ + c * 512, width)], start=True, stop=True))

            def turn_shift(q, k, u, bank):
                pe.wait_ge(max_ready, 3 * (q + 1))
                fill(u, lambda: stand_alone(pe, passed_pe) or pe.transpose(PS[0:2 * HG * TB, bank, 0:P // 2].bitcast(F16),
                                             shift[:, k, :, :, :].rearrange("p r h i -> p (r h i)"), identh[:]))

            def scores(q, k, e):
                b, _ = group_of(q)
                j, h, lo, width = CHUNKS[e]
                n = q * NCHUNK + e
                if e == 0:
                    pe.wait_ge(shift_loaded[k], 16 * (turn_of(q) + 1))
                if not known_below(n, 3):
                    pe.wait_ge(exp1_done, n - 2)
                keys = bass.ds(b * SEQ + j * P, P)
                where = PS[:, n % 3 if isinstance(n, int) else e % 3, 0:width]
                queries = slice(j * P + lo, j * P + lo + width)
                pe.matmul(where, lat_hi[:, keys], lt_hl[:, k, h, queries], start=True, stop=False)
                mm = pe.matmul(where, lat_lo[0:RANK + 2, keys], lt_hm[0:RANK + 2, k, h, queries],
                               start=False, stop=(lo > 0))
                if lo == 0:
                    mm = pe.matmul(where[:, 0:P], ident16[:], late16[:], start=False, stop=True)
                mm.then_inc(score_done, 1)

            def values(q, k, j, c):
                if c == 0 or j >= 4:
                    pe.wait_ge(exp1_done, q * NCHUNK + SLOT_END[j])
                if j == 0 and c == 0:
                    pe.wait_ge(v_ready, q + 1)
                    if known(q, 0):
                        pe.wait_ge(L[1]["routed"], 1)
                    if not known_below(q, 1):
                        pe.wait_ge(oT_ready, q)
                lo, hi = max(j * P, 512 * c), 512 * (c + 1)
                for h in range(HG):
                    v0 = (j * HG + h) * (HD + 1)
                    mm = pe.matmul(PS[32 * h:32 * h + 32, 6 + c, lo - 512 * c:hi - 512 * c],
                                   v_rows[:, k, v0:v0 + 32], prob1[j % 2][:, h, lo - j * P:hi - j * P],
                                   start=(j == 0), stop=(j == (TB - 1 if c else 3)), tile_position=(0, 32 * h))
                if c == 1:
                    mm.then_inc(pv1_done, 1)

            def turn_out(q, u, bank, o):
                pe.wait_ge(oT_ready, q + 1)

                def four():
                    for i in range(4):
                        mm = pe.transpose(PS[:, bank, i * P:(i + 1) * P],
                                          oT[:, (4 * o + i) * P:(4 * o + i + 1) * P], ident[:])
                    return mm
                fill(u, four)

            def step(q, k):
                for what, x, item, u, bank, _ in items(q, k):
                    if what == "chunk":
                        scores(q, k, x)
                    if what == "values" and (x == 0 or not known(q, 0)):
                        values(q + x, (k + x) % 2, item[2], item[3])
                    if what == "experts" and known(q, 1):
                        pe.wait_ge(aux_free, u)
                        pe.wait_ge(exp1_done, NCHUNK + SLOT_END[0])
                        moe_pe(pe, 1)
                        pe.wait_ge(L[1]["ye_ready"], NTILE)
                    if what == "block":
                        block(q + 1, 1 - k, u, bank, x)
                    if what == "shift":
                        turn_shift(q + 1, 1 - k, u, bank)
                    if what == "latent":
                        latent_heads(q + x, (k + x) % 2, u, bank, item[2])
                    if what == "output":
                        turn_out(q - 1, u, bank, x)

            for u, (what, x) in enumerate(PROLOGUE):
                if what == "latent":
                    latent_heads(x // 6, x // 6, u, 3 + u % 3, x % 6)
                if what == "block":
                    block(0, 0, u, 3 + u % 3, x)
                if what == "shift":
                    turn_shift(0, 0, u, 3 + u % 3)
            tile_loop(pe, 0, NG, step, unroll=2)
            values(NG - 1, 1, TB - 1, 1)
            for o in range(2):
                u = uses_before(NG - 1) + len(uses_of(NG - 1)) + o
                turn_out(NG - 1, u, 3 + u % 3, o)
            project_out_pe(pe)

        def project_out_pe(pe):
            pe.wait_ge(exp1_done, NG * NCHUNK)
            pe.wait_ge(aux_free, TOTAL_USES)

            def turn(n, k):
                pe.wait_ge(y_ready, n + 1)
                if not known_below(n, 2):
                    pe.wait_ge(yT_ready, n - 1)
                for i in range(4):
                    mm = pe.transpose(PS[:, k, i * P:(i + 1) * P], y_fixed[:, k, i, :], ident[:])
                mm.then_inc(y_t, 1)

            def product(n, k):
                pe.wait_ge(yT_ready, n + 1)
                if not known_below(n, 2):
                    pe.wait_ge(y_done, n - 1)
                for i in range(4):
                    mm = pe.matmul(PS[:, 2 + k, i * P:(i + 1) * P], yT[:, k, i, :], ow[:], start=True, stop=True)
                mm.then_inc(o_done, 1)

            def step(n, k):
                if not known(n, NT // 4 - 1):
                    turn(n + 1, 1 - k)
                product(n, k)
            turn(0, 0)
            tile_loop(pe, 0, NT // 4, step, unroll=2)

        def attention1_act(act):
            act.wait_ge(const1, 4)
            act.wait_ge(L[1]["ev_dve"], NT)

            def fix_values(q, k):
                b, g = group_of(q)
                if not known_below(q, 2):
                    act.wait_ge(pv1_done, TB * (q - 1))
                act.activation(v_fixed[k], v9[:, bass.ds(b * TB, TB), bass.ds(g * HG, HG), :],
                               ACT.Copy).then_inc(v_ready, 1)

            def latent_hi(q, k, u, bank, piece):
                lo, hi, pair = PIECES[piece]
                act.wait_ge(aux_full, u + 1)
                for half in range(2):
                    rows = slice(64 * half, 64 * half + 64)
                    ins = act.activation(lt_hl[rows, k, 2 * pair + half, lo:hi], PS[rows, bank, 0:hi - lo], ACT.Copy)
                ins.then_inc(lt_hi_done, 1)

            def exps(q, k, e):
                j, h, lo, width = CHUNKS[e]
                act.wait_ge(score_done, q * NCHUNK + e + 1)
                if h == 0 and lo == 0 and not (isinstance(q, int) and q * TB + j < 2):
                    act.wait_ge(pv1_done, q * TB + j - 1)
                act.activation(prob1[j % 2][:, h, lo:lo + width], PS[:, e % 3, 0:width],
                               ACT.Exp, scale=RANK ** -0.5).then_inc(exp1_done, 1)

            def copy_oT(q):
                act.wait_ge(pv1_done, TB * (q + 1))
                if not known_below(q, 1):
                    act.wait_ge(aux_full, uses_before(q) + uses_of(q).index(("output", 1)) + 1)
                act.activation(oT, PS[:, 6:8, :].rearrange("p a b -> p (a b)"), ACT.Copy).then_inc(oT_ready, 1)

            def step(q, k):
                for what, x, item, u, bank, _ in items(q, k):
                    if what == "chunk":
                        exps(q, k, x)
                        if x == SLOT_END[0] - 1 and has(q, 1) and not known(q, 0):
                            fix_values(q + 1, 1 - k)
                    if what == "values" and x == -1 and not known(q, 0):
                        copy_oT(q - 1)
                    if what == "weights" and known(q, 0) and x < ROUNDS:
                        act.wait_ge(loaded_share[x % 2], 16 * (x // 2 + 1))
                        act.activation(parts[0][:, x * SHARE:(x + 1) * SHARE], staged[x % 2],
                                       ACT.Copy).then_inc(weights_hi, 1)
                    if what == "experts" and known(q, 1):
                        moe_act(act, 1)
                    if what == "latent":
                        latent_hi(q + x, (k + x) % 2, u, bank, item[2])

            for q in range(2):
                fix_values(q, q)
            for u, (what, x) in enumerate(PROLOGUE):
                if what == "latent":
                    latent_hi(x // 6, x // 6, u, 3 + u % 3, x % 6)
            tile_loop(act, 0, NG, step, unroll=2)
            copy_oT(NG - 1)
            project_out_act(act)

        def project_out_act(act):
            act.wait_ge(aux_free, TOTAL_USES)

            def fix(n, k):
                if not known_below(n, 2):
                    act.wait_ge(y_t, n - 1)
                act.activation(y_fixed[:, k, :, :], y1[:, bass.ds(4 * n, 4), :], ACT.Copy).then_inc(y_ready, 1)

            def copy_yT(n, k):
                act.wait_ge(y_t, n + 1)
                if not known_below(n, 2):
                    act.wait_ge(o_done, n - 1)
                act.activation(yT[:, k, :, :].rearrange("p i c -> p (i c)"), PS[:, k, :], ACT.Copy).then_inc(yT_ready, 1)

            def step(n, k):
                if not (isinstance(n, int) and n >= NT // 4 - 2):
                    fix(n + 2, k)
                copy_yT(n, k)
            fix(0, 0)
            fix(1, 1)
            tile_loop(act, 0, NT // 4, step, unroll=2)

        def attention1_dve(dve):
            def latent_lo(q, k, u, bank, piece):
                lo, hi, pair = PIECES[piece]
                dve.wait_ge(lt_hi_done, len(PIECES) * q + piece + 1)
                for half in range(2):
                    h = 2 * pair + half
                    rows, others = slice(64 * half, 64 * half + 64), slice(64 - 64 * half, 128 - 64 * half)
                    ins = dve.tensor_tensor(lt_hl[others, k, h, lo:hi], PS[rows, bank, 0:hi - lo],
                                            lt_hl[rows, k, h, lo:hi], ALU.subtract)
                ins.then_inc(aux_free, 1)
                for half in range(2):
                    h, rows = 2 * pair + half, slice(64 * half, 64 * half + 64)
                    ins = dve.tensor_copy(lt_hm[0:RANK, k, h, lo:hi], lt_hl[rows, k, h, lo:hi])
                if piece == len(PIECES) - 1:
                    ins.then_inc(lt_ready, 1)

            def block(q, k, u, bank, spare, n):
                i, c, column, h = BLOCKS[n]
                width = min(512, (i + 1) * P - 512 * c)
                dve.wait_ge(aux_full, u + 1)
                accum = maxima1[:, k, h, column:column + 1]
                if column < TB:
                    dve.wait_ge(aux_free, u - 1)
                    stand_alone(dve, passed_dve)
                    ins = dve.tensor_tensor_reduce(spare[:, 0:width], PS[:, bank, 0:width], late[:, 512 - width:512],
                                                   1.0, -3e38, ALU.add, ALU.max, accum)
                else:
                    ins = dve.tensor_reduce(accum, PS[:, bank, 0:width], AX.X, ALU.max)
                ins.then_inc(aux_free, 1)

            def prepare_shift(q, k, uses):
                dve.wait_ge(aux_free, uses)
                m = maxima1[:, k, :, :]
                dve.tensor_tensor(m[:, :, 4:8], m[:, :, 4:8], m[:, :, 8:12], ALU.max).then_inc(max_ready, 1)
                dve.wait_ge(max_ready, 3 * q + 1)
                dve.tensor_scalar(shift[:, k, 0, :, :], m[:, :, 0:TB], -1.0 / SHIFT, None,
                                  ALU.mult).then_inc(max_ready, 1)
                dve.wait_ge(max_ready, 3 * q + 2)
                dve.scalar_tensor_tensor(out=shift[:, k, 1, :, :], in0=shift[:, k, 0, :, :], scalar=-SHIFT,
                                         in1=m[:, :, 0:TB], op0=ALU.mult, op1=ALU.subtract).then_inc(max_ready, 1)

            def copy_shiftT(q, k, u, bank):
                dve.wait_ge(aux_full, u + 1)
                if not known_below(q, 2):
                    dve.wait_ge(shift_loaded[k], 16 * turn_of(q))
                dve.tensor_copy(shiftT[:, k, :], PS[0:2 * HG * TB, bank, 0:P // 2].bitcast(F16))\
                   .then_inc(aux_free, 1)

            def outputs(q, u, bank, o):
                b, g = group_of(q)
                if known(q, 0):
                    dve.wait_ge(L[1]["scattered"], 16 * 2 * NT)
                dve.wait_ge(aux_full, u + 1)
                o4 = PS[:, bank, :].rearrange("p (i h c) -> p i h c", i=4, h=HG)
                dve.reciprocal(rden1[:, o, :, :], o4[:, :, :, HD]).then_inc(chain1, 1)
                dve.wait_ge(chain1, 2 * q + o + 1)
                ins = dve.tensor_tensor(
                    y1[:, bass.ds(b * TB + 4 * o, 4), bass.ds(g * HG * HD, HG * HD)]
                    .rearrange("p i (h c) -> p i h c", h=HG), o4[:, :, :, 0:HD],
                    rden1[:, o, :, :].unsqueeze(3).to_broadcast([P, 4, HG, HD]), ALU.mult)
                ins.then_inc(aux_free, 1)

            def step(q, k):
                spare = junk[0 if isinstance(q, int) and q < 2 else 1]
                for what, x, item, u, bank, odd in items(q, k):
                    if what == "block":
                        block(q + 1, 1 - k, u, bank, spare[odd], x)
                        if x == len(BLOCKS) - 1:
                            prepare_shift(q + 1, 1 - k, u + 1)
                    if what == "shift":
                        copy_shiftT(q + 1, 1 - k, u, bank)
                    if what == "latent":
                        latent_lo(q + x, (k + x) % 2, u, bank, item[2])
                    if what == "output":
                        outputs(q - 1, u, bank, x)
                    if what == "weights" and known(q, 0) and x > 0:
                        cols = slice((x - 1) * SHARE, x * SHARE)
                        dve.wait_ge(weights_hi, x)
                        dve.tensor_tensor(parts[1][:, cols], staged[(x - 1) % 2], parts[0][:, cols],
                                          ALU.subtract).then_inc(weights_split, 1)
                    if what == "experts" and known(q, 1):
                        moe_dve(dve, 1)
                        spare = junk[1]
                if isinstance(q, int) and q >= NG - 2:
                    share = (NT - 2 * (NG - 4)) // 2
                    for m in range(NT - share * (NG - q), NT - share * (NG - 1 - q), 2):
                        combine(dve, 1, m, 0, 2)
                elif not isinstance(q, int):
                    combine(dve, 1, 2 * (q - 2), 0, 2)

            for u, (what, x) in enumerate(PROLOGUE):
                if what == "latent":
                    latent_lo(x // 6, x // 6, u, 3 + u % 3, x % 6)
                if what == "block":
                    block(0, 0, u, 3 + u % 3, junk[0][u % 2], x)
                if what == "shift":
                    prepare_shift(0, 0, u)
                    copy_shiftT(0, 0, u, 3 + u % 3)
            tile_loop(dve, 0, NG, step, unroll=2)
            for o in range(2):
                u = uses_before(NG - 1) + len(uses_of(NG - 1)) + o
                outputs(NG - 1, u, 3 + u % 3, o)
            project_out_dve(dve)

        def project_out_dve(dve):
            dve.wait_ge(L[1]["gat_used"], NT)

            def step(n, k):
                dve.wait_ge(o_done, n + 1)
                if not known_below(n, 2):
                    dve.wait_ge(x_att1, n - 1)
                dve.tensor_tensor(o_tmp[:, k, :, :], PS[:, 2 + k, :].rearrange("p (i c) -> p i c", i=4),
                                  ob[:].unsqueeze(1).to_broadcast([P, 4, D]), ALU.add).then_inc(y_done, 1)
                dve.wait_ge(y_done, n + 1)
                dve.tensor_tensor(X[:, bass.ds(4 * n, 4), :], X[:, bass.ds(4 * n, 4), :], o_tmp[:, k, :, :],
                                  ALU.add).then_inc(x_att1, 1)
            tile_loop(dve, 0, NT // 4, step, unroll=2)

        def stage_sp(sp, r):
            if r >= 2:
                sp.wait_ge(weights_split, r - 1)
            sp.dma_start(staged[r % 2], a["w1"][:, r * SHARE:(r + 1) * SHARE]).then_inc(loaded_share[r % 2], 16)

        def attention1_sp(sp):
            def step(q, k):
                sp.wait_ge(aux_free, PROLOGUE.index(("shift", 0)) + 1 if known(q, 0) else uses_before(q - 1) + uses_of(q - 1).index(("shift", 1)) + 1)
                stand_alone(sp, passed_sp)
                sp.wait_ge(lt_ready, q + 1)
                sp.dma_start(lt_hm[RANK:RANK + 2, k, :, :].rearrange("r h t -> r (h t)")
                             .rearrange("r (m t) -> r m t", t=P), shiftT[:, k, :]).then_inc(shift_loaded[k], 16)
                if known(q, 0):
                    for r in range(2, ROUNDS):
                        stage_sp(sp, r)
                if known(q, 1):
                    moe_sp(sp, 1)
            tile_loop(sp, 0, NG, step, unroll=2)

        block = ctx.enter_context(nc.Block())

        @block.sync
        def _(sp):
            sp.dma_start(ident[:], a["ident"]).then_inc(loaded_wq, 16)
            sp.dma_start(wq[:], a["wqkvg"]).then_inc(loaded_wq, 16)
            for b in range(BATCH):
                sp.dma_start(X[:, b * TB:(b + 1) * TB, :], a["x"][b * SEQ:(b + 1) * SEQ, :]
                             .rearrange("(n p) d -> p n d", p=P)).then_inc(loaded_x[b], 16)
            sp.dma_start(gb[:], a["gate_b"].partition_broadcast(P)).then_inc(loaded_w0, 16)
            sp.dma_start(before[:], a["before"]).then_inc(loaded_w0, 16)
            sp.dma_start(iota_e[:], a["iota_e"].partition_broadcast(P)).then_inc(loaded_w0, 16)
            sp.dma_start(steps128[:], a["steps128"].partition_broadcast(P)).then_inc(loaded_w0, 16)
            sp.dma_start(tile_no[:], a["tile_no"].partition_broadcast(P)).then_inc(loaded_w0, 16)
            for dst, name in ((wv1, "wv1"), (basis, "basis"), (ow, "ow"), (core, "core"), (late, "late"),
                              (late16, "late16"), (ident16, "ident16"), (identh, "identh")):
                sp.dma_start(dst[:], a[name]).then_inc(loaded_w1, 16)
            sp.dma_start(heads, a["heads"]).then_inc(loaded_w1, 16)
            for dst, name in ((vb, "v_b"), (ob, "o_b")):
                sp.dma_start(dst[:], a[name].partition_broadcast(P)).then_inc(loaded_w1, 16)
            sp.dma_start(w_in[:], a["w_in0"]).then_inc(loaded_moe0, 16)
            sp.dma_start(b_in[:], a["b_in0"].partition_broadcast(P)).then_inc(loaded_moe0, 16)
            sp.dma_start(b_dn[:], a["b_dn0"].partition_broadcast(P)).then_inc(loaded_moe0, 16)
            sp.dma_start(w_dn[0:102, :, :, :], a["w_dn0"]).then_inc(loaded_moe0, 16)
            moe_sp(sp, 0)
            sp.wait_ge(L[0]["ye_ready"], NTILE)
            sp.wait_ge(x_att0, NT)
            stage_sp(sp, 0)
            stage_sp(sp, 1)
            attention1_sp(sp)
            for b in range(BATCH):
                sp.wait_ge(x_att1, TB // 4 * (b + 1))
                sp.dma_start(out[b * SEQ:(b + 1) * SEQ, :].rearrange("(n p) d -> p n d", p=P),
                             X[:, b * TB:(b + 1) * TB, :]).then_inc(S("stored"), 16)
            sp.wait_ge(S("stored"), 16 * BATCH)

        @block.gpsimd
        def _(pool):
            nc.gpsimd.memset(zeros, 0.0).then_inc(S("zero_tile"), 1)
            pool.wait_ge(S("zero_tile"), 1)
            pool.wait_ge(loaded_wq, 16 * 2)
            for b in range(BATCH):
                pool.wait_ge(loaded_x[b], 16)
            zero_slots(pool, 0)
            zero_slots(pool, 1)
            route_pool(pool, 0)
            prepare1_pool(pool)
            route_pool(pool, 1)

        @block.tensor
        def _(pe):
            pe.wait_ge(loaded_wq, 16 * 2)
            proj_pe(pe, 0)
            route_pe(pe, 0)
            attention0_pe(pe, 0, SPLIT)
            moe_pe(pe, 0)
            attention0_pe(pe, SPLIT, NT)
            pe.wait_ge(loaded_w1, 16 * W1_LOADS)
            pe.wait_ge(x_att0, NT)
            proj_pe(pe, 1)
            route_pe(pe, 1)
            attention1_pe(pe)

        @block.scalar
        def _(act):
            norm_act(act, 0)
            proj_act(act, 0)
            route_act(act, 0)
            attention0_act(act, 0, SPLIT)
            moe_act(act, 0)
            attention0_act(act, SPLIT, NT)
            norm_act(act, 1)
            proj_act(act, 1)
            route_act(act, 1)
            attention1_act(act)

        @block.vector
        def _(dve):
            dve.memset(ones[:], 1.0)
            for n in range(NT):
                if n % TB == 0:
                    dve.wait_ge(loaded_x[n // TB], 16)
                stats_dve(dve, 0, n)
            norm_dve(dve, 0)
            proj_dve(dve, 0)
            route_dve(dve, 0)
            dve.wait_ge(L[0]["xn_ready"], NT)
            attention0_dve(dve, 0, SPLIT)
            moe_dve(dve, 0)
            attention0_dve(dve, SPLIT, NT)
            norm_dve(dve, 1)
            proj_dve(dve, 1)
            route_dve(dve, 1)
            attention1_dve(dve)


INPUTS = ("L0_attn_x L0_attn_W_qkv L0_ffn_gate_w L0_ffn_gate_b L0_ffn_up_w L0_ffn_up_b L0_ffn_gp_w L0_ffn_gp_b "
          "L0_ffn_down_w L0_ffn_down_b L1_attn_basis_w L1_attn_core L1_attn_head_residual L1_attn_v_w L1_attn_v_b "
          "L1_attn_o_w L1_attn_o_b L1_ffn_Wg L1_ffn_W1 L1_ffn_W2 L1_ffn_W3").split()


def laid_out(i):
    f32 = np.float32
    a = {"x": i["L0_attn_x"].reshape(BATCH * SEQ, D)}
    a["wqkvg"] = np.concatenate([i["L0_attn_W_qkv"], i["L0_ffn_gate_w"]], 0).T
    a["gate_b"] = i["L0_ffn_gate_b"]
    a["w_in0"] = np.concatenate([i["L0_ffn_gp_w"], i["L0_ffn_up_w"]], 1).transpose(2, 0, 1)
    a["b_in0"] = np.concatenate([i["L0_ffn_gp_b"], i["L0_ffn_up_b"]], 1)
    a["w_dn0"] = i["L0_ffn_down_w"].transpose(0, 2, 1).reshape(NE, 4, 102, D).transpose(2, 0, 1, 3)
    a["b_dn0"] = i["L0_ffn_down_b"]
    w_in1 = np.concatenate([i["L1_ffn_W1"], i["L1_ffn_W3"]], 1).transpose(2, 0, 1)
    w_dn1 = np.zeros((NE, len(CH1) * P, D), f32)
    w_dn1[:, :F1] = i["L1_ffn_W2"].transpose(0, 2, 1)
    w_dn1 = w_dn1.reshape(NE, len(CH1), P, D).transpose(2, 0, 1, 3)
    a["w1"] = np.concatenate([w_in1.reshape(D, -1), w_dn1.reshape(P, -1)], 1)
    a["wv1"] = np.concatenate([i["L1_attn_v_w"], i["L1_ffn_Wg"]], 0).T
    a["basis"] = np.concatenate([i["L1_attn_basis_w"]] * 2, 0).T
    a["ow"] = i["L1_attn_o_w"].T
    a["v_b"], a["o_b"] = i["L1_attn_v_b"], i["L1_attn_o_b"]
    a["core"] = np.stack([i["L1_attn_core"], i["L1_attn_core"].T], 1)
    a["heads"] = i["L1_attn_head_residual"].transpose(1, 0, 2)
    row, col = np.arange(P)[:, None], np.arange(P)[None]
    a["late"] = np.concatenate([np.zeros((P, 3 * P), f32), np.where(col > row, f32(-BIG), f32(0))], 1).astype(mybir.dt.np(BF16))
    a["late16"] = np.where(row > col, f32(-BIG), f32(0)).astype(mybir.dt.np(BF16))
    a["ident16"] = np.eye(P).astype(mybir.dt.np(BF16))
    a["identh"] = np.eye(P, dtype=np.float16)
    a["ident"] = np.eye(P, dtype=f32)
    a["before"] = np.triu(np.ones((P, P), f32), 1)
    a["iota_e"] = np.arange(NE, dtype=f32) - NE
    a["steps128"] = np.arange(NT, dtype=f32) * P
    a["tile_no"] = np.arange(NTABLE, dtype=f32)
    return {"in_" + n: np.ascontiguousarray(v) for n, v in a.items()}


def kernel(**inputs):
    import concourse.bacc as _bacc
    from concourse.bass_utils import run_bass_kernel_spmd as _run

    arrays = laid_out({n: np.asarray(inputs[n]) for n in INPUTS})
    nc = _bacc.Bacc("TRN2", target_bir_lowering=False, num_devices=1, dynamic_dma_scratch_size=DMA_RING)
    ins = {n[3:]: nc.dram_tensor(n, v.shape, mybir.dt.from_np(v.dtype), kind="ExternalInput").ap()
           for n, v in arrays.items()}
    out = nc.dram_tensor("out", (BATCH * SEQ, D), F32, kind="ExternalOutput").ap()
    two_layers(nc, ins, out)
    r = _run(nc, [arrays], core_ids=[0])
    return r.results[0]["out"].reshape(BATCH, SEQ, D)
```
